# Optimizing a Trainium2 kernel written in Bass

```python
import numpy as np
import jax
import jax.numpy as jnp

def _softmax(x, axis=-1):
    return jax.nn.softmax(x, axis=axis)

def _gelu(x):
    return jax.nn.gelu(x, approximate=True)

def _silu(x):
    return jax.nn.silu(x)

def _sigmoid(x):
    return jax.nn.sigmoid(x)

def _layernorm(x, axis=-1, eps=1e-05):
    m = jnp.mean(x, axis=axis, keepdims=True)
    v = jnp.var(x, axis=axis, keepdims=True)
    return (x - m) / jnp.sqrt(v + eps)

def _scatter_add(tgt, idx, src, axis=0):
    return tgt.at[idx].add(src)

def _segment_sum(src, seg, n):
    return jax.ops.segment_sum(src, seg, n)
kernel_name = 'mk_prb_d2_jaxref_r8_069a81'

def setup_inputs(seed: int=0):
    np.random.seed(seed)
    _w = jnp.asarray

    def _L0_attn_setup():
        import jax, jax.numpy as jnp
        import numpy as np
        HEADS = 16
        LOCAL_HEADS = 4
        DIM = 128
        DH = DIM // HEADS
        WINDOW = 128
        BLINDSPOT = 64

        def _look_around(x, buckets):
            pad_cfg = ((0, 0), (1, 0)) + ((0, 0),) * (x.ndim - 2)
            pv = -1.0 if jnp.issubdtype(x.dtype, jnp.floating) else -1
            p = jnp.pad(x, pad_cfg, constant_values=pv)
            return jnp.concatenate([p[:, :buckets], p[:, 1:buckets + 1]], axis=2)

        def _local_attn(q, k, v):
            b, lh, t, e = q.shape
            bm = b * lh
            buckets = t // WINDOW
            bq = q.reshape(bm, buckets, WINDOW, e)
            bk = k.reshape(bm, buckets, WINDOW, e)
            bv = v.reshape(bm, buckets, WINDOW, e)
            bk2 = _look_around(bk, buckets)
            bv2 = _look_around(bv, buckets)
            ticker = jnp.arange(t, dtype=jnp.int32).reshape(1, buckets, WINDOW)
            bq_k = _look_around(ticker, buckets)
            dots = jnp.einsum('buie,buje->buij', bq, bk2) * e ** (-0.5)
            mask_value = -jnp.finfo(dots.dtype).max
            causal_mask = ticker[:, :, :, None] < bq_k[:, :, None, :]
            pad_mask = bq_k[:, :, None, :] == -1
            dots = jnp.where(causal_mask | pad_mask, mask_value, dots)
            attn = jax.nn.softmax(dots, axis=-1)
            out = jnp.einsum('buij,buje->buie', attn, bv2)
            return out.reshape(b, lh, t, e)

        def _causal_linear_attn(q, k, v):
            b, h, n, e = q.shape
            u = n // BLINDSPOT
            q = jax.nn.softmax(q, axis=-1)
            k = jax.nn.elu(k) + 1.0
            bq = q.reshape(b, h, u, BLINDSPOT, e)
            bk = k.reshape(b, h, u, BLINDSPOT, e)
            bv = v.reshape(b, h, u, BLINDSPOT, e)
            bk_cumsum = jnp.cumsum(bk.sum(axis=-2), axis=-2)
            ctx = jnp.einsum('bhund,bhune->bhude', bk, bv)
            ctx = jnp.cumsum(ctx, axis=2)
            ctx = ctx / (bk_cumsum[..., None] + 1e-06)
            ctx = jnp.pad(ctx, ((0, 0), (0, 0), (1, 0), (0, 0), (0, 0)))[:, :, :u]
            attn = jnp.einsum('bhund,bhude->bhune', bq, ctx)
            return attn.reshape(b, h, n, e)
        key = jax.random.key(seed)
        ks = jax.random.split(key, 6)
        s = 1.0 / np.sqrt(DIM)
        x = jax.random.normal(ks[0], (4, 1024, DIM), dtype=jnp.float32)
        Wq = jax.random.normal(ks[1], (DIM, DIM), dtype=jnp.float32) * s
        Wk = jax.random.normal(ks[2], (DIM, DIM), dtype=jnp.float32) * s
        Wv = jax.random.normal(ks[3], (DIM, DIM), dtype=jnp.float32) * s
        Wo = jax.random.normal(ks[4], (DIM, DIM), dtype=jnp.float32) * s
        bo = jax.random.normal(ks[5], (DIM,), dtype=jnp.float32) * 0.01
        return {'x': x, 'Wq': Wq, 'Wk': Wk, 'Wv': Wv, 'Wo': Wo, 'bo': bo}
    _L0_attn_in = _L0_attn_setup()

    def _L0_ffn_setup():
        import jax, jax.numpy as jnp
        import numpy as np
        DIM = 128
        DEPTH = 6
        HEADS = 16
        DIM_HEAD = 64
        WINDOW = 32
        INNER = HEADS * DIM_HEAD
        DIM_INNER = int(DIM * 4 * 2 / 3)
        QK_SCALE = 8.0

        def shift_tokens(t):
            a, s = jnp.split(t, 2, -1)
            s = jnp.pad(s, ((0, 0), (1, 0), (0, 0)))[:, :-1]
            return jnp.concatenate([a, s], -1)

        def l2norm(t):
            return t / jnp.maximum(jnp.linalg.norm(t, axis=-1, keepdims=True), 1e-12)

        def rotate_half(x):
            x1, x2 = jnp.split(x, 2, -1)
            return jnp.concatenate([-x2, x1], -1)

        def rotary_tables(n):
            half = jnp.arange(0, DIM_HEAD, 2, dtype=jnp.float32)
            inv_freq = 1.0 / 10000.0 ** (half / DIM_HEAD)
            t = jnp.arange(n, dtype=jnp.float32)
            freqs = t[:, None] * inv_freq[None, :]
            freqs = jnp.concatenate([freqs, freqs], -1)
            base_scale = (half + 0.4 * DIM_HEAD) / (1.4 * DIM_HEAD)
            power = (t - n // 2) / (WINDOW // 2)
            scale = base_scale[None, :] ** power[:, None]
            scale = jnp.concatenate([scale, scale], -1)
            return (freqs, scale)

        def local_attention(q, k, v):
            b, h, n, d = q.shape
            w = WINDOW
            nw = n // w
            bq = q.reshape(b, h, nw, w, d)
            bk = k.reshape(b, h, nw, w, d)
            bv = v.reshape(b, h, nw, w, d)

            def look(t):
                p = jnp.pad(t, ((0, 0), (0, 0), (1, 0), (0, 0), (0, 0)))
                return jnp.concatenate([p[:, :, :nw], p[:, :, 1:]], axis=3)
            bk2, bv2 = (look(bk), look(bv))
            seq = jnp.arange(n).reshape(nw, w)
            seq_p = jnp.pad(seq, ((1, 0), (0, 0)), constant_values=-1)
            jt = jnp.concatenate([seq_p[:nw], seq_p[1:]], axis=1)
            it = seq[:, :, None]
            jb = jt[:, None, :]
            mask = (it < jb) | (it > jb + w) | (jb == -1)
            sim = jnp.einsum('bhwie,bhwje->bhwij', bq, bk2) * QK_SCALE
            sim = jnp.where(mask, -jnp.finfo(sim.dtype).max, sim)
            attn = jax.nn.softmax(sim, -1)
            out = jnp.einsum('bhwij,bhwje->bhwie', attn, bv2)
            return out.reshape(b, h, n, d)

        def attn_layer(x, Wqkv, qs, ksc, Wo):
            b, n, _ = x.shape
            qkv = x @ Wqkv
            q, k, v = jnp.split(qkv, 3, -1)
            sh = lambda t: t.reshape(b, n, HEADS, DIM_HEAD).transpose(0, 2, 1, 3)
            q, k, v = (sh(q), sh(k), sh(v))
            q = l2norm(q) * qs
            k = l2norm(k) * ksc
            freqs, scale = rotary_tables(n)
            cos, sin = (jnp.cos(freqs), jnp.sin(freqs))
            q = q * cos * scale + rotate_half(q) * sin * scale
            inv = 1.0 / scale
            k = k * cos * inv + rotate_half(k) * sin * inv
            out = local_attention(q, k, v)
            out = out.transpose(0, 2, 1, 3).reshape(b, n, INNER)
            return out @ Wo

        def ffn_layer(x, g, bln, W1, b1, W2, b2):
            mu = x.mean(-1, keepdims=True)
            var = ((x - mu) ** 2).mean(-1, keepdims=True)
            xn = (x - mu) / jnp.sqrt(var + 1e-05) * g + bln
            hg = xn @ W1 + b1
            a, gate = jnp.split(hg, 2, -1)
            return a * jax.nn.gelu(gate, approximate=False) @ W2 + b2
        key = jax.random.key(seed)
        ks = jax.random.split(key, 8)
        B, N = (2, 256)
        init = lambda k, shape: jax.random.normal(k, shape, jnp.float32) * 0.02
        return {'x': jax.random.normal(ks[0], (B, N, DIM), jnp.float32), 'Wqkv': init(ks[1], (DEPTH, DIM, 3 * INNER)), 'q_scale': jnp.ones((DEPTH, DIM_HEAD), jnp.float32), 'k_scale': jnp.ones((DEPTH, DIM_HEAD), jnp.float32), 'Wo': init(ks[2], (DEPTH, INNER, DIM)), 'ln_g': jnp.ones((DEPTH, DIM), jnp.float32), 'ln_b': jnp.zeros((DEPTH, DIM), jnp.float32), 'W1': init(ks[3], (DEPTH, DIM, 2 * DIM_INNER)), 'b1': jnp.zeros((DEPTH, 2 * DIM_INNER), jnp.float32), 'W2': init(ks[4], (DEPTH, DIM_INNER, DIM)), 'b2': jnp.zeros((DEPTH, DIM), jnp.float32)}
    _L0_ffn_in = _L0_ffn_setup()

    def _L1_attn_setup():
        import jax, jax.numpy as jnp
        import numpy as np
        B, L, D_OUT, D_HIDDEN = (16, 512, 128, 64)
        MAX_PHASE = 6.28
        R_MIN, R_MAX = (0.9, 0.999)

        def _binop(q_i, q_j):
            A_i, b_i = q_i
            A_j, b_j = q_j
            return (A_j * A_i, A_j * b_i + b_j)

        def _reference_tuple_inner(x, theta_log, nu_log, gamma_log, B_re, B_im, C_re, C_im, D):
            diag_lambda = jnp.exp(-jnp.exp(nu_log) + 1j * jnp.exp(theta_log))
            B_norm = (B_re + 1j * B_im) * jnp.exp(gamma_log)[:, None]
            C = C_re + 1j * C_im
            Bu = jnp.einsum('hd,bld->blh', B_norm, x.astype(B_norm.dtype))
            Lam = jnp.broadcast_to(diag_lambda, Bu.shape)
            _, h = jax.lax.associative_scan(_binop, (Lam, Bu), axis=1)
            y = jnp.einsum('oh,blh->blo', C, h).real + D * x
            return (y, h[:, -1])
        key = jax.random.key(seed)
        ks = jax.random.split(key, 8)
        x = jax.random.normal(ks[0], (B, L, D_OUT), dtype=jnp.float32)
        u_th = jax.random.uniform(ks[1], (D_HIDDEN,), dtype=jnp.float32)
        theta_log = jnp.log(MAX_PHASE * u_th)
        u_nu = jax.random.uniform(ks[2], (D_HIDDEN,), dtype=jnp.float32)
        nu_log = jnp.log(-0.5 * jnp.log(u_nu * (R_MAX ** 2 - R_MIN ** 2) + R_MIN ** 2))
        diag_lambda = jnp.exp(-jnp.exp(nu_log) + 1j * jnp.exp(theta_log))
        gamma_log = jnp.log(jnp.sqrt(1.0 - jnp.abs(diag_lambda) ** 2))
        b_norm = jnp.sqrt(2.0 * D_OUT)
        c_norm = jnp.sqrt(float(D_HIDDEN))
        B_re = jax.random.normal(ks[3], (D_HIDDEN, D_OUT), dtype=jnp.float32) / b_norm
        B_im = jax.random.normal(ks[4], (D_HIDDEN, D_OUT), dtype=jnp.float32) / b_norm
        C_re = jax.random.normal(ks[5], (D_OUT, D_HIDDEN), dtype=jnp.float32) / c_norm
        C_im = jax.random.normal(ks[6], (D_OUT, D_HIDDEN), dtype=jnp.float32) / c_norm
        D = jax.random.normal(ks[7], (D_OUT,), dtype=jnp.float32)
        return {'x': x, 'theta_log': theta_log, 'nu_log': nu_log, 'gamma_log': gamma_log, 'B_re': B_re, 'B_im': B_im, 'C_re': C_re, 'C_im': C_im, 'D': D}
    _L1_attn_in = _L1_attn_setup()

    def _L1_ffn_setup():
        import jax, jax.numpy as jnp
        import numpy as np

        def _bitlinear(x, w_latent):
            scale = jax.lax.stop_gradient(jnp.clip(jnp.mean(jnp.abs(w_latent), axis=1, keepdims=True), 1e-05, None))
            tern = jnp.clip(jnp.round(w_latent / scale), -1.0, 1.0)
            w = w_latent + jax.lax.stop_gradient(tern - w_latent)
            return x @ (w * scale).T
        key = jax.random.key(seed)
        ks = jax.random.split(key, 6)
        dim, hidden, rank = (128, 512, 16)
        B, S = (4, 512)
        x = jax.random.normal(ks[0], (B, S, dim), dtype=jnp.float32)
        w_fc = 0.02 * jax.random.normal(ks[1], (hidden, dim), dtype=jnp.float32)
        w_proj = 0.02 * jax.random.normal(ks[2], (dim, hidden), dtype=jnp.float32)
        u = 0.02 * jax.random.normal(ks[3], (hidden, rank), dtype=jnp.float32)
        v = 0.02 * jax.random.normal(ks[4], (rank, dim), dtype=jnp.float32)
        fast_b = jax.random.normal(ks[5], (rank, rank), dtype=jnp.float32)
        gate = jnp.float32(0.05)
        return {'x': x, 'fast_b': fast_b, 'w_fc': w_fc, 'w_proj': w_proj, 'u': u, 'v': v, 'gate': gate}
    _L1_ffn_in = _L1_ffn_setup()
    _d = {'L0_attn_x': _L0_attn_in['x'], 'L0_attn_Wq': _L0_attn_in['Wq'], 'L0_attn_Wk': _L0_attn_in['Wk'], 'L0_attn_Wv': _L0_attn_in['Wv'], 'L0_attn_Wo': _L0_attn_in['Wo'], 'L0_attn_bo': _L0_attn_in['bo'], 'L0_ffn_Wqkv': _L0_ffn_in['Wqkv'], 'L0_ffn_q_scale': _L0_ffn_in['q_scale'], 'L0_ffn_k_scale': _L0_ffn_in['k_scale'], 'L0_ffn_Wo': _L0_ffn_in['Wo'], 'L0_ffn_ln_g': _L0_ffn_in['ln_g'], 'L0_ffn_ln_b': _L0_ffn_in['ln_b'], 'L0_ffn_W1': _L0_ffn_in['W1'], 'L0_ffn_b1': _L0_ffn_in['b1'], 'L0_ffn_W2': _L0_ffn_in['W2'], 'L0_ffn_b2': _L0_ffn_in['b2'], 'L1_attn_theta_log': _L1_attn_in['theta_log'], 'L1_attn_nu_log': _L1_attn_in['nu_log'], 'L1_attn_gamma_log': _L1_attn_in['gamma_log'], 'L1_attn_B_re': _L1_attn_in['B_re'], 'L1_attn_B_im': _L1_attn_in['B_im'], 'L1_attn_C_re': _L1_attn_in['C_re'], 'L1_attn_C_im': _L1_attn_in['C_im'], 'L1_attn_D': _L1_attn_in['D'], 'L1_ffn_fast_b': _L1_ffn_in['fast_b'], 'L1_ffn_w_fc': _L1_ffn_in['w_fc'], 'L1_ffn_w_proj': _L1_ffn_in['w_proj'], 'L1_ffn_u': _L1_ffn_in['u'], 'L1_ffn_v': _L1_ffn_in['v'], 'L1_ffn_gate': _L1_ffn_in['gate']}
    _x0 = _d['L0_attn_x']
    _d['L0_attn_x'] = jax.random.normal(jax.random.fold_in(jax.random.key(seed), 1), (1, 2048, 128), dtype=_x0.dtype)
    del _x0
    return _d

def reference(L0_attn_x, L0_attn_Wq, L0_attn_Wk, L0_attn_Wv, L0_attn_Wo, L0_attn_bo, L0_ffn_Wqkv, L0_ffn_q_scale, L0_ffn_k_scale, L0_ffn_Wo, L0_ffn_ln_g, L0_ffn_ln_b, L0_ffn_W1, L0_ffn_b1, L0_ffn_W2, L0_ffn_b2, L1_attn_theta_log, L1_attn_nu_log, L1_attn_gamma_log, L1_attn_B_re, L1_attn_B_im, L1_attn_C_re, L1_attn_C_im, L1_attn_D, L1_ffn_fast_b, L1_ffn_w_fc, L1_ffn_w_proj, L1_ffn_u, L1_ffn_v, L1_ffn_gate):

    def _L0_attn_ref(x, Wq, Wk, Wv, Wo, bo):
        import jax, jax.numpy as jnp
        import numpy as np
        HEADS = 16
        LOCAL_HEADS = 4
        DIM = 128
        DH = DIM // HEADS
        WINDOW = 128
        BLINDSPOT = 64

        def _look_around(x, buckets):
            pad_cfg = ((0, 0), (1, 0)) + ((0, 0),) * (x.ndim - 2)
            pv = -1.0 if jnp.issubdtype(x.dtype, jnp.floating) else -1
            p = jnp.pad(x, pad_cfg, constant_values=pv)
            return jnp.concatenate([p[:, :buckets], p[:, 1:buckets + 1]], axis=2)

        def _local_attn(q, k, v):
            b, lh, t, e = q.shape
            bm = b * lh
            buckets = t // WINDOW
            bq = q.reshape(bm, buckets, WINDOW, e)
            bk = k.reshape(bm, buckets, WINDOW, e)
            bv = v.reshape(bm, buckets, WINDOW, e)
            bk2 = _look_around(bk, buckets)
            bv2 = _look_around(bv, buckets)
            ticker = jnp.arange(t, dtype=jnp.int32).reshape(1, buckets, WINDOW)
            bq_k = _look_around(ticker, buckets)
            dots = jnp.einsum('buie,buje->buij', bq, bk2) * e ** (-0.5)
            mask_value = -jnp.finfo(dots.dtype).max
            causal_mask = ticker[:, :, :, None] < bq_k[:, :, None, :]
            pad_mask = bq_k[:, :, None, :] == -1
            dots = jnp.where(causal_mask | pad_mask, mask_value, dots)
            attn = jax.nn.softmax(dots, axis=-1)
            out = jnp.einsum('buij,buje->buie', attn, bv2)
            return out.reshape(b, lh, t, e)

        def _causal_linear_attn(q, k, v):
            b, h, n, e = q.shape
            u = n // BLINDSPOT
            q = jax.nn.softmax(q, axis=-1)
            k = jax.nn.elu(k) + 1.0
            bq = q.reshape(b, h, u, BLINDSPOT, e)
            bk = k.reshape(b, h, u, BLINDSPOT, e)
            bv = v.reshape(b, h, u, BLINDSPOT, e)
            bk_cumsum = jnp.cumsum(bk.sum(axis=-2), axis=-2)
            ctx = jnp.einsum('bhund,bhune->bhude', bk, bv)
            ctx = jnp.cumsum(ctx, axis=2)
            ctx = ctx / (bk_cumsum[..., None] + 1e-06)
            ctx = jnp.pad(ctx, ((0, 0), (0, 0), (1, 0), (0, 0), (0, 0)))[:, :, :u]
            attn = jnp.einsum('bhund,bhude->bhune', bq, ctx)
            return attn.reshape(b, h, n, e)
        b, t, dim = x.shape
        q = x @ Wq
        k = x @ Wk
        v = x @ Wv
        mh = lambda z: z.reshape(b, t, HEADS, DH).transpose(0, 2, 1, 3)
        q, k, v = (mh(q), mh(k), mh(v))
        lq, gq = (q[:, :LOCAL_HEADS], q[:, LOCAL_HEADS:])
        lk, gk = (k[:, :LOCAL_HEADS], k[:, LOCAL_HEADS:])
        lv, gv = (v[:, :LOCAL_HEADS], v[:, LOCAL_HEADS:])
        local_out = _local_attn(lq, lk, lv)
        global_out = _causal_linear_attn(gq, gk, gv)
        attn = jnp.concatenate([local_out, global_out], axis=1)
        attn = attn.transpose(0, 2, 1, 3).reshape(b, t, dim)
        return attn @ Wo + bo

    def _L0_ffn_ref(x, Wqkv, q_scale, k_scale, Wo, ln_g, ln_b, W1, b1, W2, b2):
        import jax, jax.numpy as jnp
        import numpy as np
        DIM = 128
        DEPTH = 6
        HEADS = 16
        DIM_HEAD = 64
        WINDOW = 32
        INNER = HEADS * DIM_HEAD
        DIM_INNER = int(DIM * 4 * 2 / 3)
        QK_SCALE = 8.0

        def shift_tokens(t):
            a, s = jnp.split(t, 2, -1)
            s = jnp.pad(s, ((0, 0), (1, 0), (0, 0)))[:, :-1]
            return jnp.concatenate([a, s], -1)

        def l2norm(t):
            return t / jnp.maximum(jnp.linalg.norm(t, axis=-1, keepdims=True), 1e-12)

        def rotate_half(x):
            x1, x2 = jnp.split(x, 2, -1)
            return jnp.concatenate([-x2, x1], -1)

        def rotary_tables(n):
            half = jnp.arange(0, DIM_HEAD, 2, dtype=jnp.float32)
            inv_freq = 1.0 / 10000.0 ** (half / DIM_HEAD)
            t = jnp.arange(n, dtype=jnp.float32)
            freqs = t[:, None] * inv_freq[None, :]
            freqs = jnp.concatenate([freqs, freqs], -1)
            base_scale = (half + 0.4 * DIM_HEAD) / (1.4 * DIM_HEAD)
            power = (t - n // 2) / (WINDOW // 2)
            scale = base_scale[None, :] ** power[:, None]
            scale = jnp.concatenate([scale, scale], -1)
            return (freqs, scale)

        def local_attention(q, k, v):
            b, h, n, d = q.shape
            w = WINDOW
            nw = n // w
            bq = q.reshape(b, h, nw, w, d)
            bk = k.reshape(b, h, nw, w, d)
            bv = v.reshape(b, h, nw, w, d)

            def look(t):
                p = jnp.pad(t, ((0, 0), (0, 0), (1, 0), (0, 0), (0, 0)))
                return jnp.concatenate([p[:, :, :nw], p[:, :, 1:]], axis=3)
            bk2, bv2 = (look(bk), look(bv))
            seq = jnp.arange(n).reshape(nw, w)
            seq_p = jnp.pad(seq, ((1, 0), (0, 0)), constant_values=-1)
            jt = jnp.concatenate([seq_p[:nw], seq_p[1:]], axis=1)
            it = seq[:, :, None]
            jb = jt[:, None, :]
            mask = (it < jb) | (it > jb + w) | (jb == -1)
            sim = jnp.einsum('bhwie,bhwje->bhwij', bq, bk2) * QK_SCALE
            sim = jnp.where(mask, -jnp.finfo(sim.dtype).max, sim)
            attn = jax.nn.softmax(sim, -1)
            out = jnp.einsum('bhwij,bhwje->bhwie', attn, bv2)
            return out.reshape(b, h, n, d)

        def attn_layer(x, Wqkv, qs, ksc, Wo):
            b, n, _ = x.shape
            qkv = x @ Wqkv
            q, k, v = jnp.split(qkv, 3, -1)
            sh = lambda t: t.reshape(b, n, HEADS, DIM_HEAD).transpose(0, 2, 1, 3)
            q, k, v = (sh(q), sh(k), sh(v))
            q = l2norm(q) * qs
            k = l2norm(k) * ksc
            freqs, scale = rotary_tables(n)
            cos, sin = (jnp.cos(freqs), jnp.sin(freqs))
            q = q * cos * scale + rotate_half(q) * sin * scale
            inv = 1.0 / scale
            k = k * cos * inv + rotate_half(k) * sin * inv
            out = local_attention(q, k, v)
            out = out.transpose(0, 2, 1, 3).reshape(b, n, INNER)
            return out @ Wo

        def ffn_layer(x, g, bln, W1, b1, W2, b2):
            mu = x.mean(-1, keepdims=True)
            var = ((x - mu) ** 2).mean(-1, keepdims=True)
            xn = (x - mu) / jnp.sqrt(var + 1e-05) * g + bln
            hg = xn @ W1 + b1
            a, gate = jnp.split(hg, 2, -1)
            return a * jax.nn.gelu(gate, approximate=False) @ W2 + b2
        for i in range(DEPTH):
            x = attn_layer(shift_tokens(x), Wqkv[i], q_scale[i], k_scale[i], Wo[i]) + x
            x = ffn_layer(shift_tokens(x), ln_g[i], ln_b[i], W1[i], b1[i], W2[i], b2[i]) + x
        return x

    def _L1_attn_ref(x, theta_log, nu_log, gamma_log, B_re, B_im, C_re, C_im, D):
        import jax, jax.numpy as jnp
        import numpy as np
        B, L, D_OUT, D_HIDDEN = (16, 512, 128, 64)
        MAX_PHASE = 6.28
        R_MIN, R_MAX = (0.9, 0.999)

        def _binop(q_i, q_j):
            A_i, b_i = q_i
            A_j, b_j = q_j
            return (A_j * A_i, A_j * b_i + b_j)

        def _reference_tuple_inner(x, theta_log, nu_log, gamma_log, B_re, B_im, C_re, C_im, D):
            diag_lambda = jnp.exp(-jnp.exp(nu_log) + 1j * jnp.exp(theta_log))
            B_norm = (B_re + 1j * B_im) * jnp.exp(gamma_log)[:, None]
            C = C_re + 1j * C_im
            Bu = jnp.einsum('hd,bld->blh', B_norm, x.astype(B_norm.dtype))
            Lam = jnp.broadcast_to(diag_lambda, Bu.shape)
            _, h = jax.lax.associative_scan(_binop, (Lam, Bu), axis=1)
            y = jnp.einsum('oh,blh->blo', C, h).real + D * x
            return (y, h[:, -1])
        return _reference_tuple_inner(x, theta_log, nu_log, gamma_log, B_re, B_im, C_re, C_im, D)[0]

    def _L1_ffn_ref(x, fast_b, w_fc, w_proj, u, v, gate):
        import jax, jax.numpy as jnp
        import numpy as np

        def _bitlinear(x, w_latent):
            scale = jax.lax.stop_gradient(jnp.clip(jnp.mean(jnp.abs(w_latent), axis=1, keepdims=True), 1e-05, None))
            tern = jnp.clip(jnp.round(w_latent / scale), -1.0, 1.0)
            w = w_latent + jax.lax.stop_gradient(tern - w_latent)
            return x @ (w * scale).T
        h = _bitlinear(x, w_fc) + gate * (x @ v.T @ fast_b.T @ u.T)
        r = jnp.maximum(h, 0.0)
        return _bitlinear(r * r, w_proj)
    x = L0_attn_x
    xn = _layernorm(x, axis=-1)
    x = x + _L0_attn_ref(xn, L0_attn_Wq, L0_attn_Wk, L0_attn_Wv, L0_attn_Wo, L0_attn_bo) + _L0_ffn_ref(xn, L0_ffn_Wqkv, L0_ffn_q_scale, L0_ffn_k_scale, L0_ffn_Wo, L0_ffn_ln_g, L0_ffn_ln_b, L0_ffn_W1, L0_ffn_b1, L0_ffn_W2, L0_ffn_b2)
    xn = _layernorm(x, axis=-1)
    x = x + _L1_attn_ref(xn, L1_attn_theta_log, L1_attn_nu_log, L1_attn_gamma_log, L1_attn_B_re, L1_attn_B_im, L1_attn_C_re, L1_attn_C_im, L1_attn_D) + _L1_ffn_ref(xn, L1_ffn_fast_b, L1_ffn_w_fc, L1_ffn_w_proj, L1_ffn_u, L1_ffn_v, L1_ffn_gate)
    return x

_drawn_inputs = setup_inputs


def setup_inputs(seed=0):
    import zlib

    import numpy as np

    out = dict(_drawn_inputs(seed))
    spreads = {'L0_ffn_q_scale': (1.0, 0.6),
     'L0_ffn_k_scale': (1.0, 0.6),
     'L0_ffn_ln_g': (1.0, 0.6),
     'L0_ffn_ln_b': (0.0, 0.8),
     'L0_ffn_b1': (0.0, 0.8),
     'L0_ffn_b2': (0.0, 0.1)}
    factors = {'L0_attn_bo': 8.0,
     'L0_ffn_W1': 3.613,
     'L0_ffn_W2': 3.547,
     'L1_ffn_fast_b': 8.0,
     'L1_ffn_w_fc': 8.0,
     'L1_ffn_w_proj': 7.745,
     'L1_ffn_u': 8.0,
     'L1_ffn_v': 8.0}
    for name, (base, spread) in spreads.items():
        noise = np.random.default_rng([zlib.crc32(name.encode()), seed]).standard_normal(out[name].shape)
        drawn = base * np.exp(spread * noise) if base else spread * noise
        out[name] = jnp.asarray(drawn.astype(out[name].dtype))
    for name, factor in factors.items():
        out[name] = (out[name] * factor).astype(out[name].dtype)
    return out
```

```python
from contextlib import ExitStack

import concourse.bass as bass
import numpy as np
from concourse import mybir

F32 = mybir.dt.float32
BF16 = mybir.dt.bfloat16
ALU = mybir.AluOpType
ACT = mybir.ActivationFunctionType
AX = mybir.AxisListType

P = 128
T = 2048
D = 128
NT = T // P
NG = 4
GT = T // NG
BANK = 512

DEPTH = 6
HEADS = 16
DH = 64
WIN = 32
INNER = HEADS * DH
FF = int(D * 4 * 2 / 3)
FCH = [(c * P, min(P, FF - c * P)) for c in range(-(-FF // P))]
PAD = WIN
XW = PAD + T + P + 1
UT = 4
UNITS = NT * UT
BODY = 8
LAG = 5
CREDIT = 8
MASKED = -1.0e30
LN_EPS = 1e-5
NPAR = 3 + 2 * len(FCH)


def flat(ap):
    return ap.rearrange("p a b -> p (a b)")


def program(nc, a, out):
    ctx = ExitStack()
    with ctx:
        def sb(name, shape, dt=F32):
            return ctx.enter_context(nc.sbuf_tensor(name, shape, dt))

        def sem(name):
            return ctx.enter_context(nc.semaphore(name))

        PS = ctx.enter_context(nc.psum_tensor("PS", [P, 8, BANK], F32))

        XT = sb("XT", [P, T])
        XN = sb("XN", [P, T])
        X0 = sb("X0", [P, XW])
        X1 = sb("X1", [P, XW])
        ident = sb("ident", [P, P])
        ident_bf = sb("ident_bf", [P, P], BF16)
        mean_w = sb("mean_w", [P, P])
        eps_c = sb("eps_c", [P, 1])

        loaded_x = sem("loaded_x")
        loaded_const = sem("loaded_const")
        const_ready = sem("const_ready")
        ident_ready = sem("ident_ready")

        a_w = sb("a_w", [P, 4 * D])
        a_bo = sb("a_bo", [P, 1])
        l_w = sb("l_w", [P, 8, P])
        l_vec = sb("l_vec", [P, 5])
        l_gate = sb("l_gate", [P, 1])
        l_b = sb("l_b", [P, D])
        l_ct = sb("l_ct", [P, D])
        l_fb = sb("l_fb", [16, 16])
        l_ut = sb("l_ut", [16, 512])
        l_v = sb("l_v", [16, D])
        loaded_a = sem("loaded_a")
        loaded_l = sem("loaded_l")
        w = dict(PS=PS, XT=XT, XN=XN, X0=X0, X1=X1, ident=ident, ident_bf=ident_bf, mean_w=mean_w, eps_c=eps_c,
                      loaded_x=loaded_x, loaded_const=loaded_const, const_ready=const_ready,
                      ident_ready=ident_ready, a_w=a_w, a_bo=a_bo, l_w=l_w, l_vec=l_vec, l_gate=l_gate, l_b=l_b,
                      l_ct=l_ct, l_fb=l_fb, l_ut=l_ut, l_v=l_v, loaded_a=loaded_a, loaded_l=loaded_l)
        stage_norm_input(nc, a, w)
        stage_mixed_attention(nc, a, w)
        stage_layers(nc, a, w)
        stage_last_layer(nc, a, w, out)


def stage_norm_input(nc, a, m):
    PS, XT, XN, X0, X1 = m["PS"], m["XT"], m["XN"], m["X0"], m["X1"]
    with ExitStack() as ctx:
        def sb(name, shape, dt=F32):
            return ctx.enter_context(nc.sbuf_tensor(name, shape, dt))

        def sem(name):
            return ctx.enter_context(nc.semaphore(name))

        xin = sb("xin", [P, NT, D])
        sqr = sb("sqr", [P, T])
        turned = sem("turned")
        xt_ready = sem("xt_ready")
        mean_done = sem("mean_done")
        centred = sem("centred")
        squared = sem("squared")
        var_done = sem("var_done")
        logged = sem("logged")
        rstd_ready = sem("rstd_ready")
        xn_ready = sem("xn_ready")
        x0_set = sem("x0_set")
        block = ctx.enter_context(nc.Block())

        @block.sync
        def _(sp):
            sp.dma_start(m["ident"][:, :], a["c_ident"]).then_inc(m["loaded_const"], 16)
            for q in range(NG):
                sp.dma_start(xin[:, 4 * q:4 * q + 4, :],
                             a["L0_attn_x"][0, q * GT:(q + 1) * GT, :].rearrange("(n p) d -> p n d", p=P))\
                  .then_inc(m["loaded_x"], 16)
            sp.dma_start(m["a_w"][:, :], a["a_w"]).then_inc(m["loaded_a"], 16)
            sp.dma_start(m["a_bo"][:, :], a["a_bo"]).then_inc(m["loaded_a"], 16)
            for t, n in ((m["l_vec"], "l_vec"), (m["l_gate"], "l_gate"), (m["l_b"], "l_b"), (m["l_ct"], "l_ct"),
                         (m["l_fb"], "L1_ffn_fast_b"), (m["l_ut"], "l_ut"), (m["l_v"], "L1_ffn_v")):
                sp.dma_start(t[:, :], a[n]).then_inc(m["loaded_l"], 16)
            sp.dma_start(m["l_w"][:, :, :], a["l_w"]).then_inc(m["loaded_l"], 16)

        @block.gpsimd
        def _(pool):
            pool.memset(m["mean_w"][:, :], 1.0 / D).then_inc(m["const_ready"], 1)
            pool.memset(m["eps_c"][:, :], LN_EPS).then_inc(m["const_ready"], 1)
            pool.memset(X0[:, :], 0.0).then_inc(m["const_ready"], 1)
            pool.memset(X1[:, :], 0.0).then_inc(m["const_ready"], 1)

        @block.tensor
        def _(pe):
            pe.wait_ge(m["loaded_const"], 16)
            pe.wait_ge(m["loaded_x"], 16 * NG)
            for n in range(NT):
                pe.transpose(PS[:, n // 4, (n % 4) * P:(n % 4 + 1) * P], xin[:, n, :], m["ident"][:, :])\
                  .then_inc(turned, 1)
            pe.wait_ge(m["const_ready"], 4)
            for g in range(NG):
                pe.wait_ge(xt_ready, g + 1)
                pe.matmul(PS[:, 4 + g, :], m["mean_w"][:, :], XT[:, g * GT:(g + 1) * GT], start=True, stop=True)\
                  .then_inc(mean_done, 1)
            for g in range(NG):
                pe.wait_ge(squared, g + 1)
                pe.matmul(PS[:, g, :], m["mean_w"][:, :], sqr[:, g * GT:(g + 1) * GT], start=True, stop=True)\
                  .then_inc(var_done, 1)

        @block.scalar
        def _(act):
            for g in range(NG):
                act.wait_ge(turned, 4 * g + 4)
                act.activation(XT[:, g * GT:(g + 1) * GT], PS[:, g, :], ACT.Copy).then_inc(xt_ready, 1)
            for g in range(NG):
                act.wait_ge(centred, g + 1)
                act.activation(sqr[:, g * GT:(g + 1) * GT], XN[:, g * GT:(g + 1) * GT], ACT.Square)\
                   .then_inc(squared, 1)
            act.wait_ge(var_done, NG)
            act.wait_ge(m["const_ready"], 4)
            act.activation(sqr[:, :], flat(PS[:, 0:4, :]), ACT.Ln, bias=m["eps_c"][:, 0:1]).then_inc(logged, 1)
            act.wait_ge(logged, 1)
            act.activation(sqr[:, :], sqr[:, :], ACT.Exp, scale=-0.5).then_inc(rstd_ready, 1)

        @block.vector
        def _(dve):
            dve.wait_ge(m["loaded_const"], 16)
            dve.tensor_copy(m["ident_bf"][:, :], m["ident"][:, :]).then_inc(m["ident_ready"], 1)
            for g in range(NG):
                dve.wait_ge(mean_done, g + 1)
                dve.tensor_tensor(XN[:, g * GT:(g + 1) * GT], XT[:, g * GT:(g + 1) * GT], PS[:, 4 + g, :],
                                  ALU.subtract).then_inc(centred, 1)
            dve.wait_ge(rstd_ready, 1)
            dve.wait_ge(m["const_ready"], 4)
            for g in range(NG):
                cols = slice(g * GT, (g + 1) * GT)
                dve.tensor_tensor(XN[:, cols], XN[:, cols], sqr[:, cols], ALU.mult).then_inc(xn_ready, 1)
                dve.wait_ge(xn_ready, g + 1)
                dve.tensor_copy(X0[0:64, PAD + g * GT:PAD + (g + 1) * GT], XN[0:64, cols]).then_inc(x0_set, 1)
                dve.tensor_copy(X0[64:128, PAD + 1 + g * GT:PAD + 1 + (g + 1) * GT], XN[64:128, cols])\
                   .then_inc(x0_set, 1)


def stage_mixed_attention(nc, a, m):
    PS, XT, XN = m["PS"], m["XT"], m["XN"]
    LH, E = 4, 8
    LW = LH * E
    GW = D - LW
    GH = GW // E
    BLK = 64
    PA = PS[:, 0, :]
    PB = PS[0:LW, 1, :]
    SCO = PS[:, 2:4, :].rearrange("p b n -> p (b n)").rearrange("p (h n) -> p h n", h=LH)
    PTB = PS[:, 4:6, :].rearrange("p b n -> p (b n)")
    QF = PS[0:GW, 6, 0:P]
    CT = PS[:, 6, P:2 * P]
    OG = PS[:, 6, 2 * P:2 * P + GW]
    OL = PS[:, 6, 2 * P + GW:2 * P + GW + LH * (E + 1)].rearrange("p (h e) -> p h e", h=LH)
    CX = PS[0:GW, 7, 0:GW + 1]

    with ExitStack() as ctx:
        def sb(name, shape, dt=F32):
            return ctx.enter_context(nc.sbuf_tensor(name, shape, dt))

        def sem(name):
            return ctx.enter_context(nc.semaphore(name))

        wq_z = sb("wq_z", [P, LH, LW])
        maskf = sb("a_maskf", [P, 2, 2 * P])
        mask = sb("a_mask", [P, 2, 2 * P], BF16)
        bmask = sb("a_bmask", [GW, GW])
        ones = sb("a_ones", [P, 1])
        xs = [sb(f"a_xs{i}", [P, P]) for i in range(2)]
        qk = [sb(f"a_qk{i}", [P, 2 * D]) for i in range(2)]
        kt = [sb(f"a_kt{i}", [LW, P]) for i in range(4)]
        qz = [sb(f"a_qz{i}", [LW, LH, P]) for i in range(2)]
        vx = [sb(f"a_vx{i}", [P, GW + 1]) for i in range(2)]
        vl = [sb(f"a_vl{i}", [P, LH, E + 1]) for i in range(4)]
        qm = [sb(f"a_qm{i}", [P, GH]) for i in range(2)]
        qd = [sb(f"a_qd{i}", [P, GW]) for i in range(2)]
        qe = [sb(f"a_qe{i}", [P, GW]) for i in range(2)]
        qs = [sb(f"a_qs{i}", [P, GH]) for i in range(2)]
        qi = [sb(f"a_qi{i}", [P, GH]) for i in range(2)]
        qf = [sb(f"a_qf{i}", [P, GW]) for i in range(2)]
        ke = [sb(f"a_ke{i}", [P, GW]) for i in range(2)]
        kp = [sb(f"a_kp{i}", [P, GW]) for i in range(2)]
        kf = [sb(f"a_kf{i}", [P, GW]) for i in range(2)]
        qft = [sb(f"a_qft{i}", [GW, P]) for i in range(2)]
        cx = sb("a_cx", [GW, GW + 1])
        cd = sb("a_cd", [GW, 1])
        cr = sb("a_cr", [GW, 1])
        cn = [sb(f"a_cn{i}", [GW, GW]) for i in range(2)]
        mx = sb("a_mx", [P, LH])
        sm = sb("a_sm", [P, LH, 2 * P])
        pr = [sb(f"a_pr{i}", [P, LH, 2 * P]) for i in range(2)]
        pt = sb("a_pt", [P, LH * 2 * P])
        oi = sb("a_oi", [P, LH])
        oc = [sb(f"a_oc{i}", [P, D]) for i in range(4)]
        oct_ = sb("a_oct", [P, P])

        loaded = sem("a_loaded")
        prepared = sem("a_prepared")
        zeroed = sem("a_zeroed")
        pe_sems = ("proj", "qft", "cx", "sc", "pt", "pv", "ct", "out")
        act_sems = ("qk", "kt", "qz", "vx", "vl", "ke", "qe", "qfe", "ex", "pte", "cte")
        dve_sems = ("qm", "qs", "qi", "kf", "cxa", "cda", "cra", "cn", "mx", "sm", "og", "oi", "ol", "xt")
        pool_sems = ("xs", "qd", "qf", "kp")
        sems = {f"{e}_{n}": sem(f"a_{e}_{n}") for e, ns in (
            ("pe", pe_sems), ("act", act_sems), ("dve", dve_sems), ("pool", pool_sems)) for n in ns}
        S = sems
        block = ctx.enter_context(nc.Block())
        TB = 4

        def n_(b, j):
            return b * TB + (CREDIT + j + 1)

        def n2(b, j, i):
            return b * (2 * TB) + (CREDIT + 2 * j + i + 1)

        def credit(eng, names):
            for n in names:
                eng.sem_inc(sems[n], CREDIT)

        def tiles(eng, slot):
            for k in range(TB):
                slot(0, k, lambda lag, k=k: k >= lag)
            with eng.Fori(1, NT // TB) as b:
                for k in range(TB):
                    slot(b, k, lambda lag: True)
            for k in range(3):
                slot(NT // TB, k, lambda lag, k=k: k < lag)

        @block.sync
        def _(sp):
            sp.dma_start(maskf[:, :, :], a["a_mask"]).then_inc(loaded, 16)
            sp.dma_start(bmask[:, :], a["a_bmask"]).then_inc(loaded, 16)

        @block.tensor
        def _(pe):
            def slot(b, k, on_):
                if on_(0):
                    pe.wait_ge(S["pool_xs"], n_(b, k))
                    pe.wait_ge(S["act_vl"], n_(b, k) - 1)
                    x = xs[k % 2][:, :]
                    pe.matmul(PA[:, 0:3 * D], x, m["a_w"][:, 0:3 * D], start=True, stop=True)
                    pe.matmul(PA[0:LW, 3 * D:4 * D], m["a_w"][:, D:D + LW], x, start=True, stop=True)
                    for h in range(LH):
                        last = pe.matmul(PB[:, h * P:(h + 1) * P], wq_z[:, h, :], x, start=True, stop=True)
                    last.then_inc(S["pe_proj"], 1)
                if on_(1):
                    j = k - 1
                    pe.wait_ge(S["pool_qf"], n_(b, j))
                    pe.wait_ge(S["dve_og"], n_(b, j) - 1)
                    pe.wait_ge(S["dve_ol"], n_(b, j) - 2)
                    pe.wait_ge(S["dve_xt"], n_(b, j) - 3)
                    pe.transpose(QF, qf[j % 2][:, :], m["ident"][:, :]).then_inc(S["pe_qft"], 1)
                if on_(2):
                    j = k - 2
                    pe.wait_ge(S["act_ex"], n_(b, j))
                    pe.wait_ge(S["act_pte"], n_(b, j) - 1)
                    for h in range(LH):
                        for c in range(2):
                            last = pe.transpose(PTB[:, (2 * h + c) * P:(2 * h + c + 1) * P],
                                                pr[j % 2][:, h, c * P:(c + 1) * P], m["ident"][:, :])
                    last.then_inc(S["pe_pt"], 1)
                if on_(1):
                    j = k - 1
                    def linear(i):
                        rows = slice(BLK * i, BLK * i + BLK)
                        pe.wait_ge(S["act_qfe"], n_(b, j))
                        pe.wait_ge(S["dve_cn"], n2(b, j, i) - 1)
                        pe.matmul(OG[rows, :], qft[j % 2][:, rows], cn[i][:, :], start=True, stop=True)
                        pe.wait_ge(S["dve_kf"], n_(b, j))
                        pe.wait_ge(S["act_vx"], n_(b, j))
                        pe.matmul(CX, kf[j % 2][rows, :], vx[j % 2][rows, :], start=True, stop=True)\
                          .then_inc(S["pe_cx"], 1)

                    linear(0)
                    pe.wait_ge(S["act_kt"], n_(b, j))
                    pe.wait_ge(S["act_qz"], n_(b, j))
                    pe.wait_ge(S["dve_sm"], n_(b, j) - 1)
                    first = isinstance(b, int) and b == 0 and j == 0
                    for h in range(LH):
                        pe.matmul(SCO[:, h, :], m["ident_bf"][:, :], mask[:, 0 if first else 1, :],
                                  start=(h % 2 == 0), stop=False, skip_group_check=True)
                    for h in range(LH):
                        for c in range(2):
                            last = pe.matmul(SCO[:, h, c * P:(c + 1) * P], qz[j % 2][:, h, :],
                                             kt[(j - 1 + c) % 4][:, :], start=False, stop=True,
                                             skip_group_check=True)
                    last.then_inc(S["pe_sc"], 1)
                    linear(1)
                if on_(2):
                    j = k - 2
                    pe.wait_ge(S["act_pte"], n_(b, j))
                    pe.wait_ge(S["act_vl"], n_(b, j))
                    if not on_(1):
                        pe.wait_ge(S["dve_og"], n_(b, k - 2))
                        pe.wait_ge(S["dve_ol"], n_(b, k - 3))
                        pe.wait_ge(S["dve_xt"], n_(b, k - 4))
                    for h in range(LH):
                        for c in range(2):
                            last = pe.matmul(OL[:, h, :], pt[:, (2 * h + c) * P:(2 * h + c + 1) * P],
                                             vl[(j - 1 + c) % 4][:, h, :], start=(c == 0), stop=(c == 1))
                    last.then_inc(S["pe_pv"], 1)
                if on_(3):
                    j = k - 3
                    pe.wait_ge(S["dve_ol"], n_(b, j))
                    if not on_(2):
                        pe.wait_ge(S["dve_xt"], n_(b, j) - 1)
                    pe.transpose(CT, oc[j % 4][:, :], m["ident"][:, :]).then_inc(S["pe_ct"], 1)
                    pe.wait_ge(S["act_cte"], n_(b, j))
                    pe.matmul(CT, m["a_w"][:, 3 * D:4 * D], oct_[:, :], start=True, stop=True).then_inc(S["pe_out"], 1)

            credit(pe, ["pe_" + n for n in pe_sems])
            pe.wait_ge(prepared, 3)
            pe.wait_ge(zeroed, 2)
            pe.wait_ge(m["loaded_a"], 32)
            tiles(pe, slot)

        @block.scalar
        def _(act):
            def slot(b, k, on_):
                if on_(1):
                    j = k - 1
                    act.wait_ge(S["pe_qft"], n_(b, j))
                    act.wait_ge(S["pe_cx"], n2(b, j - 2, 1))
                    act.activation(qft[j % 2][:, :], QF, ACT.Copy).then_inc(S["act_qfe"], 1)
                if on_(2):
                    j = k - 2
                    act.wait_ge(S["pe_pt"], n_(b, j))
                    act.wait_ge(S["pe_pv"], n_(b, j) - 1)
                    act.activation(pt[:, :], PTB, ACT.Copy).then_inc(S["act_pte"], 1)
                if on_(0):
                    n = n_(b, k)
                    i = k % 2
                    act.wait_ge(S["pe_proj"], n)
                    act.wait_ge(S["pool_qd"], n - 2)
                    act.wait_ge(S["pool_kp"], n - 2)
                    act.wait_ge(S["act_ke"], n - 2)
                    act.activation(qk[i][:, :], PA[:, 0:2 * D], ACT.Copy).then_inc(S["act_qk"], 1)
                    act.wait_ge(S["pe_sc"], n - 2)
                    act.activation(kt[k % 4][:, :], PA[0:LW, 3 * D:4 * D], ACT.Copy).then_inc(S["act_kt"], 1)
                    act.activation(qz[i][:, :, :].rearrange("p h n -> p (h n)"), PB, ACT.Copy)\
                       .then_inc(S["act_qz"], 1)
                    act.wait_ge(S["pe_cx"], n2(b, k - 2, 1))
                    act.activation(vx[i][:, 0:GW], PA[:, 2 * D + LW:3 * D], ACT.Copy).then_inc(S["act_vx"], 1)
                    act.wait_ge(S["pe_pv"], n - 3)
                    act.activation(vl[k % 4][:, :, 0:E],
                                   PA[:, 2 * D:2 * D + LW].rearrange("p (h e) -> p h e", h=LH), ACT.Copy)\
                       .then_inc(S["act_vl"], 1)
                    act.wait_ge(S["act_qk"], n)
                    act.wait_ge(S["dve_kf"], n - 2)
                    act.activation(ke[i][:, :], qk[i][:, D + LW:2 * D], ACT.Exp).then_inc(S["act_ke"], 1)
                    act.wait_ge(S["pool_qd"], n)
                    act.wait_ge(S["pool_qf"], n - 2)
                    act.activation(qe[i][:, :], qd[i][:, :], ACT.Exp).then_inc(S["act_qe"], 1)
                if on_(1):
                    j = k - 1
                    act.wait_ge(S["dve_sm"], n_(b, j))
                    act.wait_ge(S["pe_pt"], n_(b, j) - 2)
                    act.activation(pr[j % 2][:, :, :], sm[:, :, :], ACT.Exp, scale=float(E) ** -0.5)\
                       .then_inc(S["act_ex"], 1)
                if on_(3):
                    j = k - 3
                    act.wait_ge(S["pe_ct"], n_(b, j))
                    act.wait_ge(S["pe_out"], n_(b, j) - 1)
                    act.activation(oct_[:, :], CT, ACT.Copy).then_inc(S["act_cte"], 1)

            credit(act, ["act_" + n for n in act_sems])
            act.wait_ge(zeroed, 2)
            tiles(act, slot)

        @block.vector
        def _(dve):
            def heads(x, n=GH):
                return x.rearrange("p (h e) -> p h e", h=n)

            def slot(b, k, on_):
                if on_(0):
                    n = n_(b, k)
                    i = k % 2
                    dve.wait_ge(S["act_qk"], n)
                    dve.wait_ge(S["pool_qd"], n - 2)
                    dve.tensor_reduce(qm[i][:, :], heads(qk[i][:, LW:D]), AX.X, ALU.max).then_inc(S["dve_qm"], 1)
                def context(j, i):
                    nb = n2(b, j, i)
                    dve.wait_ge(S["pe_cx"], nb)
                    dve.wait_ge(S["dve_cn"], nb - 1)
                    dve.tensor_tensor(cx[:, :], CX, cx[:, :], ALU.add).then_inc(S["dve_cxa"], 1)
                    dve.wait_ge(S["dve_cxa"], nb)
                    dve.tensor_scalar(cd[:, :], cx[:, GW:GW + 1], 1e-6, None, ALU.add).then_inc(S["dve_cda"], 1)
                    dve.wait_ge(S["dve_cda"], nb)
                    dve.reciprocal(cr[:, :], cd[:, :]).then_inc(S["dve_cra"], 1)
                    dve.wait_ge(S["dve_cra"], nb)
                    dve.scalar_tensor_tensor(out=cn[(i + 1) % 2][:, :], in0=cx[:, 0:GW], scalar=cr[:, 0:1],
                                             in1=bmask[:, :], op0=ALU.mult, op1=ALU.mult).then_inc(S["dve_cn"], 1)

                if on_(1):
                    j = k - 1
                    context(j, 0)
                    n = n_(b, j)
                    dve.wait_ge(S["pe_sc"], n)
                    dve.tensor_reduce(mx[:, :], SCO, AX.X, ALU.max).then_inc(S["dve_mx"], 1)
                    dve.wait_ge(S["dve_mx"], n)
                    dve.wait_ge(S["act_ex"], n - 1)
                    dve.tensor_tensor(sm[:, :, :], SCO, mx[:, :].unsqueeze(2).to_broadcast([P, LH, 2 * P]),
                                      ALU.subtract).then_inc(S["dve_sm"], 1)
                    context(j, 1)
                if on_(0):
                    n = n_(b, k)
                    i = k % 2
                    dve.wait_ge(S["act_qe"], n)
                    dve.tensor_reduce(qs[i][:, :], heads(qe[i][:, :]), AX.X, ALU.add).then_inc(S["dve_qs"], 1)
                    dve.wait_ge(S["dve_qs"], n)
                    dve.wait_ge(S["pool_qf"], n - 2)
                    dve.reciprocal(qi[i][:, :], qs[i][:, :]).then_inc(S["dve_qi"], 1)
                    dve.wait_ge(S["act_ke"], n)
                    dve.wait_ge(S["pool_kp"], n)
                    dve.wait_ge(S["pe_cx"], n2(b, k - 2, 1))
                    dve.scalar_tensor_tensor(out=kf[i][:, :], in0=ke[i][:, :], scalar=1.0, in1=kp[i][:, :],
                                             op0=ALU.min, op1=ALU.add).then_inc(S["dve_kf"], 1)
                if on_(3):
                    dve.wait_ge(S["pe_out"], n_(b, k - 3))
                if on_(2):
                    dve.wait_ge(S["pe_pv"], n_(b, k - 2))
                if on_(1):
                    j = k - 1
                    dve.wait_ge(S["pe_cx"], n2(b, j, 1))
                    dve.wait_ge(S["pe_ct"], n_(b, j) - 4)
                    dve.tensor_copy(oc[j % 4][:, LW:D], OG).then_inc(S["dve_og"], 1)
                if on_(2):
                    j = k - 2
                    n = n_(b, j)
                    dve.reciprocal(oi[:, :], OL[:, :, E]).then_inc(S["dve_oi"], 1)
                    dve.wait_ge(S["dve_oi"], n)
                    dve.tensor_tensor(heads(oc[j % 4][:, 0:LW], LH), OL[:, :, 0:E],
                                      oi[:, :].unsqueeze(2).to_broadcast([P, LH, E]), ALU.mult)\
                       .then_inc(S["dve_ol"], 1)
                if on_(3):
                    j = k - 3
                    cols = bass.ds(b * (TB * P) + j * P, P)
                    dve.scalar_tensor_tensor(out=XT[:, cols], in0=CT, scalar=m["a_bo"][:, 0:1], in1=XT[:, cols],
                                             op0=ALU.add, op1=ALU.add).then_inc(S["dve_xt"], 1)

            credit(dve, ["dve_" + n for n in dve_sems])
            dve.wait_ge(loaded, 32)
            dve.wait_ge(m["loaded_a"], 32)
            dve.tensor_copy(mask[:, :, :], maskf[:, :, :]).then_inc(prepared, 1)
            dve.memset(cx[:, :], 0.0).then_inc(prepared, 1)
            dve.memset(cn[0][:, :], 0.0).then_inc(prepared, 1)
            dve.wait_ge(prepared, 3)
            dve.wait_ge(zeroed, 2)
            tiles(dve, slot)

        @block.gpsimd
        def _(pool):
            def heads(x):
                return x.rearrange("p (h e) -> p h e", h=GH)

            def slot(b, k, on_):
                if on_(0):
                    n = n_(b, k)
                    i = k % 2
                    pool.wait_ge(S["pe_proj"], n - 2)
                    pool.tensor_tensor(xs[i][:, :], XN[:, bass.ds(b * (TB * P) + k * P, P)],
                                       ones[:, 0:1].to_broadcast([P, P]), ALU.mult).then_inc(S["pool_xs"], 1)
                    pool.wait_ge(S["act_qk"], n)
                    pool.wait_ge(S["dve_qm"], n)
                    pool.wait_ge(S["act_qe"], n - 2)
                    pool.tensor_tensor(heads(qd[i][:, :]), heads(qk[i][:, LW:D]),
                                       qm[i][:, :].unsqueeze(2).to_broadcast([P, GH, E]), ALU.subtract)\
                        .then_inc(S["pool_qd"], 1)
                    pool.wait_ge(zeroed, 1)
                    pool.wait_ge(S["dve_kf"], n - 2)
                    pool.tensor_scalar(kp[i][:, :], qk[i][:, D + LW:2 * D], 0.0, None, ALU.max)\
                        .then_inc(S["pool_kp"], 1)
                    pool.wait_ge(S["dve_qi"], n)
                    pool.wait_ge(S["act_qe"], n)
                    pool.wait_ge(S["pe_qft"], n - 2)
                    pool.tensor_tensor(heads(qf[i][:, :]), heads(qe[i][:, :]),
                                       qi[i][:, :].unsqueeze(2).to_broadcast([P, GH, E]), ALU.mult)\
                        .then_inc(S["pool_qf"], 1)

            credit(pool, ["pool_" + n for n in pool_sems])
            pool.memset(ones[:, :], 1.0)
            pool.memset(wq_z[:, :, :], 0.0)
            pool.memset(kt[3][:, :], 0.0)
            for v in vx:
                pool.memset(v[:, :], 1.0)
            for v in vl:
                last = pool.memset(v[:, :, :], 1.0)
            last.then_inc(zeroed, 1)
            pool.wait_ge(zeroed, 1)
            pool.wait_ge(m["loaded_a"], 32)
            for h in range(LH):
                last = pool.tensor_copy(wq_z[:, h, h * E:(h + 1) * E], m["a_w"][:, h * E:(h + 1) * E])
            last.then_inc(zeroed, 1)
            pool.wait_ge(zeroed, 2)
            tiles(pool, slot)


def stage_layers(nc, a, m):
    PS, X0, X1 = m["PS"], m["X0"], m["X1"]
    QK = [PS[:, 0, :], PS[:, 1, :]]
    VB = PS[:, 2, :]
    TR = PS[:, 3, :]
    PO = PS[:, 4, :]
    SO = PS[:, 5:7, :]
    SC, OC, OE = 0, 2 * 2 * WIN, DH + 1
    AC = PS[:, 7, 0:P]

    with ExitStack() as ctx:
        def sb(name, shape, dt=F32):
            return ctx.enter_context(nc.sbuf_tensor(name, shape, dt))

        def sem(name):
            return ctx.enter_context(nc.semaphore(name))

        wqkv = sb("wqkv", [P, 3 * INNER])
        wo = sb("wo", [P, HEADS // 2, D])
        w1 = sb("w1", [P, 2 * FF])
        w2 = sb("w2", [P, len(FCH), D])
        par = sb("par", [P, NPAR])
        qks = sb("qks", [P, DEPTH, 4 * DH])
        xpos = sb("xpos", [P, 4 * DH])
        rot = sb("rot", [P, NT + 1, 2 * DH])
        kshift = sb("kshift", [P, 1])
        maskf = sb("maskf", [P, 2, P])
        mask = sb("mask", [P, 2, P], BF16)
        half_c = sb("half_c", [P, 8])
        ones = sb("ones", [P, 1])
        xs = [sb(f"xs{i}", [P, WIN + P]) for i in range(2)]
        lay4 = sb("lay4", [P, 4 * DH])
        tab = [sb(f"tab{i}", [P, 4, DH]) for i in range(2)]
        sq = [sb(f"sq{i}", [P, BANK]) for i in range(2)]
        ss = [sb(f"ss{i}", [P, 8]) for i in range(2)]
        sg = [sb(f"sg{i}", [P, 8]) for i in range(2)]
        rn = [sb(f"rn{i}", [P, 8]) for i in range(2)]
        qn = [sb(f"qn{i}", [P, BANK]) for i in range(2)]
        cm = [sb(f"cm{i}", [P, BANK]) for i in range(2)]
        rs = [sb(f"rs{i}", [P, BANK]) for i in range(2)]
        qr = [sb(f"qr{i}", [P, BANK]) for i in range(2)]
        qkt = [sb(f"qkt{i}", [P, 4, WIN + P]) for i in range(UT)]
        vs = [sb(f"vs{i}", [P, 4, 2, DH + 1]) for i in range(4)]
        mx = [sb(f"mx{i}", [P, 2, 2]) for i in range(2)]
        sm = [sb(f"sm{i}", [P, 2, 2, DH]) for i in range(2)]
        pr = [sb(f"pr{i}", [P, 2, P]) for i in range(2)]
        po = [sb(f"po{i}", [P, BANK]) for i in range(2)]
        ri = [sb(f"ri{i}", [P, 2, 2]) for i in range(2)]
        on = [sb(f"on{i}", [P, 2, 2, DH]) for i in range(2)]
        xc = sb("xc", [P, T])
        st = sb("st", [P, T])
        gl = [sb(f"gl{i}", [P, GT]) for i in range(2)]
        hb = [[sb(f"hb{i}_{c}", [P, GT]) for c in range(len(FCH))] for i in range(2)]

        loaded_tab, loaded_qkv, loaded_wo, loaded_mlp = (sem(n) for n in
                                                        ("loaded_tab", "loaded_qkv", "loaded_wo", "loaded_mlp"))
        ready = sem("ready")
        unit_sems = {n: sem("u_" + n) for n in (
            "qk_done", "v_done", "tr_done", "pv_done", "s_done", "wo_done", "po_done",
            "sq_ready", "v_ready", "qkt_ready", "po_ready", "p_ready",
            "ss_ready", "qn_ready", "cm_ready", "qr_ready", "ri_ready", "on_ready", "mx_ready", "sm_ready",
            "kp_ready", "sg_ready", "rn_ready", "rs_ready")}
        S = unit_sems
        x_staged, tab_ready, lay_ready, x1_ready = (sem(n) for n in ("x_staged", "tab_ready", "lay_ready", "x1_ready"))
        mean_done, centred, squared, var_done, logged, rstd_ready, scaled, xn_ready = (
            sem(n) for n in ("f_mean_done", "f_centred", "f_squared", "f_var_done", "f_logged", "f_rstd_ready",
                             "f_scaled", "f_xn_ready"))
        ha_done, hg_done, gl_ready, h_ready, mo_done, x0_ready = (
            sem(n) for n in ("ha_done", "hg_done", "gl_ready", "h_ready", "mo_done", "x0_ready"))
        block = ctx.enter_context(nc.Block())

        def n_unit(l, b, j):
            return l * UNITS + b * BODY + (CREDIT + j + 1)

        def n_po(l, b, k):
            return l * (UNITS + 1) + b * BODY + (CREDIT + k - 3 + 1)

        def n_tile(l, b, t):
            return l * (NT + 1) + b * 2 + (t + 1)

        def n_x1(l, b, t):
            return l * (2 * NT) + b * 4 + 2 * (t + 1)

        def layer_slots(eng, slot, l):
            for k in range(BODY):
                slot(l, 0, k, lambda lag, k=k: k >= lag)
            with eng.Fori(1, UNITS // BODY) as b:
                for k in range(BODY):
                    slot(l, b, k, lambda lag: True)
            for k in range(LAG):
                slot(l, UNITS // BODY, k, lambda lag, k=k: k < lag)

        @block.sync
        def _(sp):
            sp.dma_start(qks[:, :, :], a["c_qk_scales"]).then_inc(loaded_tab, 16)
            sp.dma_start(xpos[:, :], a["c_xpos"]).then_inc(loaded_tab, 16)
            sp.dma_start(rot[:, :, :], a["c_rot"]).then_inc(loaded_tab, 16)
            sp.dma_start(kshift[:, :], a["c_kshift"]).then_inc(loaded_tab, 16)
            sp.dma_start(maskf[:, :, :], a["c_mask"]).then_inc(loaded_tab, 16)

            def load_qkv(l):
                sp.dma_start(wqkv[:, :], a["L0_ffn_Wqkv"][bass.ds(l, 1), :, :].rearrange("o p n -> p (o n)"))\
                  .then_inc(loaded_qkv, 16)

            def load_wo(l):
                sp.dma_start(flat(wo[:, :, :]), a["l_wo"][bass.ds(l, 1), :, :].rearrange("o p n -> p (o n)"))\
                  .then_inc(loaded_wo, 16)

            def load_mlp(l):
                sp.dma_start(w1[:, :], a["L0_ffn_W1"][bass.ds(l, 1), :, :].rearrange("o p n -> p (o n)"))\
                  .then_inc(loaded_mlp, 16)
                sp.dma_start(flat(w2[:, :, :]), a["l_w2"][bass.ds(l, 1), :, :].rearrange("o p n -> p (o n)"))\
                  .then_inc(loaded_mlp, 16)
                sp.dma_start(par[:, :], a["l_par"][bass.ds(l, 1), :, :].rearrange("o p n -> p (o n)"))\
                  .then_inc(loaded_mlp, 16)

            load_qkv(0)
            load_wo(0)
            load_mlp(0)
            with sp.Fori(0, DEPTH - 1) as l:
                sp.wait_ge(S["v_done"], n_unit(l, 0, UNITS - 1))
                load_qkv(l + 1)
                sp.wait_ge(S["wo_done"], n_unit(l, 0, UNITS - 1))
                load_wo(l + 1)
                sp.wait_ge(x0_ready, l * (2 * NG) + 2 * NG + CREDIT)
                load_mlp(l + 1)

        @block.tensor
        def _(pe):
            def slot(l, b, k, on_):
                if on_(0):
                    g, par_ = k % UT, (k // UT) % 2
                    if g == 0:
                        pe.wait_ge(x_staged, n_tile(l, b, k // UT))
                    pe.wait_ge(S["qn_ready"], n_unit(l, b, k) - 2)
                    w = wqkv[:, 0:2 * INNER].rearrange("p (s n) -> p s n", s=2)[:, :, g * 256:(g + 1) * 256]
                    pe.matmul(QK[k % 2], xs[par_][:, WIN:WIN + P], w, start=True, stop=True).then_inc(S["qk_done"], 1)
                if on_(0):
                    g, par_ = k % UT, (k // UT) % 2
                    pe.wait_ge(S["v_ready"], n_unit(l, b, k) - 1)
                    wv = wqkv[:, 2 * INNER + g * 256:2 * INNER + (g + 1) * 256].rearrange(
                        "p (r h e) -> p h r e", r=2, h=2)
                    for w in range(4):
                        for h in range(2):
                            last = pe.matmul(VB[64 * h:64 * h + 64, w * P:(w + 1) * P],
                                             xs[par_][:, WIN * w:WIN * w + 2 * WIN], wv[:, h, :, :],
                                             start=True, stop=True)
                    last.then_inc(S["v_done"], 1)
                if on_(3) or on_(4):
                    pe.wait_ge(S["po_ready"], n_po(l, b, k) - 1)
                    last = None
                    if on_(3):
                        j = k - 3
                        pe.wait_ge(S["p_ready"], n_unit(l, b, j))
                        for p in range(2):
                            last = pe.transpose(PO[:, p * P:(p + 1) * P], pr[j % 2][:, p, :], m["ident"][:, :])
                    if on_(4):
                        j = k - 4
                        pe.wait_ge(S["on_ready"], n_unit(l, b, j))
                        for p in range(2):
                            last = pe.transpose(PO[:, (2 + p) * P:(3 + p) * P],
                                                on[j % 2][:, p, :, :].rearrange("p a b -> p (a b)"), m["ident"][:, :])
                    last.then_inc(S["po_done"], 1)
                if on_(2):
                    j = k - 2
                    pe.wait_ge(S["qr_ready"], n_unit(l, b, j))
                    pe.wait_ge(S["qkt_ready"], n_unit(l, b, j) - 1)
                    for p in range(4):
                        last = pe.transpose(TR[:, p * P:(p + 1) * P], qr[j % 2][:, p * P:(p + 1) * P], m["ident"][:, :])
                    last.then_inc(S["tr_done"], 1)
                if on_(5):
                    j = k - 5
                    g = j % UT
                    if g == 0:
                        pe.wait_ge(x1_ready, n_x1(l, b, j // UT) - 2 + CREDIT)
                    pe.wait_ge(S["po_ready"], n_po(l, b, k) - 1)
                    for p in range(2):
                        last = pe.matmul(AC, wo[:, 2 * g + p, :], po[(k - 1) % 2][:, (2 + p) * P:(3 + p) * P],
                                         start=(g == 0 and p == 0), stop=(g == UT - 1 and p == 1))
                    last.then_inc(S["wo_done"], 1)
                if on_(4):
                    pe.wait_ge(S["on_ready"], n_unit(l, b, k - 4))
                if on_(3):
                    pe.wait_ge(S["sm_ready"], n_unit(l, b, k - 3))
                    pe.wait_ge(S["v_ready"], n_unit(l, b, k - 3))
                    pe.wait_ge(S["po_ready"], n_po(l, b, k))
                if on_(2):
                    pe.wait_ge(S["qkt_ready"], n_unit(l, b, k - 2))
                    pe.wait_ge(S["kp_ready"], n_unit(l, b, k - 2))
                if on_(2) or on_(3):
                    first_tile = isinstance(b, int) and b == 0 and k - 2 < UT
                    for h in range(2):
                        pe.matmul(SO[:, h, SC:SC + P], m["ident_bf"][:, :], mask[:, 0 if first_tile else 1, :],
                                  start=True, stop=False, skip_group_check=True)
                if on_(3):
                    j = k - 3
                    for p in range(2):
                        for w in range(4):
                            for h in range(2):
                                rows = slice(64 * h, 64 * h + 64)
                                last = pe.matmul(SO[WIN * w:WIN * w + WIN, h, OC + p * OE:OC + (p + 1) * OE],
                                                 po[k % 2][rows, p * P + WIN * w:p * P + WIN * w + WIN],
                                                 vs[j % 4][rows, w, p, :], start=False, stop=True,
                                                 skip_group_check=True)
                    last.then_inc(S["pv_done"], 1)
                if on_(2):
                    j = k - 2
                    g = j % UT
                    for p in range(2):
                        for w in range(4):
                            for h in range(2):
                                rows = slice(64 * h, 64 * h + 64)
                                last = pe.matmul(SO[WIN * w:WIN * w + WIN, h, SC + p * 64:SC + (p + 1) * 64],
                                                 qkt[g][rows, p, WIN + WIN * w:2 * WIN + WIN * w],
                                                 qkt[g][rows, 2 + p, WIN * w:WIN * w + 2 * WIN],
                                                 start=False, stop=True, skip_group_check=True)
                    last.then_inc(S["s_done"], 1)

            def mlp(l):
                pe.wait_ge(x1_ready, n_x1(l, 0, NT - 1) + CREDIT)
                for g in range(NG):
                    pe.matmul(PS[:, g, :], m["mean_w"][:, :], X1[:, PAD + g * GT:PAD + (g + 1) * GT],
                              start=True, stop=True).then_inc(mean_done, 1)
                for g in range(NG):
                    pe.wait_ge(squared, l * NG + (g + 1))
                    pe.matmul(PS[:, 4 + g, :], m["mean_w"][:, :], st[:, g * GT:(g + 1) * GT],
                              start=True, stop=True).then_inc(var_done, 1)
                pe.wait_ge(loaded_mlp, l * 48 + 48)

                def hidden(g, c):
                    o, n = FCH[c]
                    if c == 0:
                        pe.wait_ge(xn_ready, l * NG + (g + 1))
                    if g > 0:
                        pe.wait_ge(h_ready, l * (NG * 3) + (g - 1) * 3 + c + 1)
                    x = xc[:, g * GT:(g + 1) * GT]
                    pe.matmul(PS[0:n, 2 * c + 1, :], w1[:, FF + o:FF + o + n], x, start=True, stop=True)\
                      .then_inc(hg_done, 1)
                    pe.matmul(PS[0:n, 2 * c, :], w1[:, o:o + n], x, start=True, stop=True).then_inc(ha_done, 1)

                def outp(g):
                    pe.wait_ge(h_ready, l * (NG * 3) + g * 3 + 3)
                    if g >= 2:
                        pe.wait_ge(x0_ready, l * (2 * NG) + 2 * (g - 1) + CREDIT)
                    for c, (o, n) in enumerate(FCH):
                        last = pe.matmul(PS[:, 6 + g % 2, :], w2[0:n, c, :], hb[g % 2][c][0:n, :],
                                         start=(c == 0), stop=(c == len(FCH) - 1))
                    last.then_inc(mo_done, 1)

                for g in range(NG):
                    for c in range(len(FCH)):
                        hidden(g, c)
                        if c == 0 and g > 0:
                            outp(g - 1)
                outp(NG - 1)

            for s in (S["qk_done"], S["v_done"], S["tr_done"], S["pv_done"], S["s_done"], S["wo_done"], S["po_done"]):
                pe.sem_inc(s, CREDIT)
            pe.wait_ge(ready, 3)
            with pe.Fori(0, DEPTH) as l:
                pe.wait_ge(loaded_qkv, l * 16 + 16)
                pe.wait_ge(loaded_wo, l * 16 + 16)
                layer_slots(pe, slot, l)
                mlp(l)

        @block.scalar
        def _(act):
            def slot(l, b, k, on_):
                if on_(3) or on_(4):
                    act.wait_ge(S["po_done"], n_po(l, b, k))
                    lo, hi = (0 if on_(3) else 2 * P), (4 * P if on_(4) else 2 * P)
                    if on_(3):
                        act.wait_ge(S["pv_done"], n_unit(l, b, k - 3) - 2)
                    if on_(4):
                        act.wait_ge(S["wo_done"], n_unit(l, b, k - 4) - 2)
                    act.activation(po[k % 2][:, lo:hi], PO[:, lo:hi], ACT.Copy).then_inc(S["po_ready"], 1)
                if on_(2):
                    j = k - 2
                    act.wait_ge(S["tr_done"], n_unit(l, b, j))
                    act.wait_ge(S["kp_ready"], n_unit(l, b, j))
                    act.activation(qkt[j % UT][:, :, WIN:WIN + P], TR.rearrange("p (a b) -> p a b", a=4), ACT.Copy)\
                       .then_inc(S["qkt_ready"], 1)
                if on_(0):
                    act.wait_ge(S["qk_done"], n_unit(l, b, k))
                    act.wait_ge(S["ss_ready"], n_unit(l, b, k) - 2)
                    act.activation(sq[k % 2][:, :], QK[k % 2], ACT.Square).then_inc(S["sq_ready"], 1)
                    act.wait_ge(S["v_done"], n_unit(l, b, k))
                    act.wait_ge(S["pv_done"], n_unit(l, b, k) - 4)
                    act.activation(vs[k % 4][:, :, :, 0:DH], VB.rearrange("p (w r e) -> p w r e", w=4, r=2),
                                   ACT.Copy).then_inc(S["v_ready"], 1)
                if on_(2):
                    j = k - 2
                    act.wait_ge(S["sm_ready"], n_unit(l, b, j))
                    act.wait_ge(S["po_done"], n_po(l, b, k + 1) - 2)
                    act.activation(pr[j % 2][:, :, :].rearrange("p a b -> p (a b)"),
                                   sm[j % 2][:, :, :, :].rearrange("p a b c -> p (a b c)"), ACT.Exp)\
                       .then_inc(S["p_ready"], 1)

            def mlp(l):
                for g in range(NG):
                    act.wait_ge(centred, l * NG + (g + 1))
                    act.activation(st[:, g * GT:(g + 1) * GT], xc[:, g * GT:(g + 1) * GT], ACT.Square)\
                       .then_inc(squared, 1)
                act.wait_ge(var_done, l * NG + NG)
                act.activation(st[:, :], flat(PS[:, 4:8, :]), ACT.Ln, bias=m["eps_c"][:, 0:1]).then_inc(logged, 1)
                act.wait_ge(logged, l + 1)
                act.activation(st[:, :], st[:, :], ACT.Exp, scale=-0.5).then_inc(rstd_ready, 1)
                for g in range(NG):
                    for c, (o, n) in enumerate(FCH):
                        i = 3 * g + c
                        act.wait_ge(hg_done, l * (NG * 3) + (i + 1))
                        act.wait_ge(h_ready, l * (NG * 3) + (i + 1 - 2)) if i >= 2 else None
                        act.activation(gl[i % 2][0:n, :], PS[0:n, 2 * c + 1, :], ACT.Gelu,
                                       bias=par[0:n, 3 + 3 + c:3 + 3 + c + 1]).then_inc(gl_ready, 1)

            for s in (S["sq_ready"], S["v_ready"], S["qkt_ready"], S["po_ready"], S["p_ready"]):
                act.sem_inc(s, CREDIT)
            act.wait_ge(ready, 3)
            with act.Fori(0, DEPTH) as l:
                layer_slots(act, slot, l)
                act.wait_ge(loaded_mlp, l * 48 + 48)
                mlp(l)

        @block.vector
        def _(dve):
            for s in (S["ss_ready"], S["sg_ready"], S["qn_ready"], S["cm_ready"], S["qr_ready"], S["ri_ready"], S["on_ready"],
                      S["mx_ready"], S["sm_ready"], x1_ready, x0_ready):
                dve.sem_inc(s, CREDIT)
            dve.wait_ge(loaded_tab, 80)
            dve.memset(half_c[:, :], -0.5).then_inc(ready, 1)
            dve.memset(ones[:, :], 1.0).then_inc(ready, 1)
            dve.tensor_copy(mask[:, :, :], maskf[:, :, :]).then_inc(ready, 1)

            def heads(x):
                return x.rearrange("p (h e) -> p h e", e=DH)

            def slot(l, b, k, on_):
                if on_(1):
                    j = k - 1
                    n = n_unit(l, b, j)
                    i = j % 2
                    dve.wait_ge(S["rn_ready"], n)
                    dve.wait_ge(S["rs_ready"], n - 2)
                    dve.tensor_tensor(heads(qn[i][:, :]), heads(QK[i]),
                                      rn[i][:, :].unsqueeze(2).to_broadcast([P, 8, DH]), ALU.mult)\
                       .then_inc(S["qn_ready"], 1)
                    dve.wait_ge(S["qn_ready"], n)
                    if j % UT == 0:
                        dve.wait_ge(tab_ready, n_tile(l, b, j // UT))
                    for s in range(2):
                        last = dve.tensor_tensor(
                            heads(cm[i][:, 256 * s:256 * s + 256]), heads(qn[i][:, 256 * s:256 * s + 256]),
                            tab[(j // UT) % 2][:, 2 * s, :].unsqueeze(1).to_broadcast([P, 4, DH]), ALU.mult)
                    last.then_inc(S["cm_ready"], 1)
                if on_(0):
                    n = n_unit(l, b, k)
                    dve.wait_ge(S["sq_ready"], n)
                    dve.tensor_reduce(ss[k % 2][:, :], heads(sq[k % 2][:, :]), AX.X, ALU.add)\
                       .then_inc(S["ss_ready"], 1)
                    dve.wait_ge(S["ss_ready"], n)
                    dve.wait_ge(S["rn_ready"], n - 2)
                    dve.tensor_scalar(sg[k % 2][:, :], ss[k % 2][:, :], 1e-24, None, ALU.max)\
                       .then_inc(S["sg_ready"], 1)
                if on_(1):
                    j = k - 1
                    n = n_unit(l, b, j)
                    dve.wait_ge(S["cm_ready"], n)
                    dve.wait_ge(S["rs_ready"], n)
                    dve.wait_ge(S["tr_done"], n - 2)
                    dve.tensor_tensor(qr[j % 2][:, :], cm[j % 2][:, :], rs[j % 2][:, :], ALU.add)\
                       .then_inc(S["qr_ready"], 1)
                if on_(5) and k % UT == 0:
                    j = k - 5
                    dve.wait_ge(S["wo_done"], n_unit(l, b, j))
                    t0 = b * (2 * P) + (j // UT) * P + PAD
                    for h in range(2):
                        r = slice(64 * h, 64 * h + 64)
                        dve.tensor_tensor(X1[r, bass.ds(t0 + h, P)], AC[r, :], X0[r, bass.ds(t0 + h, P)], ALU.add)\
                           .then_inc(x1_ready, 1)
                if on_(2):
                    j = k - 2
                    n = n_unit(l, b, j)
                    dve.wait_ge(S["s_done"], n)
                    sc = SO[:, :, SC:SC + P].rearrange("p h (r e) -> p h r e", r=2)
                    dve.tensor_reduce(mx[j % 2][:, :, :], sc, AX.X, ALU.max).then_inc(S["mx_ready"], 1)
                    dve.wait_ge(S["mx_ready"], n)
                    dve.wait_ge(S["p_ready"], n - 2)
                    dve.tensor_tensor(sm[j % 2][:, :, :, :].rearrange("p r h e -> p h r e"), sc,
                                      mx[j % 2][:, :, :].unsqueeze(3).to_broadcast([P, 2, 2, DH]), ALU.subtract)\
                       .then_inc(S["sm_ready"], 1)
                if on_(3):
                    j = k - 3
                    n = n_unit(l, b, j)
                    dve.wait_ge(S["pv_done"], n)
                    if on_(2):
                        dve.wait_ge(S["s_done"], n + 1)
                    o = SO[:, :, OC:OC + 2 * OE].rearrange("p h (r e) -> p h r e", e=OE)
                    dve.reciprocal(ri[j % 2][:, :, :], o[:, :, :, DH]).then_inc(S["ri_ready"], 1)
                    dve.wait_ge(S["ri_ready"], n)
                    dve.wait_ge(S["po_done"], n_po(l, b, k + 1) - 2)
                    dve.tensor_tensor(on[j % 2][:, :, :, :].rearrange("p r h e -> p h r e"), o[:, :, :, 0:DH],
                                      ri[j % 2][:, :, :].unsqueeze(3).to_broadcast([P, 2, 2, DH]), ALU.mult)\
                       .then_inc(S["on_ready"], 1)

            def mlp(l):
                for g in range(NG):
                    c0 = g * GT
                    dve.wait_ge(mean_done, l * NG + (g + 1))
                    dve.tensor_tensor(xc[:, c0:c0 + GT], X1[:, PAD + c0:PAD + c0 + GT], PS[:, g, :], ALU.subtract)\
                       .then_inc(centred, 1)
                dve.wait_ge(rstd_ready, l + 1)
                for g in range(NG):
                    cols = slice(g * GT, (g + 1) * GT)
                    dve.tensor_tensor(xc[:, cols], xc[:, cols], st[:, cols], ALU.mult).then_inc(scaled, 1)
                    dve.wait_ge(scaled, l * NG + (g + 1))
                    dve.tensor_scalar(xc[:, cols], xc[:, cols], par[:, 0:1], par[:, 1:2], ALU.mult, ALU.add)\
                       .then_inc(xn_ready, 1)
                for g in range(NG):
                    for c, (o, n) in enumerate(FCH):
                        i = 3 * g + c
                        dve.wait_ge(ha_done, l * (NG * 3) + (i + 1))
                        dve.wait_ge(gl_ready, l * (NG * 3) + (i + 1))
                        if g >= 2:
                            dve.wait_ge(mo_done, l * NG + (g - 1))
                        dve.scalar_tensor_tensor(out=hb[g % 2][c][0:n, :], in0=PS[0:n, 2 * c, :],
                                                 scalar=par[0:n, 3 + c:3 + c + 1], in1=gl[i % 2][0:n, :],
                                                 op0=ALU.add, op1=ALU.mult).then_inc(h_ready, 1)
                        if c == 0 and g > 0:
                            residual(l, g - 1)
                residual(l, NG - 1)

            def residual(l, g):
                dve.wait_ge(mo_done, l * NG + (g + 1))
                for h in range(2):
                    r = slice(64 * h, 64 * h + 64)
                    c0 = PAD + h + g * GT
                    dve.scalar_tensor_tensor(out=X0[r, c0:c0 + GT], in0=PS[r, 6 + g % 2, :], scalar=par[r, 2:3],
                                             in1=X1[r, c0:c0 + GT], op0=ALU.add, op1=ALU.add)\
                       .then_inc(x0_ready, 1)

            with dve.Fori(0, DEPTH) as l:
                layer_slots(dve, slot, l)
                dve.wait_ge(loaded_mlp, l * 48 + 48)
                mlp(l)

        @block.gpsimd
        def _(pool):
            for s in (S["kp_ready"], S["rn_ready"], S["rs_ready"]):
                pool.sem_inc(s, CREDIT)
            for v in vs:
                pool.memset(v[:, :, :, :], 1.0)
            for q in qkt:
                last = pool.memset(q[:, :, :], 0.0)
            last.then_inc(lay_ready, 1)
            pool.wait_ge(lay_ready, 1)
            pool.wait_ge(ready, 3)

            def stage(l, b, t):
                if not (isinstance(b, int) and b == 0 and t < 2):
                    pool.wait_ge(S["v_done"], n_unit(l, b, (t - 1) * UT - 1))
                pool.tensor_tensor(xs[t % 2][:, :], X0[:, bass.ds(b * (2 * P) + t * P, WIN + P)],
                                   ones[:, 0:1].to_broadcast([P, WIN + P]), ALU.mult).then_inc(x_staged, 1)

            def table(l, b, t):
                if not (isinstance(b, int) and b == 0 and t < 2):
                    pool.wait_ge(S["cm_ready"], n_unit(l, b, (t - 1) * UT - 1))
                pool.tensor_tensor(
                    tab[t % 2][:, :, :].rearrange("p (s c) e -> p s (c e)", s=2),
                    lay4[:, :].rearrange("p (s n) -> p s n", s=2),
                    rot[:, bass.ds(b * 2 + t, 1), :].to_broadcast([P, 2, 2 * DH]), ALU.mult).then_inc(tab_ready, 1)

            def slot(l, b, k, on_):
                if on_(1):
                    j = k - 1
                    n = n_unit(l, b, j)
                    i = j % 2
                    pool.wait_ge(S["qn_ready"], n)
                    pool.wait_ge(S["qr_ready"], n - 2)
                    pool.wait_ge(tab_ready, n_tile(l, b, j // UT))
                    for s in range(2):
                        for h in range(2):
                            def part(x, hh):
                                return x[:, 256 * s:256 * s + 256].rearrange(
                                    "p (n h e) -> p n h e", n=4, h=2)[:, :, hh, :]
                            last = pool.tensor_tensor(
                                part(rs[i], h), part(qn[i], 1 - h),
                                tab[(j // UT) % 2][:, 2 * s + 1, 32 * h:32 * h + 32].unsqueeze(1)
                                .to_broadcast([P, 4, 32]), ALU.mult)
                    last.then_inc(S["rs_ready"], 1)
                if on_(0):
                    n = n_unit(l, b, k)
                    i = k % 2
                    g = k % UT
                    pool.wait_ge(S["s_done"], n - 4)
                    pool.wait_ge(S["qkt_ready"], n - 4)
                    pool.tensor_tensor(qkt[g][:, 2:4, 0:WIN], qkt[g][:, 2:4, P:P + WIN],
                                       kshift[:, 0:1].unsqueeze(2).to_broadcast([P, 2, WIN]), ALU.mult)\
                        .then_inc(S["kp_ready"], 1)
                    if k % UT == 1:
                        stage(l, b, k // UT + 1)
                    if k % UT == 2:
                        table(l, b, k // UT + 1)
                    pool.wait_ge(S["sg_ready"], n)
                    pool.wait_ge(S["qn_ready"], n - 2)
                    pool.tensor_tensor(rn[i][:, :], sg[i][:, :], half_c[:, :], ALU.pow).then_inc(S["rn_ready"], 1)

            with pool.Fori(0, DEPTH) as l:
                pool.wait_ge(x0_ready, l * (2 * NG) + CREDIT)
                pool.tensor_tensor(lay4[:, :], xpos[:, :], qks[:, bass.ds(l, 1), :].rearrange("p o n -> p (o n)"),
                                   ALU.mult).then_inc(lay_ready, 1)
                stage(l, 0, 0)
                pool.wait_ge(lay_ready, l + 2)
                table(l, 0, 0)
                layer_slots(pool, slot, l)


def stage_last_layer(nc, a, m, out):
    PS, XT, XN, X0 = m["PS"], m["XT"], m["XN"], m["X0"]
    HID = 64
    FH = 512
    FC = FH // P
    STEPS = T.bit_length() - 1
    TWO_PI = 2.0 * np.pi
    TP_HI = float(np.float32(6.28125))
    TP_LO = float(np.float32(TWO_PI - 6.28125))
    ROUND = 12582912.0
    PI_F = float(np.nextafter(np.float32(np.pi), np.float32(0)))

    with ExitStack() as ctx:
        def sb(name, shape, dt=F32):
            return ctx.enter_context(nc.sbuf_tensor(name, shape, dt))

        def sem(name):
            return ctx.enter_context(nc.semaphore(name))

        sqr = sb("l_sqr", [P, T])
        hs = sb("l_hs", [P, T])
        rr = sb("l_rr", [P, FC, T])
        lw = m["l_w"]
        wabs = sb("l_wabs", [P, 2 * FC, P])
        wt = sb("l_wt", [P, 2 * FC, P])
        wsum = sb("l_wsum", [P, 2 * FC])
        wsc = sb("l_wsc", [P, 2 * FC])
        wsr = sb("l_wsr", [P, 2 * FC])
        ptot = sb("l_ptot", [P, 1])
        wfin = sb("l_wfin", [P, 2 * FC, P])
        wtt = sb("l_wtt", [P, 2 * FC, P])
        t1 = sb("l_t1", [16, FH])
        ex = sb("l_ex", [P, 4])
        ang = sb("l_ang", [P, 2])
        rev = sb("l_rev", [P, 2])
        sc2 = sb("l_sc2", [P, 2])
        ab = sb("l_ab", [P, 2])
        bs = sb("l_bs", [P, D])
        bt = sb("l_bt", [P, D])
        cs = sb("l_cs", [P, D])
        sj = sb("l_sj", [P, P])
        la = sb("l_la", [P, STEPS, 2 * P])
        tmp = [sb(f"l_tmp{i}", [P, GT]) for i in range(2)]
        yt = sb("l_yt", [P, T])
        yo = sb("l_yo", [P, NT, D])

        x1_set, v_step, a_step, p_step = sem("l_x1_set"), sem("l_v_step"), sem("l_a_step"), sem("l_p_step")
        mean_done, centred, squared, var_done, logged, rstd_ready, xn_ready = (
            sem("l_" + n) for n in ("mean_done", "centred", "squared", "var_done", "logged", "rstd_ready", "xn_ready"))
        lam_exp, lam_sin, lam_set, pow_done, pow_ready = (
            sem("l_" + n) for n in ("lam_exp", "lam_sin", "lam_set", "pow_done", "pow_ready"))
        babs, wfin_ready, wt_done, wt_ready, bt_done, bt_ready, t1_done, t1_ready, lr_done, wlr_ready = (
            sem("l_" + n) for n in ("babs", "wfin_ready", "wt_done", "wt_ready", "bt_done", "bt_ready",
                                    "t1_done", "t1_ready", "lr_done", "wlr_ready"))
        c_ready, bu_done, bu_ready, sh_done, hs_ready = (
            sem("l_" + n) for n in ("c_ready", "bu_done", "bu_ready", "sh_done", "hs_ready"))
        h_done, relu_ready, rr_ready, y_done, yd_ready, yt_ready, back_done, yo_ready, stored = (
            sem("l_" + n) for n in ("h_done", "relu_ready", "rr_ready", "y_done", "yd_ready", "yt_ready",
                                    "back_done", "yo_ready", "stored"))
        block = ctx.enter_context(nc.Block())

        scan = [(s, g) for s in range(STEPS) for g in range(NG - 1, -1, -1) if (g + 1) * GT > (1 << s)]

        def scan_count(s, g):
            while (s, g) not in scan:
                s -= 1
            return scan.index((s, g)) + 1

        def hidden_after(n):
            return range(n, n + 1) if n < NG * FC else range(0)

        @block.sync
        def _(sp):
            for g in range(NG):
                sp.wait_ge(yo_ready, g + 1)
                sp.dma_start(out[0, g * GT:(g + 1) * GT, :].rearrange("(n p) d -> p n d", p=P),
                             yo[:, 4 * g:4 * g + 4, :]).then_inc(stored, 16)
            sp.wait_ge(stored, 16 * NG)

        @block.tensor
        def _(pe):
            pe.wait_ge(x1_set, 2 * NG)
            for g in range(NG):
                pe.matmul(PS[:, g, :], m["mean_w"][:, :], XT[:, g * GT:(g + 1) * GT], start=True, stop=True)\
                  .then_inc(mean_done, 1)
            for g in range(NG):
                pe.wait_ge(squared, g + 1)
                pe.matmul(PS[:, 4 + g, :], m["mean_w"][:, :], sqr[:, g * GT:(g + 1) * GT], start=True, stop=True)\
                  .then_inc(var_done, 1)
            pe.wait_ge(centred, NG)
            pe.wait_ge(bt_ready, 1)
            pe.transpose(PS[:, 0, 0:P], bs[:, :], m["ident"][:, :]).then_inc(bt_done, 1)
            for s in range(STEPS - 1):
                pe.wait_ge(lam_set if s == 0 else pow_ready, 2 if s == 0 else s)
                pe.matmul(PS[:, 1, 0:P], la[:, s, P:2 * P], la[:, s, 0:P], start=True, stop=True)
                pe.matmul(PS[:, 1, P:2 * P], la[:, s, 0:P], la[:, s, P:2 * P], start=True, stop=True)\
                  .then_inc(pow_done, 1)
            pe.wait_ge(wfin_ready, 1)
            for c in range(2 * FC):
                last = pe.transpose(PS[:, 2 + c // 4, (c % 4) * P:(c % 4 + 1) * P], wfin[:, c, :], m["ident"][:, :])
            last.then_inc(wt_done, 1)
            pe.wait_ge(bt_ready, 2)
            pe.matmul(PS[0:16, 0, :], m["l_fb"][:, :], m["l_ut"][:, :], start=True, stop=True).then_inc(t1_done, 1)
            pe.wait_ge(t1_ready, 1)
            pe.wait_ge(pow_ready, STEPS - 1)
            pe.matmul(PS[:, 1, :], m["l_v"][:, :], t1[:, :], start=True, stop=True).then_inc(lr_done, 1)
            for g in range(NG):
                pe.wait_ge(xn_ready, g + 1)
                pe.matmul(PS[:, 4 + g, :], bt[:, :], XN[:, g * GT:(g + 1) * GT], start=True, stop=True)\
                  .then_inc(bu_done, 1)
            pe.wait_ge(wlr_ready, 1)

            def hidden(i):
                g, c = i // FC, i % FC
                if i >= 2:
                    pe.wait_ge(relu_ready, i - 1)
                pe.matmul(PS[:, 6 + i % 2, :], wtt[:, c, :], XN[:, g * GT:(g + 1) * GT], start=True, stop=True)\
                  .then_inc(h_done, 1)

            for n, (s, g) in enumerate(scan):
                lo = max(g * GT, 1 << s)
                if s == 0:
                    pe.wait_ge(bu_ready, NG)
                else:
                    need = max(scan_count(s - 1, gg) for gg in
                               range((lo - (1 << s)) // GT, ((g + 1) * GT - (1 << s) - 1) // GT + 1))
                    pe.wait_ge(hs_ready, need)
                if n >= 4:
                    pe.wait_ge(hs_ready, n - 3)
                pe.matmul(PS[:, n % 4, 0:(g + 1) * GT - lo], la[:, s, 0:P],
                          hs[:, lo - (1 << s):(g + 1) * GT - (1 << s)], start=True, stop=True).then_inc(sh_done, 1)
                for i in hidden_after(n):
                    hidden(i)
            pe.wait_ge(hs_ready, len(scan))
            pe.wait_ge(c_ready, 1)
            for g in range(NG):
                cols = slice(g * GT, (g + 1) * GT)
                pe.matmul(PS[:, g, :], cs[:, :], hs[:, cols], start=True, stop=False)
                pe.wait_ge(rr_ready, FC * (g + 1))
                for c in range(FC):
                    last = pe.matmul(PS[:, g, :], wtt[:, FC + c, :], rr[:, c, cols], start=False, stop=(c == FC - 1))
                last.then_inc(y_done, 1)
            for g in range(NG):
                pe.wait_ge(yt_ready, g + 1)
                for n in range(4 * g, 4 * g + 4):
                    last = pe.transpose(PS[:, 4 + g, (n % 4) * P:(n % 4 + 1) * P], yt[:, n * P:(n + 1) * P],
                                        m["ident"][:, :])
                last.then_inc(back_done, 1)

        @block.scalar
        def _(act):
            act.wait_ge(m["loaded_l"], 16 * 8)
            act.activation(ex[:, 0:3], m["l_vec"][:, 0:3], ACT.Exp).then_inc(lam_exp, 1)
            act.wait_ge(lam_exp, 1)
            act.activation(ex[:, 3:4], ex[:, 0:1], ACT.Exp, scale=-1.0).then_inc(lam_exp, 1)
            act.activation(wabs[:, :, :], lw[:, :, :], ACT.Abs).then_inc(babs, 1)
            act.wait_ge(lam_sin, 1)
            act.activation(sc2[:, :], rev[:, :], ACT.Sin).then_inc(lam_exp, 1)
            for g in range(NG):
                act.wait_ge(centred, g + 1)
                act.activation(sqr[:, g * GT:(g + 1) * GT], XN[:, g * GT:(g + 1) * GT], ACT.Square)\
                   .then_inc(squared, 1)
            act.wait_ge(bt_done, 1)
            act.activation(bt[:, :], PS[:, 0, 0:P], ACT.Copy).then_inc(a_step, 1)
            for s in range(STEPS - 1):
                act.wait_ge(pow_done, s + 1)
                act.activation(la[:, s + 1, :], PS[:, 1, 0:2 * P], ACT.Copy).then_inc(pow_ready, 1)
                if s == 2:
                    act.wait_ge(var_done, NG)
                    act.activation(sqr[:, :], flat(PS[:, 4:8, :]), ACT.Ln, bias=m["eps_c"][:, 0:1])\
                       .then_inc(logged, 1)
                    act.wait_ge(logged, 1)
                    act.activation(sqr[:, :], sqr[:, :], ACT.Exp, scale=-0.5).then_inc(rstd_ready, 1)
            act.wait_ge(wt_done, 1)
            act.activation(wtt[:, :, :].rearrange("p c n -> p (c n)"), flat(PS[:, 2:4, :]), ACT.Copy)\
               .then_inc(wt_ready, 1)
            act.wait_ge(t1_done, 1)
            act.activation(t1[:, :], PS[0:16, 0, :], ACT.Copy, scale=m["l_gate"][0:16, 0:1]).then_inc(t1_ready, 1)
            for g in range(NG):
                act.wait_ge(bu_done, g + 1)
                act.activation(hs[:, g * GT:(g + 1) * GT], PS[:, 4 + g, :], ACT.Copy).then_inc(bu_ready, 1)
            for i in range(NG * FC):
                g, c = i // FC, i % FC
                act.wait_ge(h_done, i + 1)
                act.activation(rr[:, c, g * GT:(g + 1) * GT], PS[:, 6 + i % 2, :], ACT.Relu).then_inc(relu_ready, 1)
            for g in range(NG):
                act.wait_ge(back_done, g + 1)
                act.activation(yo[:, 4 * g:4 * g + 4, :].rearrange("p n d -> p (n d)"), PS[:, 4 + g, :], ACT.Copy)\
                   .then_inc(yo_ready, 1)

        @block.gpsimd
        def _(pool):
            for i in range(NG * FC):
                g, c = i // FC, i % FC
                r = rr[:, c, g * GT:(g + 1) * GT]
                pool.wait_ge(relu_ready, i + 1)
                pool.tensor_tensor(r, r, r, ALU.mult).then_inc(rr_ready, 1)

        @block.vector
        def _(dve):
            for g in range(NG):
                for h in range(2):
                    r = slice(64 * h, 64 * h + 64)
                    c0 = g * GT
                    dve.tensor_tensor(XT[r, c0:c0 + GT], XT[r, c0:c0 + GT],
                                      X0[r, PAD + h + c0:PAD + h + c0 + GT], ALU.add).then_inc(x1_set, 1)
            step = [0]

            def chain(ins):
                step[0] += 1
                ins.then_inc(v_step, 1)
                dve.wait_ge(v_step, step[0])

            dve.wait_ge(lam_exp, 2)
            chain(dve.tensor_scalar(ang[:, 0:1], ex[:, 1:2], 1.0 / TWO_PI, None, ALU.mult))
            chain(dve.tensor_scalar(ang[:, 1:2], ex[:, 1:2], 1.0 / TWO_PI, 0.25, ALU.mult, ALU.add))
            chain(dve.tensor_scalar(ang[:, :], ang[:, :], ROUND, ROUND, ALU.add, ALU.subtract))
            for i in range(2):
                chain(dve.scalar_tensor_tensor(out=rev[:, i:i + 1], in0=ang[:, i:i + 1], scalar=-TP_HI,
                                               in1=ex[:, 1:2], op0=ALU.mult, op1=ALU.add))
            chain(dve.scalar_tensor_tensor(out=rev[:, :], in0=ang[:, :], scalar=-TP_LO, in1=rev[:, :],
                                           op0=ALU.mult, op1=ALU.add))
            chain(dve.tensor_scalar(rev[:, 1:2], rev[:, 1:2], float(np.pi / 2), None, ALU.add))
            dve.tensor_scalar(rev[:, :], rev[:, :], PI_F, -PI_F, ALU.min, ALU.max).then_inc(lam_sin, 1)
            for g in range(NG):
                cols = slice(g * GT, (g + 1) * GT)
                dve.wait_ge(mean_done, g + 1)
                dve.tensor_tensor(XN[:, cols], XT[:, cols], PS[:, g, :], ALU.subtract).then_inc(centred, 1)
            dve.tensor_scalar(bs[:, :], m["l_b"][:, :], ex[:, 2:3], None, ALU.mult).then_inc(bt_ready, 1)
            dve.wait_ge(lam_exp, 3)
            chain(dve.tensor_scalar(ab[:, 0:1], sc2[:, 1:2], ex[:, 3:4], None, ALU.mult))
            chain(dve.tensor_scalar(ab[:, 1:2], sc2[:, 0:1], ex[:, 3:4], m["l_vec"][:, 3:4], ALU.mult, ALU.mult))
            for h in range(2):
                chain(dve.tensor_scalar(sj[:, 64 * h:64 * h + 64], m["ident"][:, 64 - 64 * h:128 - 64 * h], ab[:, 1:2],
                                        None, ALU.mult))
            dve.scalar_tensor_tensor(out=la[:, 0, 0:P], in0=m["ident"][:, :], scalar=ab[:, 0:1], in1=sj[:, :],
                                     op0=ALU.mult, op1=ALU.add).then_inc(lam_set, 1)
            dve.scalar_tensor_tensor(out=la[:, 0, P:2 * P], in0=m["ident"][:, :], scalar=ab[:, 0:1], in1=sj[:, :],
                                     op0=ALU.mult, op1=ALU.subtract).then_inc(lam_set, 1)
            dve.tensor_scalar(cs[:, :], m["l_ct"][:, :], m["l_vec"][:, 3:4], None, ALU.mult).then_inc(c_ready, 1)
            dve.wait_ge(babs, 1)
            chain(dve.tensor_reduce(wsum[:, :], wabs[:, :, :], AX.X, ALU.add))
            chain(dve.tensor_reduce(ptot[:, :], wsum[:, FC:2 * FC], AX.X, ALU.add))
            chain(dve.tensor_scalar(wsc[:, 0:FC], wsum[:, 0:FC], 1.0 / D, 1e-5, ALU.mult, ALU.max))
            chain(dve.tensor_scalar(wsc[:, FC:2 * FC], ptot[:, 0:1].to_broadcast([P, FC]), 1.0 / FH, 1e-5,
                                    ALU.mult, ALU.max))
            chain(dve.reciprocal(wsr[:, :], wsc[:, :]))
            wide = [P, 2 * FC, P]
            chain(dve.tensor_tensor(wt[:, :, :], lw[:, :, :], wsr[:, :].unsqueeze(2).to_broadcast(wide), ALU.mult))
            chain(dve.tensor_scalar(wt[:, :, :], wt[:, :, :], ROUND, ROUND, ALU.add, ALU.subtract))
            chain(dve.tensor_scalar(wt[:, :, :], wt[:, :, :], -1.0, 1.0, ALU.max, ALU.min))
            chain(dve.tensor_tensor(wt[:, :, :], wt[:, :, :], lw[:, :, :], ALU.subtract))
            chain(dve.tensor_tensor(wt[:, :, :], wt[:, :, :], lw[:, :, :], ALU.add))
            dve.tensor_tensor(wfin[:, :, :], wt[:, :, :], wsc[:, :].unsqueeze(2).to_broadcast(wide), ALU.mult)\
               .then_inc(wfin_ready, 1)
            dve.wait_ge(a_step, 1)
            dve.sem_inc(bt_ready, 1)
            dve.wait_ge(rstd_ready, 1)
            for g in range(NG):
                cols = slice(g * GT, (g + 1) * GT)
                dve.tensor_tensor(XN[:, cols], XN[:, cols], sqr[:, cols], ALU.mult).then_inc(xn_ready, 1)
            dve.wait_ge(lr_done, 1)
            dve.wait_ge(wt_ready, 1)
            w = wtt[:, 0:FC, :].rearrange("p c n -> p (c n)")
            dve.tensor_tensor(w, w, PS[:, 1, :], ALU.add).then_inc(wlr_ready, 1)
            for n, (s, g) in enumerate(scan):
                lo = max(g * GT, 1 << s)
                cols = slice(lo, (g + 1) * GT)
                if s == 0:
                    dve.wait_ge(bu_ready, NG)
                dve.wait_ge(sh_done, n + 1)
                dve.tensor_tensor(hs[:, cols], PS[:, n % 4, 0:(g + 1) * GT - lo], hs[:, cols], ALU.add)\
                   .then_inc(hs_ready, 1)
            for g in range(NG):
                cols = slice(g * GT, (g + 1) * GT)
                dve.wait_ge(y_done, g + 1)
                dve.scalar_tensor_tensor(out=tmp[g % 2][:, :], in0=XN[:, cols], scalar=m["l_vec"][:, 4:5],
                                         in1=PS[:, g, :], op0=ALU.mult, op1=ALU.add).then_inc(yd_ready, 1)
                dve.wait_ge(yd_ready, g + 1)
                dve.tensor_tensor(yt[:, cols], XT[:, cols], tmp[g % 2][:, :], ALU.add).then_inc(yt_ready, 1)


def constants():
    half = np.arange(0, DH, 2, dtype=np.float32)
    inv_freq = (1.0 / np.power(np.float32(10000.0), half / np.float32(DH))).astype(np.float32)
    freqs = (np.arange(T, dtype=np.float32)[:, None] * inv_freq[None, :]).astype(np.float32).astype(np.float64)
    cos = np.concatenate([np.cos(freqs)] * 2, -1)
    sin = np.concatenate([np.sin(freqs)] * 2, -1)
    rot = np.zeros((P, NT + 1, 2, DH), np.float32)
    rot[:, :NT, 0] = cos.reshape(NT, P, DH).transpose(1, 0, 2)
    rot[:, :NT, 1] = sin.reshape(NT, P, DH).transpose(1, 0, 2)
    base = ((half.astype(np.float64) + 0.4 * DH) / (1.4 * DH))
    base = np.concatenate([base, base])
    power = (np.arange(P) - P // 2)[:, None] / (WIN // 2)
    sc = base[None, :] ** power
    sign = np.concatenate([-np.ones(DH // 2), np.ones(DH // 2)])
    xpos = np.stack([8.0 * sc, 8.0 * sc * sign, 1.0 / sc, sign / sc], 1).astype(np.float32)
    kshift = np.concatenate([base, base])[:, None] ** (P / (WIN // 2))
    i, c = np.arange(P)[:, None] % WIN, np.arange(2 * WIN)[None, :]
    ok = (c >= i) & (c <= i + WIN)
    first = ok & ~((np.arange(P)[:, None] < WIN) & (c < WIN))
    mask = np.stack([np.where(v, 0.0, MASKED) for v in (np.tile(first, 2), np.tile(ok, 2))], 1)
    q, c = np.arange(P)[:, None], np.arange(2 * P)[None, :]
    own = c - P <= q
    a_mask = np.stack([np.where(v, 0.0, MASKED) for v in (own & (c >= P), own)], 1)
    g = np.arange(96) // 8
    return {
        "a_mask": a_mask.astype(np.float32),
        "a_bmask": (g[:, None] == g[None, :]).astype(np.float32),
        "c_ident": np.eye(P, dtype=np.float32),
        "c_rot": rot.reshape(P, NT + 1, 2 * DH),
        "c_xpos": xpos.reshape(P, 4 * DH),
        "c_kshift": kshift.astype(np.float32),
        "c_mask": mask.astype(np.float32),
    }


def lay_out(x):
    def chunks(v):
        z = np.zeros((DEPTH, len(FCH) * P), np.float32)
        z[:, :FF] = v
        return z.reshape(DEPTH, len(FCH), P).transpose(0, 2, 1)

    b1 = np.asarray(x["L0_ffn_b1"])
    par = np.concatenate([np.asarray(x["L0_ffn_ln_g"])[:, :, None], np.asarray(x["L0_ffn_ln_b"])[:, :, None],
                          np.asarray(x["L0_ffn_b2"])[:, :, None], chunks(b1[:, :FF]), chunks(b1[:, FF:])], 2)
    w2 = np.zeros((DEPTH, len(FCH) * P, D), np.float32)
    w2[:, :FF] = np.asarray(x["L0_ffn_W2"])
    qs, ks = np.asarray(x["L0_ffn_q_scale"]), np.asarray(x["L0_ffn_k_scale"])
    h = DH // 2
    def f(n):
        return np.asarray(x[n])

    def twice(n):
        return np.concatenate([f(n), f(n)])

    sign = np.concatenate([np.ones(64), -np.ones(64)]).astype(np.float32)
    vec = np.stack([twice("L1_attn_nu_log"), twice("L1_attn_theta_log"), twice("L1_attn_gamma_log"), sign,
                    f("L1_attn_D")], 1)
    four = np.concatenate([qs, qs[:, h:], qs[:, :h], ks, ks[:, h:], ks[:, :h]], 1)
    return {
        "a_w": np.concatenate([f("L0_attn_W" + c) for c in "qkvo"], 1),
        "a_bo": f("L0_attn_bo")[:, None],
        "l_vec": vec,
        "l_gate": np.broadcast_to(f("L1_ffn_gate").reshape(1, 1), (P, 1)),
        "l_b": np.concatenate([f("L1_attn_B_re"), f("L1_attn_B_im")], 0),
        "l_ct": np.concatenate([f("L1_attn_C_re").T, f("L1_attn_C_im").T], 0),
        "l_ut": f("L1_ffn_u").T,
        "l_w": np.concatenate([f("L1_ffn_w_fc").reshape(4, P, D).transpose(1, 0, 2),
                               f("L1_ffn_w_proj").reshape(P, 4, P)], 1),
        "l_par": par,
        "l_w2": w2.reshape(DEPTH, len(FCH), P, D).transpose(0, 2, 1, 3).reshape(DEPTH, P, len(FCH) * D),
        "l_wo": np.asarray(x["L0_ffn_Wo"]).reshape(DEPTH, HEADS // 2, P, D).transpose(0, 2, 1, 3)
        .reshape(DEPTH, P, HEADS // 2 * D),
        "c_qk_scales": np.broadcast_to(four[None], (P, DEPTH, 4 * DH)),
    }


_INS = ["L0_attn_x", "L0_ffn_Wqkv", "L0_ffn_W1", "L1_ffn_fast_b", "L1_ffn_v"]
_OUTS = [((1, T, D), "float32")]


def kernel(**inputs):
    import concourse.bacc as _bacc
    from concourse.bass_utils import run_bass_kernel_spmd as _run

    nc = _bacc.Bacc("TRN2", target_bir_lowering=False, num_devices=1)
    given = {n: np.asarray(inputs[n]) for n in _INS}
    given.update(lay_out(inputs))
    given.update(constants())
    arrays, args = {}, {}
    for name, v in given.items():
        v = np.ascontiguousarray(v)
        arrays[f"in_{name}_dram"] = v
        args[name] = nc.dram_tensor(f"in_{name}_dram", v.shape, mybir.dt.from_np(v.dtype), kind="ExternalInput").ap()
    shape, dtype = _OUTS[0]
    out = nc.dram_tensor("out_0_dram", shape, mybir.dt.from_np(np.dtype(dtype)), kind="ExternalOutput").ap()
    program(nc, args, out)
    r = _run(nc, [arrays], core_ids=[0])
    return r.results[0]["out_0_dram"]
```

```python
from contextlib import ExitStack

import concourse.bass as bass
import numpy as np
from concourse import mybir

F32 = mybir.dt.float32
BF16 = mybir.dt.bfloat16
ALU = mybir.AluOpType
ACT = mybir.ActivationFunctionType
AX = mybir.AxisListType

P = 128
T = 2048
D = 128
NT = T // P
NG = 4
GT = T // NG
BANK = 512

DEPTH = 6
HEADS = 16
DH = 64
WIN = 32
INNER = HEADS * DH
FF = int(D * 4 * 2 / 3)
FCH = [(c * P, min(P, FF - c * P)) for c in range(-(-FF // P))]
PAD = WIN
XW = PAD + T + P + 1
UT = 4
UNITS = NT * UT
BODY = 8
LAG = 5
CREDIT = 8
MASKED = -1.0e30
LN_EPS = 1e-5
NPAR = 3 + 2 * len(FCH)


def flat(ap):
    return ap.rearrange("p a b -> p (a b)")


def program(nc, a, out):
    ctx = ExitStack()
    with ctx:
        def sb(name, shape, dt=F32):
            return ctx.enter_context(nc.sbuf_tensor(name, shape, dt))

        def sem(name):
            return ctx.enter_context(nc.semaphore(name))

        PS = ctx.enter_context(nc.psum_tensor("PS", [P, 8, BANK], F32))

        XT = sb("XT", [P, T])
        XN = sb("XN", [P, T])
        X0 = sb("X0", [P, XW])
        X1 = sb("X1", [P, XW])
        ident = sb("ident", [P, P])
        ident_bf = sb("ident_bf", [P, P], BF16)
        mean_w = sb("mean_w", [P, P])
        eps_c = sb("eps_c", [P, 1])

        loaded_x = sem("loaded_x")
        loaded_const = sem("loaded_const")
        const_ready = sem("const_ready")
        ident_ready = sem("ident_ready")

        a_w = sb("a_w", [P, 4 * D])
        a_bo = sb("a_bo", [P, 1])
        l_w = sb("l_w", [P, 8, P])
        l_vec = sb("l_vec", [P, 5])
        l_gate = sb("l_gate", [P, 1])
        l_b = sb("l_b", [P, D])
        l_ct = sb("l_ct", [P, D])
        l_fb = sb("l_fb", [16, 16])
        l_ut = sb("l_ut", [16, 512])
        l_v = sb("l_v", [16, D])
        loaded_a = sem("loaded_a")
        loaded_l = sem("loaded_l")

        wqkv = sb("wqkv", [P, 3 * INNER])
        wo = sb("wo", [P, HEADS // 2, D])
        w1 = sb("w1", [P, 2 * FF])
        w2 = sb("w2", [P, len(FCH), D])
        par = sb("par", [P, NPAR])
        qks = sb("qks", [P, DEPTH, 4 * DH])
        xpos = sb("xpos", [P, 4 * DH])
        rot = sb("rot", [P, NT + 1, 2 * DH])
        kshift = sb("kshift", [P, 1])
        maskf = sb("maskf", [P, 2, P])
        loaded_tab, loaded_qkv, loaded_wo, loaded_mlp = (sem(n) for n in
                                                        ("loaded_tab", "loaded_qkv", "loaded_wo", "loaded_mlp"))
        w = dict(PS=PS, XT=XT, XN=XN, X0=X0, X1=X1, ident=ident, ident_bf=ident_bf, mean_w=mean_w, eps_c=eps_c,
                      loaded_x=loaded_x, loaded_const=loaded_const, const_ready=const_ready,
                      ident_ready=ident_ready, a_w=a_w, a_bo=a_bo, l_w=l_w, l_vec=l_vec, l_gate=l_gate, l_b=l_b,
                      l_ct=l_ct, l_fb=l_fb, l_ut=l_ut, l_v=l_v, loaded_a=loaded_a, loaded_l=loaded_l, wqkv=wqkv, wo=wo, w1=w1,
                      w2=w2, par=par, qks=qks, xpos=xpos, rot=rot, kshift=kshift, maskf=maskf,
                      loaded_tab=loaded_tab, loaded_qkv=loaded_qkv, loaded_wo=loaded_wo, loaded_mlp=loaded_mlp)
        stage_norm_input(nc, a, w)
        stage_mixed_attention(nc, a, w)
        stage_layers(nc, a, w)
        stage_last_layer(nc, a, w, out)


def stage_norm_input(nc, a, m):
    PS, XT, XN, X0, X1 = m["PS"], m["XT"], m["XN"], m["X0"], m["X1"]
    with ExitStack() as ctx:
        def sb(name, shape, dt=F32):
            return ctx.enter_context(nc.sbuf_tensor(name, shape, dt))

        def sem(name):
            return ctx.enter_context(nc.semaphore(name))

        xin = sb("xin", [P, NT, D])
        sqr = sb("sqr", [P, T])
        turned = sem("turned")
        xt_ready = sem("xt_ready")
        mean_done = sem("mean_done")
        centred = sem("centred")
        squared = sem("squared")
        var_done = sem("var_done")
        logged = sem("logged")
        rstd_ready = sem("rstd_ready")
        xn_ready = sem("xn_ready")
        x0_set = sem("x0_set")
        block = ctx.enter_context(nc.Block())

        @block.sync
        def _(sp):
            sp.dma_start(m["ident"][:, :], a["c_ident"]).then_inc(m["loaded_const"], 16)
            for q in range(NG):
                sp.dma_start(xin[:, 4 * q:4 * q + 4, :],
                             a["L0_attn_x"][0, q * GT:(q + 1) * GT, :].rearrange("(n p) d -> p n d", p=P))\
                  .then_inc(m["loaded_x"], 16)
            sp.dma_start(m["a_w"][:, :], a["a_w"]).then_inc(m["loaded_a"], 16)
            sp.dma_start(m["a_bo"][:, :], a["a_bo"]).then_inc(m["loaded_a"], 16)
            for t, n in ((m["qks"][:, :, :], "c_qk_scales"), (m["xpos"][:, :], "c_xpos"), (m["rot"][:, :, :], "c_rot"),
                         (m["kshift"][:, :], "c_kshift"), (m["maskf"][:, :, :], "c_mask")):
                sp.dma_start(t, a[n]).then_inc(m["loaded_tab"], 16)
            sp.dma_start(m["wqkv"][:, :], a["L0_ffn_Wqkv"][0, :, :]).then_inc(m["loaded_qkv"], 16)
            sp.dma_start(flat(m["wo"][:, :, :]), a["l_wo"][0, :, :]).then_inc(m["loaded_wo"], 16)
            sp.dma_start(m["w1"][:, :], a["L0_ffn_W1"][0, :, :]).then_inc(m["loaded_mlp"], 16)
            sp.dma_start(flat(m["w2"][:, :, :]), a["l_w2"][0, :, :]).then_inc(m["loaded_mlp"], 16)
            sp.dma_start(m["par"][:, :], a["l_par"][0, :, :]).then_inc(m["loaded_mlp"], 16)
            for t, n in ((m["l_vec"], "l_vec"), (m["l_gate"], "l_gate"), (m["l_b"], "l_b"), (m["l_ct"], "l_ct"),
                         (m["l_fb"], "L1_ffn_fast_b"), (m["l_ut"], "l_ut"), (m["l_v"], "L1_ffn_v")):
                sp.dma_start(t[:, :], a[n]).then_inc(m["loaded_l"], 16)
            sp.dma_start(m["l_w"][:, :, :], a["l_w"]).then_inc(m["loaded_l"], 16)

        @block.gpsimd
        def _(pool):
            pool.memset(m["mean_w"][:, :], 1.0 / D).then_inc(m["const_ready"], 1)
            pool.memset(m["eps_c"][:, :], LN_EPS).then_inc(m["const_ready"], 1)
            pool.memset(X0[:, :], 0.0).then_inc(m["const_ready"], 1)
            pool.memset(X1[:, :], 0.0).then_inc(m["const_ready"], 1)

        @block.tensor
        def _(pe):
            pe.wait_ge(m["loaded_const"], 16)
            pe.wait_ge(m["loaded_x"], 16 * NG)
            for n in range(NT):
                pe.transpose(PS[:, n // 4, (n % 4) * P:(n % 4 + 1) * P], xin[:, n, :], m["ident"][:, :])\
                  .then_inc(turned, 1)
            pe.wait_ge(m["const_ready"], 4)
            for g in range(NG):
                pe.wait_ge(xt_ready, g + 1)
                pe.matmul(PS[:, 4 + g, :], m["mean_w"][:, :], XT[:, g * GT:(g + 1) * GT], start=True, stop=True)\
                  .then_inc(mean_done, 1)
            for g in range(NG):
                pe.wait_ge(squared, g + 1)
                pe.matmul(PS[:, g, :], m["mean_w"][:, :], sqr[:, g * GT:(g + 1) * GT], start=True, stop=True)\
                  .then_inc(var_done, 1)

        @block.scalar
        def _(act):
            for g in range(NG):
                act.wait_ge(turned, 4 * g + 4)
                act.activation(XT[:, g * GT:(g + 1) * GT], PS[:, g, :], ACT.Copy).then_inc(xt_ready, 1)
            for g in range(NG):
                act.wait_ge(centred, g + 1)
                act.activation(sqr[:, g * GT:(g + 1) * GT], XN[:, g * GT:(g + 1) * GT], ACT.Square)\
                   .then_inc(squared, 1)
            act.wait_ge(var_done, NG)
            act.wait_ge(m["const_ready"], 4)
            act.activation(sqr[:, :], flat(PS[:, 0:4, :]), ACT.Ln, bias=m["eps_c"][:, 0:1]).then_inc(logged, 1)
            act.wait_ge(logged, 1)
            act.activation(sqr[:, :], sqr[:, :], ACT.Exp, scale=-0.5).then_inc(rstd_ready, 1)

        @block.vector
        def _(dve):
            dve.wait_ge(m["loaded_const"], 16)
            dve.tensor_copy(m["ident_bf"][:, :], m["ident"][:, :]).then_inc(m["ident_ready"], 1)
            for g in range(NG):
                dve.wait_ge(mean_done, g + 1)
                dve.tensor_tensor(XN[:, g * GT:(g + 1) * GT], XT[:, g * GT:(g + 1) * GT], PS[:, 4 + g, :],
                                  ALU.subtract).then_inc(centred, 1)
            dve.wait_ge(rstd_ready, 1)
            dve.wait_ge(m["const_ready"], 4)
            for g in range(NG):
                cols = slice(g * GT, (g + 1) * GT)
                dve.tensor_tensor(XN[:, cols], XN[:, cols], sqr[:, cols], ALU.mult).then_inc(xn_ready, 1)
                dve.wait_ge(xn_ready, g + 1)
                dve.tensor_copy(X0[0:64, PAD + g * GT:PAD + (g + 1) * GT], XN[0:64, cols]).then_inc(x0_set, 1)
                dve.tensor_copy(X0[64:128, PAD + 1 + g * GT:PAD + 1 + (g + 1) * GT], XN[64:128, cols])\
                   .then_inc(x0_set, 1)


def stage_mixed_attention(nc, a, m):
    PS, XT, XN = m["PS"], m["XT"], m["XN"]
    LH, E = 4, 8
    LW = LH * E
    GW = D - LW
    GH = GW // E
    BLK = 64
    PA = PS[:, 0, :]
    PB = PS[0:LW, 1, :]
    SCO = PS[:, 2:4, :].rearrange("p b n -> p (b n)").rearrange("p (h n) -> p h n", h=LH)
    PTB = PS[:, 4:6, :].rearrange("p b n -> p (b n)")
    QF = PS[0:GW, 6, 0:P]
    CT = PS[:, 6, P:2 * P]
    OG = PS[:, 6, 2 * P:2 * P + GW]
    OL = PS[:, 6, 2 * P + GW:2 * P + GW + LH * (E + 1)].rearrange("p (h e) -> p h e", h=LH)
    CX = PS[0:GW, 7, 0:GW + 1]

    with ExitStack() as ctx:
        def sb(name, shape, dt=F32):
            return ctx.enter_context(nc.sbuf_tensor(name, shape, dt))

        def sem(name):
            return ctx.enter_context(nc.semaphore(name))

        wq_z = sb("wq_z", [P, LH, LW])
        maskf = sb("a_maskf", [P, 2, 2 * P])
        mask = sb("a_mask", [P, 2, 2 * P], BF16)
        bmask = sb("a_bmask", [GW, GW])
        ones = sb("a_ones", [P, 1])
        xs = [sb(f"a_xs{i}", [P, P]) for i in range(2)]
        qk = [sb(f"a_qk{i}", [P, 2 * D]) for i in range(2)]
        kt = [sb(f"a_kt{i}", [LW, P]) for i in range(4)]
        qz = [sb(f"a_qz{i}", [LW, LH, P]) for i in range(2)]
        vx = [sb(f"a_vx{i}", [P, GW + 1]) for i in range(2)]
        vl = [sb(f"a_vl{i}", [P, LH, E + 1]) for i in range(4)]
        qm = [sb(f"a_qm{i}", [P, GH]) for i in range(2)]
        qd = [sb(f"a_qd{i}", [P, GW]) for i in range(2)]
        qe = [sb(f"a_qe{i}", [P, GW]) for i in range(2)]
        qs = [sb(f"a_qs{i}", [P, GH]) for i in range(2)]
        qi = [sb(f"a_qi{i}", [P, GH]) for i in range(2)]
        qf = [sb(f"a_qf{i}", [P, GW]) for i in range(2)]
        ke = [sb(f"a_ke{i}", [P, GW]) for i in range(2)]
        kp = [sb(f"a_kp{i}", [P, GW]) for i in range(2)]
        kf = [sb(f"a_kf{i}", [P, GW]) for i in range(2)]
        qft = [sb(f"a_qft{i}", [GW, P]) for i in range(2)]
        cx = sb("a_cx", [GW, GW + 1])
        cd = sb("a_cd", [GW, 1])
        cr = sb("a_cr", [GW, 1])
        cn = [sb(f"a_cn{i}", [GW, GW]) for i in range(2)]
        mx = sb("a_mx", [P, LH])
        sm = sb("a_sm", [P, LH, 2 * P])
        pr = [sb(f"a_pr{i}", [P, LH, 2 * P]) for i in range(2)]
        pt = sb("a_pt", [P, LH * 2 * P])
        oi = sb("a_oi", [P, LH])
        oc = [sb(f"a_oc{i}", [P, D]) for i in range(4)]
        oct_ = sb("a_oct", [P, P])

        loaded = sem("a_loaded")
        prepared = sem("a_prepared")
        zeroed = sem("a_zeroed")
        pe_sems = ("proj", "qft", "cx", "sc", "pt", "pv", "ct", "out")
        act_sems = ("qk", "kt", "qz", "vx", "vl", "ke", "qe", "qfe", "ex", "pte", "cte")
        dve_sems = ("qm", "qs", "qi", "kf", "cxa", "cda", "cra", "cn", "mx", "sm", "og", "oi", "ol", "xt")
        pool_sems = ("xs", "qd", "qf", "kp")
        sems = {f"{e}_{n}": sem(f"a_{e}_{n}") for e, ns in (
            ("pe", pe_sems), ("act", act_sems), ("dve", dve_sems), ("pool", pool_sems)) for n in ns}
        S = sems
        block = ctx.enter_context(nc.Block())
        TB = 4

        def n_(b, j):
            return b * TB + (CREDIT + j + 1)

        def n2(b, j, i):
            return b * (2 * TB) + (CREDIT + 2 * j + i + 1)

        def credit(eng, names):
            for n in names:
                eng.sem_inc(sems[n], CREDIT)

        def tiles(eng, slot):
            for k in range(TB):
                slot(0, k, lambda lag, k=k: k >= lag)
            with eng.Fori(1, NT // TB) as b:
                for k in range(TB):
                    slot(b, k, lambda lag: True)
            for k in range(3):
                slot(NT // TB, k, lambda lag, k=k: k < lag)

        @block.sync
        def _(sp):
            sp.dma_start(maskf[:, :, :], a["a_mask"]).then_inc(loaded, 16)
            sp.dma_start(bmask[:, :], a["a_bmask"]).then_inc(loaded, 16)

        @block.tensor
        def _(pe):
            def slot(b, k, on_):
                if on_(0):
                    pe.wait_ge(S["pool_xs"], n_(b, k))
                    pe.wait_ge(S["act_vl"], n_(b, k) - 1)
                    x = xs[k % 2][:, :]
                    pe.matmul(PA[:, 0:3 * D], x, m["a_w"][:, 0:3 * D], start=True, stop=True)
                    pe.matmul(PA[0:LW, 3 * D:4 * D], m["a_w"][:, D:D + LW], x, start=True, stop=True)
                    for h in range(LH):
                        last = pe.matmul(PB[:, h * P:(h + 1) * P], wq_z[:, h, :], x, start=True, stop=True)
                    last.then_inc(S["pe_proj"], 1)
                if on_(2):
                    j = k - 2
                    pe.wait_ge(S["act_ex"], n_(b, j))
                    pe.wait_ge(S["act_pte"], n_(b, j) - 1)
                    for h in range(LH):
                        for c in range(2):
                            last = pe.transpose(PTB[:, (2 * h + c) * P:(2 * h + c + 1) * P],
                                                pr[j % 2][:, h, c * P:(c + 1) * P], m["ident"][:, :])
                    last.then_inc(S["pe_pt"], 1)
                if on_(1) or on_(3):
                    if on_(2):
                        pe.wait_ge(S["dve_og"], n_(b, k - 2))
                    pe.wait_ge(S["dve_ol"], n_(b, k - 3))
                    pe.wait_ge(S["dve_xt"], n_(b, k - 4))
                if on_(1):
                    j = k - 1
                    pe.wait_ge(S["pool_qf"], n_(b, j))
                    pe.transpose(QF, qf[j % 2][:, :], m["ident"][:, :]).then_inc(S["pe_qft"], 1)
                if on_(3):
                    pe.transpose(CT, oc[(k - 3) % 4][:, :], m["ident"][:, :]).then_inc(S["pe_ct"], 1)

                def scores(hs):
                    j = k - 1
                    first = isinstance(b, int) and b == 0 and j == 0
                    for h in hs:
                        pe.matmul(SCO[:, h, :], m["ident_bf"][:, :], mask[:, 0 if first else 1, :],
                                  start=(h % 2 == 0), stop=False, skip_group_check=True)
                    for h in hs:
                        for c in range(2):
                            last = pe.matmul(SCO[:, h, c * P:(c + 1) * P], qz[j % 2][:, h, :],
                                             kt[(j - 1 + c) % 4][:, :], start=False, stop=True,
                                             skip_group_check=True)
                    return last

                def linear(i):
                    j = k - 1
                    rows = slice(BLK * i, BLK * i + BLK)
                    pe.wait_ge(S["dve_cn"], n2(b, j, i) - 1)
                    pe.matmul(OG[rows, :], qft[j % 2][:, rows], cn[i][:, :], start=True, stop=True)
                    pe.wait_ge(S["dve_kf"], n_(b, j))
                    pe.wait_ge(S["act_vx"], n_(b, j))
                    pe.matmul(CX, kf[j % 2][rows, :], vx[j % 2][rows, :], start=True, stop=True)\
                      .then_inc(S["pe_cx"], 1)

                if on_(1):
                    pe.wait_ge(S["act_kt"], n_(b, k - 1))
                    pe.wait_ge(S["act_qz"], n_(b, k - 1))
                    pe.wait_ge(S["dve_sm"], n_(b, k - 1) - 1)
                    scores((0, 1))
                    pe.wait_ge(S["act_qfe"], n_(b, k - 1))
                if on_(3):
                    pe.wait_ge(S["act_cte"], n_(b, k - 3))
                if on_(1):
                    linear(0)
                if on_(3):
                    pe.matmul(CT, m["a_w"][:, 3 * D:4 * D], oct_[:, :], start=True, stop=True).then_inc(S["pe_out"], 1)
                if on_(1):
                    scores((2, 3)).then_inc(S["pe_sc"], 1)
                if on_(2):
                    j = k - 2
                    pe.wait_ge(S["act_pte"], n_(b, j))
                    pe.wait_ge(S["act_vl"], n_(b, j))
                    for h in range(LH):
                        for c in range(2):
                            last = pe.matmul(OL[:, h, :], pt[:, (2 * h + c) * P:(2 * h + c + 1) * P],
                                             vl[(j - 1 + c) % 4][:, h, :], start=(c == 0), stop=(c == 1))
                    last.then_inc(S["pe_pv"], 1)
                if on_(1):
                    linear(1)

            credit(pe, ["pe_" + n for n in pe_sems])
            pe.wait_ge(prepared, 3)
            pe.wait_ge(zeroed, 2)
            pe.wait_ge(m["loaded_a"], 32)
            tiles(pe, slot)

        @block.scalar
        def _(act):
            def slot(b, k, on_):
                n = n_(b, k)
                i = k % 2
                if on_(0):
                    act.wait_ge(S["pe_proj"], n)
                    act.wait_ge(S["pool_qd"], n - 2)
                    act.wait_ge(S["pool_kp"], n - 2)
                    act.wait_ge(S["act_ke"], n - 2)
                    act.activation(qk[i][:, :], PA[:, 0:2 * D], ACT.Copy).then_inc(S["act_qk"], 1)
                    act.wait_ge(S["pe_sc"], n - 2)
                    act.activation(kt[k % 4][:, :], PA[0:LW, 3 * D:4 * D], ACT.Copy).then_inc(S["act_kt"], 1)
                    act.activation(qz[i][:, :, :].rearrange("p h n -> p (h n)"), PB, ACT.Copy)\
                       .then_inc(S["act_qz"], 1)
                    act.wait_ge(S["pe_cx"], n2(b, k - 2, 1))
                    act.activation(vx[i][:, 0:GW], PA[:, 2 * D + LW:3 * D], ACT.Copy).then_inc(S["act_vx"], 1)
                    act.wait_ge(S["pe_pv"], n - 3)
                    act.activation(vl[k % 4][:, :, 0:E],
                                   PA[:, 2 * D:2 * D + LW].rearrange("p (h e) -> p h e", h=LH), ACT.Copy)\
                       .then_inc(S["act_vl"], 1)
                if on_(3):
                    act.wait_ge(S["pe_ct"], n_(b, k - 3))
                if on_(1):
                    j = k - 1
                    act.wait_ge(S["pe_qft"], n_(b, j))
                    act.wait_ge(S["pe_cx"], n2(b, j - 2, 1))
                    act.activation(qft[j % 2][:, :], QF, ACT.Copy).then_inc(S["act_qfe"], 1)
                if on_(3):
                    act.wait_ge(S["pe_out"], n_(b, k - 3) - 1)
                    act.activation(oct_[:, :], CT, ACT.Copy).then_inc(S["act_cte"], 1)
                if on_(2):
                    j = k - 2
                    act.wait_ge(S["pe_pt"], n_(b, j))
                    act.wait_ge(S["pe_pv"], n_(b, j) - 1)
                    act.activation(pt[:, :], PTB, ACT.Copy).then_inc(S["act_pte"], 1)
                if on_(0):
                    act.wait_ge(S["act_qk"], n)
                    act.wait_ge(S["dve_kf"], n - 2)
                    act.activation(ke[i][:, :], qk[i][:, D + LW:2 * D], ACT.Exp).then_inc(S["act_ke"], 1)
                    act.wait_ge(S["pool_qd"], n)
                    act.wait_ge(S["pool_qf"], n - 2)
                    act.activation(qe[i][:, :], qd[i][:, :], ACT.Exp).then_inc(S["act_qe"], 1)
                if on_(1):
                    j = k - 1
                    act.wait_ge(S["dve_sm"], n_(b, j))
                    act.wait_ge(S["pe_pt"], n_(b, j) - 2)
                    act.activation(pr[j % 2][:, :, :], sm[:, :, :], ACT.Exp, scale=float(E) ** -0.5)\
                       .then_inc(S["act_ex"], 1)

            credit(act, ["act_" + n for n in act_sems])
            act.wait_ge(zeroed, 2)
            tiles(act, slot)

        @block.vector
        def _(dve):
            def heads(x, n=GH):
                return x.rearrange("p (h e) -> p h e", h=n)

            def slot(b, k, on_):
                if on_(0):
                    n = n_(b, k)
                    i = k % 2
                    dve.wait_ge(S["act_qk"], n)
                    dve.wait_ge(S["pool_qd"], n - 2)
                    dve.tensor_reduce(qm[i][:, :], heads(qk[i][:, LW:D]), AX.X, ALU.max).then_inc(S["dve_qm"], 1)
                def context(j, i):
                    nb = n2(b, j, i)
                    dve.wait_ge(S["pe_cx"], nb)
                    dve.wait_ge(S["dve_cn"], nb - 1)
                    dve.tensor_tensor(cx[:, :], CX, cx[:, :], ALU.add).then_inc(S["dve_cxa"], 1)
                    dve.wait_ge(S["dve_cxa"], nb)
                    dve.tensor_scalar(cd[:, :], cx[:, GW:GW + 1], 1e-6, None, ALU.add).then_inc(S["dve_cda"], 1)
                    dve.wait_ge(S["dve_cda"], nb)
                    dve.reciprocal(cr[:, :], cd[:, :]).then_inc(S["dve_cra"], 1)
                    dve.wait_ge(S["dve_cra"], nb)
                    dve.scalar_tensor_tensor(out=cn[(i + 1) % 2][:, :], in0=cx[:, 0:GW], scalar=cr[:, 0:1],
                                             in1=bmask[:, :], op0=ALU.mult, op1=ALU.mult).then_inc(S["dve_cn"], 1)

                if on_(1):
                    j = k - 1
                    context(j, 0)
                    n = n_(b, j)
                    dve.wait_ge(S["pe_sc"], n)
                    dve.tensor_reduce(mx[:, :], SCO, AX.X, ALU.max).then_inc(S["dve_mx"], 1)
                    dve.wait_ge(S["dve_mx"], n)
                    dve.wait_ge(S["act_ex"], n - 1)
                    dve.tensor_tensor(sm[:, :, :], SCO, mx[:, :].unsqueeze(2).to_broadcast([P, LH, 2 * P]),
                                      ALU.subtract).then_inc(S["dve_sm"], 1)
                if on_(0):
                    n = n_(b, k)
                    i = k % 2
                    dve.wait_ge(S["act_qe"], n)
                    dve.tensor_reduce(qs[i][:, :], heads(qe[i][:, :]), AX.X, ALU.add).then_inc(S["dve_qs"], 1)
                    dve.wait_ge(S["dve_qs"], n)
                    dve.wait_ge(S["pool_qf"], n - 2)
                    dve.reciprocal(qi[i][:, :], qs[i][:, :]).then_inc(S["dve_qi"], 1)
                    dve.wait_ge(S["act_ke"], n)
                    dve.wait_ge(S["pool_kp"], n)
                    dve.wait_ge(S["pe_cx"], n2(b, k - 2, 1))
                    dve.scalar_tensor_tensor(out=kf[i][:, :], in0=ke[i][:, :], scalar=1.0, in1=kp[i][:, :],
                                             op0=ALU.min, op1=ALU.add).then_inc(S["dve_kf"], 1)
                if on_(3):
                    dve.wait_ge(S["pe_out"], n_(b, k - 3))
                if on_(2):
                    dve.wait_ge(S["pe_pv"], n_(b, k - 2))
                if on_(1):
                    j = k - 1
                    dve.wait_ge(S["pe_cx"], n2(b, j, 1))
                    dve.wait_ge(S["pe_ct"], n_(b, j) - 4)
                    dve.tensor_copy(oc[j % 4][:, LW:D], OG).then_inc(S["dve_og"], 1)
                if on_(2):
                    j = k - 2
                    n = n_(b, j)
                    dve.reciprocal(oi[:, :], OL[:, :, E]).then_inc(S["dve_oi"], 1)
                    dve.wait_ge(S["dve_oi"], n)
                    dve.tensor_tensor(heads(oc[j % 4][:, 0:LW], LH), OL[:, :, 0:E],
                                      oi[:, :].unsqueeze(2).to_broadcast([P, LH, E]), ALU.mult)\
                       .then_inc(S["dve_ol"], 1)
                if on_(3):
                    j = k - 3
                    cols = bass.ds(b * (TB * P) + j * P, P)
                    dve.scalar_tensor_tensor(out=XT[:, cols], in0=CT, scalar=m["a_bo"][:, 0:1], in1=XT[:, cols],
                                             op0=ALU.add, op1=ALU.add).then_inc(S["dve_xt"], 1)
                if on_(1):
                    context(k - 1, 1)

            credit(dve, ["dve_" + n for n in dve_sems])
            dve.wait_ge(loaded, 32)
            dve.wait_ge(m["loaded_a"], 32)
            dve.tensor_copy(mask[:, :, :], maskf[:, :, :]).then_inc(prepared, 1)
            dve.memset(cx[:, :], 0.0).then_inc(prepared, 1)
            dve.memset(cn[0][:, :], 0.0).then_inc(prepared, 1)
            dve.wait_ge(prepared, 3)
            dve.wait_ge(zeroed, 2)
            tiles(dve, slot)

        @block.gpsimd
        def _(pool):
            def heads(x):
                return x.rearrange("p (h e) -> p h e", h=GH)

            def slot(b, k, on_):
                n = n_(b, k)
                i = k % 2
                if on_(0):
                    pool.wait_ge(S["pe_proj"], n - 2)
                    pool.tensor_tensor(xs[i][:, :], XN[:, bass.ds(b * (TB * P) + k * P, P)],
                                       ones[:, 0:1].to_broadcast([P, P]), ALU.mult).then_inc(S["pool_xs"], 1)
                if on_(1):
                    j = k - 1
                    pool.wait_ge(S["dve_qi"], n - 1)
                    pool.wait_ge(S["act_qe"], n - 1)
                    pool.wait_ge(S["pe_qft"], n - 3)
                    pool.tensor_tensor(heads(qf[j % 2][:, :]), heads(qe[j % 2][:, :]),
                                       qi[j % 2][:, :].unsqueeze(2).to_broadcast([P, GH, E]), ALU.mult)\
                        .then_inc(S["pool_qf"], 1)
                if on_(0):
                    pool.wait_ge(S["act_qk"], n)
                    pool.wait_ge(S["dve_qm"], n)
                    pool.wait_ge(S["act_qe"], n - 2)
                    pool.wait_ge(S["dve_kf"], n - 2)
                    pool.tensor_tensor(heads(qd[i][:, :]), heads(qk[i][:, LW:D]),
                                       qm[i][:, :].unsqueeze(2).to_broadcast([P, GH, E]), ALU.subtract)\
                        .then_inc(S["pool_qd"], 1)
                    pool.tensor_scalar(kp[i][:, :], qk[i][:, D + LW:2 * D], 0.0, None, ALU.max)\
                        .then_inc(S["pool_kp"], 1)

            credit(pool, ["pool_" + n for n in pool_sems])
            pool.memset(ones[:, :], 1.0)
            pool.memset(wq_z[:, :, :], 0.0)
            pool.memset(kt[3][:, :], 0.0)
            for v in vx:
                pool.memset(v[:, :], 1.0)
            for v in vl:
                last = pool.memset(v[:, :, :], 1.0)
            last.then_inc(zeroed, 1)
            pool.wait_ge(zeroed, 1)
            pool.wait_ge(m["loaded_a"], 32)
            for h in range(LH):
                last = pool.tensor_copy(wq_z[:, h, h * E:(h + 1) * E], m["a_w"][:, h * E:(h + 1) * E])
            last.then_inc(zeroed, 1)
            pool.wait_ge(zeroed, 2)
            tiles(pool, slot)


def stage_layers(nc, a, m):
    PS, X0, X1 = m["PS"], m["X0"], m["X1"]
    wqkv, wo, w1, w2, par, qks, xpos, rot, kshift, maskf = (
        m[n] for n in ("wqkv", "wo", "w1", "w2", "par", "qks", "xpos", "rot", "kshift", "maskf"))
    loaded_tab, loaded_qkv, loaded_wo, loaded_mlp = (
        m[n] for n in ("loaded_tab", "loaded_qkv", "loaded_wo", "loaded_mlp"))
    QK = [PS[:, 0, :], PS[:, 1, :]]
    VB = PS[:, 2, :]
    TR = PS[:, 3, :]
    PO = PS[:, 4, :]
    SO = PS[:, 5:7, :]
    SC, OC, OE = 0, 2 * 2 * WIN, DH + 1
    AC = PS[:, 7, 0:P]
    LN = BANK - P
    MU, VA, RB = PS[:, 5, LN:BANK], PS[:, 6, LN:LN + 1], PS[:, 5, LN:BANK]
    MU_E, VA_E, RB_E = PS[:, 7, LN:BANK], PS[:, 7, LN:LN + 1], PS[:, 7, LN:BANK]

    with ExitStack() as ctx:
        def sb(name, shape, dt=F32):
            return ctx.enter_context(nc.sbuf_tensor(name, shape, dt))

        def sem(name):
            return ctx.enter_context(nc.semaphore(name))

        mask = sb("mask", [P, 2, P], BF16)
        half_c = sb("half_c", [P, 8])
        ones = sb("ones", [P, 1])
        xs = [sb(f"xs{i}", [P, WIN + P]) for i in range(2)]
        lay4 = sb("lay4", [P, 4 * DH])
        tab = [sb(f"tab{i}", [P, 4, DH]) for i in range(2)]
        sq = [sb(f"sq{i}", [P, BANK]) for i in range(2)]
        ss = [sb(f"ss{i}", [P, 8]) for i in range(2)]
        sg = [sb(f"sg{i}", [P, 8]) for i in range(2)]
        rn = [sb(f"rn{i}", [P, 8]) for i in range(2)]
        qn = [sb(f"qn{i}", [P, BANK]) for i in range(2)]
        cm = [sb(f"cm{i}", [P, BANK]) for i in range(2)]
        rs = [sb(f"rs{i}", [P, BANK]) for i in range(2)]
        qr = [sb(f"qr{i}", [P, BANK]) for i in range(2)]
        qkt = [sb(f"qkt{i}", [P, 4, WIN + P]) for i in range(UT)]
        vs = [sb(f"vs{i}", [P, 4, 2, DH + 1]) for i in range(4)]
        mx = [sb(f"mx{i}", [P, 2, 2]) for i in range(2)]
        sm = [sb(f"sm{i}", [P, 2, 2, DH]) for i in range(2)]
        pr = [sb(f"pr{i}", [P, 2, P]) for i in range(2)]
        po = [sb(f"po{i}", [P, BANK]) for i in range(2)]
        ri = [sb(f"ri{i}", [P, 2, 2]) for i in range(2)]
        on = [sb(f"on{i}", [P, 2, 2, DH]) for i in range(2)]
        xc = sb("xc", [P, T])
        sqt = sb("sqt", [P, P])
        ve = sb("ve", [P, 1])
        rl = sb("rl", [P, 1])
        gl = [sb(f"gl{i}", [P, GT]) for i in range(2)]
        hb = [[sb(f"hb{i}_{c}", [P, GT]) for c in range(len(FCH))] for i in range(2)]

        ready = sem("ready")
        unit_sems = {n: sem("u_" + n) for n in (
            "qk_done", "v_done", "tr_done", "pv_done", "s_done", "wo_done", "po_done",
            "sq_ready", "v_ready", "qkt_ready", "po_ready", "p_ready",
            "ss_ready", "qn_ready", "cm_ready", "qr_ready", "ri_ready", "on_ready", "mx_ready", "sm_ready",
            "kp_ready", "sg_ready", "rn_ready", "rs_ready")}
        S = unit_sems
        x_staged, tab_ready, lay_ready, x1_ready = (sem(n) for n in ("x_staged", "tab_ready", "lay_ready", "x1_ready"))
        mean_done, centred, squared, var_done, var_ready, rstd_ready, spread, scaled, xn_ready = (
            sem(n) for n in ("f_mean_done", "f_centred", "f_squared", "f_var_done", "f_var_ready", "f_rstd_ready",
                             "f_spread", "f_scaled", "f_xn_ready"))
        ha_done, hg_done, gl_ready, h_ready, mo_done, x0_ready = (
            sem(n) for n in ("ha_done", "hg_done", "gl_ready", "h_ready", "mo_done", "x0_ready"))
        block = ctx.enter_context(nc.Block())

        def n_unit(l, b, j):
            return l * UNITS + b * BODY + (CREDIT + j + 1)

        def n_po(l, b, k):
            return l * (UNITS + 1) + b * BODY + (CREDIT + k - 3 + 1)

        def n_tile(l, b, t):
            return l * (NT + 1) + b * 2 + (t + 1)

        def n_x1(l, b, t):
            return l * (2 * NT) + b * 4 + 2 * (t + 1)

        def n_ln(l, b, k):
            return l * NT + b * 2 + (CREDIT + k // UT - 1)

        def layer_slots(eng, slot, l, after=None):
            for b in range(2):
                for k in range(BODY):
                    slot(l, b, k, lambda lag, s=b * BODY + k: s >= lag)
            with eng.Fori(2, UNITS // BODY) as b:
                for k in range(BODY):
                    slot(l, b, k, lambda lag: True)
            for k in range(LAG):
                slot(l, UNITS // BODY, k, lambda lag, k=k: k < lag)
                if after is not None:
                    after(k)

        @block.sync
        def _(sp):
            def load_qkv(l):
                sp.dma_start(wqkv[:, :], a["L0_ffn_Wqkv"][bass.ds(l, 1), :, :].rearrange("o p n -> p (o n)"))\
                  .then_inc(loaded_qkv, 16)

            def load_wo(l):
                sp.dma_start(flat(wo[:, :, :]), a["l_wo"][bass.ds(l, 1), :, :].rearrange("o p n -> p (o n)"))\
                  .then_inc(loaded_wo, 16)

            def load_mlp(l):
                sp.dma_start(w1[:, :], a["L0_ffn_W1"][bass.ds(l, 1), :, :].rearrange("o p n -> p (o n)"))\
                  .then_inc(loaded_mlp, 16)
                sp.dma_start(flat(w2[:, :, :]), a["l_w2"][bass.ds(l, 1), :, :].rearrange("o p n -> p (o n)"))\
                  .then_inc(loaded_mlp, 16)
                sp.dma_start(par[:, :], a["l_par"][bass.ds(l, 1), :, :].rearrange("o p n -> p (o n)"))\
                  .then_inc(loaded_mlp, 16)

            with sp.Fori(0, DEPTH - 1) as l:
                sp.wait_ge(S["v_done"], n_unit(l, 0, UNITS - 1))
                load_qkv(l + 1)
                sp.wait_ge(S["wo_done"], n_unit(l, 0, UNITS - 1))
                load_wo(l + 1)
                sp.wait_ge(x0_ready, l * (2 * NG) + 2 * NG + CREDIT)
                load_mlp(l + 1)

        @block.tensor
        def _(pe):
            def mean(out_, cols):
                pe.matmul(out_, m["mean_w"][:, :], X1[:, cols], start=True, stop=True).then_inc(mean_done, 1)

            def variance(out_):
                pe.matmul(out_, sqt[:, :], m["mean_w"][:, 0:1], start=True, stop=True).then_inc(var_done, 1)

            def spread_out(out_):
                pe.matmul(out_, rl[:, 0:1].to_broadcast([P, P]), m["ident"][:, :], start=True, stop=True)\
                  .then_inc(spread, 1)

            def slot(l, b, k, on_):
                if on_(0):
                    g, par_ = k % UT, (k // UT) % 2
                    if g == 0:
                        pe.wait_ge(x_staged, n_tile(l, b, k // UT))
                    pe.wait_ge(S["qn_ready"], n_unit(l, b, k) - 2)
                    w = wqkv[:, 0:2 * INNER].rearrange("p (s n) -> p s n", s=2)[:, :, g * 256:(g + 1) * 256]
                    pe.matmul(QK[k % 2], xs[par_][:, WIN:WIN + P], w, start=True, stop=True).then_inc(S["qk_done"], 1)
                if on_(5):
                    j = k - 5
                    g = j % UT
                    if g == 0:
                        pe.wait_ge(x1_ready, n_x1(l, b, j // UT) - 2 + CREDIT)
                    pe.wait_ge(S["po_ready"], n_po(l, b, k) - 1)
                    for p in range(2):
                        last = pe.matmul(AC, wo[:, 2 * g + p, :], po[(k - 1) % 2][:, (2 + p) * P:(3 + p) * P],
                                         start=(g == 0 and p == 0), stop=(g == UT - 1 and p == 1))
                    last.then_inc(S["wo_done"], 1)
                def values(windows):
                    g, par_ = k % UT, (k // UT) % 2
                    wv = wqkv[:, 2 * INNER + g * 256:2 * INNER + (g + 1) * 256].rearrange(
                        "p (r h e) -> p h r e", r=2, h=2)
                    for w in windows:
                        for h in range(2):
                            last = pe.matmul(VB[64 * h:64 * h + 64, w * P:(w + 1) * P],
                                             xs[par_][:, WIN * w:WIN * w + 2 * WIN], wv[:, h, :, :],
                                             start=True, stop=True)
                    return last

                if on_(0):
                    pe.wait_ge(S["v_ready"], n_unit(l, b, k) - 1)
                    values((0,))
                if on_(3) or on_(4):
                    pe.wait_ge(S["po_ready"], n_po(l, b, k) - 1)
                    last = None
                    if on_(3):
                        j = k - 3
                        pe.wait_ge(S["p_ready"], n_unit(l, b, j))
                        for p in range(2):
                            last = pe.transpose(PO[:, p * P:(p + 1) * P], pr[j % 2][:, p, :], m["ident"][:, :])
                    if on_(4):
                        j = k - 4
                        pe.wait_ge(S["on_ready"], n_unit(l, b, j))
                        for p in range(2):
                            last = pe.transpose(PO[:, (2 + p) * P:(3 + p) * P],
                                                on[j % 2][:, p, :, :].rearrange("p a b -> p (a b)"), m["ident"][:, :])
                    last.then_inc(S["po_done"], 1)
                if on_(0):
                    values((1,))
                if on_(2):
                    j = k - 2
                    pe.wait_ge(S["qr_ready"], n_unit(l, b, j))
                    pe.wait_ge(S["qkt_ready"], n_unit(l, b, j) - 1)
                    for p in range(4):
                        last = pe.transpose(TR[:, p * P:(p + 1) * P], qr[j % 2][:, p * P:(p + 1) * P], m["ident"][:, :])
                    last.then_inc(S["tr_done"], 1)
                if on_(0):
                    values((2,))
                if on_(4):
                    pe.wait_ge(S["on_ready"], n_unit(l, b, k - 4))
                if on_(3):
                    pe.wait_ge(S["sm_ready"], n_unit(l, b, k - 3))
                    pe.wait_ge(S["v_ready"], n_unit(l, b, k - 3))
                    pe.wait_ge(S["po_ready"], n_po(l, b, k))
                first_tile = isinstance(b, int) and b == 0 and k - 2 < UT

                def open_with_mask():
                    for h in range(2):
                        pe.matmul(SO[:, h, SC:SC + P], m["ident_bf"][:, :], mask[:, 0 if first_tile else 1, :],
                                  start=True, stop=False, skip_group_check=True)

                if on_(0):
                    values((3,)).then_inc(S["v_done"], 1)
                elif on_(3):
                    open_with_mask()
                if k % UT == 1 and on_(6):
                    pe.wait_ge(x1_ready, n_x1(l, b, k // UT - 2) + CREDIT)
                    mean(MU, bass.ds(b * (2 * P) + (k // UT - 2) * P + PAD, P))
                if k % UT == 2 and on_(7):
                    pe.wait_ge(squared, n_ln(l, b, k))
                    variance(VA)
                if k % UT == 3 and on_(8):
                    pe.wait_ge(rstd_ready, n_ln(l, b, k))
                    spread_out(RB)
                if on_(3):
                    j = k - 3
                    for p in range(2):
                        for w in range(4):
                            for h in range(2):
                                rows = slice(64 * h, 64 * h + 64)
                                last = pe.matmul(SO[WIN * w:WIN * w + WIN, h, OC + p * OE:OC + (p + 1) * OE],
                                                 po[k % 2][rows, p * P + WIN * w:p * P + WIN * w + WIN],
                                                 vs[j % 4][rows, w, p, :], start=True, stop=True,
                                                 skip_group_check=True)
                    last.then_inc(S["pv_done"], 1)
                if on_(2):
                    pe.wait_ge(S["qkt_ready"], n_unit(l, b, k - 2))
                    pe.wait_ge(S["kp_ready"], n_unit(l, b, k - 2))
                    open_with_mask()
                if on_(2):
                    j = k - 2
                    g = j % UT
                    for p in range(2):
                        for w in range(4):
                            for h in range(2):
                                rows = slice(64 * h, 64 * h + 64)
                                last = pe.matmul(SO[WIN * w:WIN * w + WIN, h, SC + p * 64:SC + (p + 1) * 64],
                                                 qkt[g][rows, p, WIN + WIN * w:2 * WIN + WIN * w],
                                                 qkt[g][rows, 2 + p, WIN * w:WIN * w + 2 * WIN],
                                                 start=False, stop=True, skip_group_check=True)
                    last.then_inc(S["s_done"], 1)

            def hidden(l, g, c):
                o, n = FCH[c]
                if c == 0:
                    pe.wait_ge(xn_ready, l * NT + (4 * g + 4 + CREDIT))
                if g > 0:
                    pe.wait_ge(h_ready, l * (NG * 3) + (g - 1) * 3 + c + 1)
                x = xc[:, g * GT:(g + 1) * GT]
                pe.matmul(PS[0:n, 2 * c + 1, :], w1[:, FF + o:FF + o + n], x, start=True, stop=True)\
                  .then_inc(hg_done, 1)
                pe.matmul(PS[0:n, 2 * c, :], w1[:, o:o + n], x, start=True, stop=True).then_inc(ha_done, 1)

            def outp(l, g):
                pe.wait_ge(h_ready, l * (NG * 3) + g * 3 + 3)
                if g == 1:
                    pe.wait_ge(scaled, l * NT + (NT + CREDIT))
                if g >= 2:
                    pe.wait_ge(x0_ready, l * (2 * NG) + 2 * (g - 1) + CREDIT)
                for c, (o, n) in enumerate(FCH):
                    last = pe.matmul(PS[:, 6 + g % 2, :], w2[0:n, c, :], hb[g % 2][c][0:n, :],
                                     start=(c == 0), stop=(c == len(FCH) - 1))
                last.then_inc(mo_done, 1)

            def early(l, k):
                if k == 2:
                    pe.wait_ge(loaded_mlp, l * 48 + 48)
                    pe.wait_ge(S["sq_ready"], n_unit(l, 0, UNITS - 1))
                    pe.wait_ge(S["qn_ready"], n_unit(l, 0, UNITS - 1))
                    hidden(l, 0, 0)
                if k == 3:
                    pe.wait_ge(S["v_ready"], n_unit(l, 0, UNITS - 1))
                    pe.wait_ge(S["qkt_ready"], n_unit(l, 0, UNITS - 1))
                    hidden(l, 0, 1)

            def mlp(l):
                pe.wait_ge(x1_ready, n_x1(l, 0, NT - 1) + CREDIT)
                mean(MU_E, slice(PAD + (NT - 1) * P, PAD + NT * P))
                pe.wait_ge(S["po_ready"], n_po(l, 0, UNITS + 3))
                pe.wait_ge(scaled, l * NT + (NT - 1 + CREDIT))
                hidden(l, 0, 2)
                pe.wait_ge(squared, l * NT + (NT + CREDIT))
                variance(VA_E)
                hidden(l, 1, 0)
                pe.wait_ge(rstd_ready, l * NT + (NT + CREDIT))
                spread_out(RB_E)
                outp(l, 0)
                for g in range(1, NG):
                    for c in range(len(FCH)):
                        if (g, c) != (1, 0):
                            hidden(l, g, c)
                        if c == 0 and g > 1:
                            outp(l, g - 1)
                outp(l, NG - 1)

            for s in (S["qk_done"], S["v_done"], S["tr_done"], S["pv_done"], S["s_done"], S["wo_done"], S["po_done"],
                      mean_done, var_done, spread):
                pe.sem_inc(s, CREDIT)
            pe.wait_ge(ready, 3)
            with pe.Fori(0, DEPTH) as l:
                pe.wait_ge(loaded_qkv, l * 16 + 16)
                pe.wait_ge(loaded_wo, l * 16 + 16)
                layer_slots(pe, slot, l, lambda k: early(l, k))
                mlp(l)

        @block.scalar
        def _(act):
            def squares(n, cols):
                act.wait_ge(centred, n)
                act.wait_ge(var_done, n - 1)
                act.activation(sqt[:, :], xc[:, cols], ACT.Square).then_inc(squared, 1)

            def slot(l, b, k, on_):
                if on_(3):
                    j = k - 3
                    act.wait_ge(S["sm_ready"], n_unit(l, b, j))
                    act.wait_ge(S["po_done"], n_po(l, b, k) - 2)
                    act.activation(pr[j % 2][:, :, :].rearrange("p a b -> p (a b)"),
                                   sm[j % 2][:, :, :, :].rearrange("p a b c -> p (a b c)"), ACT.Exp)\
                       .then_inc(S["p_ready"], 1)
                if k % UT == 2 and on_(7):
                    squares(n_ln(l, b, k), bass.ds(b * (2 * P) + (k // UT - 2) * P, P))
                if on_(0):
                    act.wait_ge(S["qk_done"], n_unit(l, b, k))
                    act.wait_ge(S["ss_ready"], n_unit(l, b, k) - 2)
                    act.activation(sq[k % 2][:, :], QK[k % 2], ACT.Square).then_inc(S["sq_ready"], 1)
                if on_(3) or on_(4):
                    act.wait_ge(S["po_done"], n_po(l, b, k))
                    lo, hi = (0 if on_(3) else 2 * P), (4 * P if on_(4) else 2 * P)
                    if on_(3):
                        act.wait_ge(S["pv_done"], n_unit(l, b, k - 3) - 2)
                    if on_(4):
                        act.wait_ge(S["wo_done"], n_unit(l, b, k - 4) - 2)
                    act.activation(po[k % 2][:, lo:hi], PO[:, lo:hi], ACT.Copy).then_inc(S["po_ready"], 1)
                if on_(2):
                    j = k - 2
                    act.wait_ge(S["tr_done"], n_unit(l, b, j))
                    act.wait_ge(S["kp_ready"], n_unit(l, b, j))
                    act.activation(qkt[j % UT][:, :, WIN:WIN + P], TR.rearrange("p (a b) -> p a b", a=4), ACT.Copy)\
                       .then_inc(S["qkt_ready"], 1)
                if on_(0):
                    act.wait_ge(S["v_done"], n_unit(l, b, k))
                    act.wait_ge(S["pv_done"], n_unit(l, b, k) - 4)
                    act.activation(vs[k % 4][:, :, :, 0:DH], VB.rearrange("p (w r e) -> p w r e", w=4, r=2),
                                   ACT.Copy).then_inc(S["v_ready"], 1)

            def mlp(l):
                for g in range(NG):
                    for c, (o, n) in enumerate(FCH):
                        i = 3 * g + c
                        act.wait_ge(hg_done, l * (NG * 3) + (i + 1))
                        act.wait_ge(h_ready, l * (NG * 3) + (i + 1 - 2)) if i >= 2 else None
                        act.activation(gl[i % 2][0:n, :], PS[0:n, 2 * c + 1, :], ACT.Gelu,
                                       bias=par[0:n, 3 + 3 + c:3 + 3 + c + 1]).then_inc(gl_ready, 1)
                        if i == 0:
                            squares(l * NT + (NT + CREDIT), slice((NT - 1) * P, NT * P))

            for s in (S["sq_ready"], S["v_ready"], S["qkt_ready"], S["po_ready"], S["p_ready"], squared):
                act.sem_inc(s, CREDIT)
            act.wait_ge(ready, 3)
            with act.Fori(0, DEPTH) as l:
                layer_slots(act, slot, l)
                act.wait_ge(loaded_mlp, l * 48 + 48)
                mlp(l)

        @block.vector
        def _(dve):
            for s in (S["ss_ready"], S["sg_ready"], S["qn_ready"], S["cm_ready"], S["qr_ready"], S["ri_ready"], S["on_ready"],
                      S["mx_ready"], S["sm_ready"], x1_ready, x0_ready, centred, var_ready, scaled, xn_ready):
                dve.sem_inc(s, CREDIT)
            dve.wait_ge(loaded_tab, 80)
            dve.memset(half_c[:, :], -0.5).then_inc(ready, 1)
            dve.memset(ones[:, :], 1.0).then_inc(ready, 1)
            dve.tensor_copy(mask[:, :, :], maskf[:, :, :]).then_inc(ready, 1)

            def heads(x):
                return x.rearrange("p (h e) -> p h e", e=DH)

            def centre(mu, n, c0):
                dve.wait_ge(mean_done, n)
                static = isinstance(c0, int)
                dve.tensor_tensor(xc[:, slice(c0, c0 + P) if static else bass.ds(c0, P)],
                                  X1[:, slice(PAD + c0, PAD + c0 + P) if static else bass.ds(c0 + PAD, P)],
                                  mu, ALU.subtract).then_inc(centred, 1)

            def variance(va, n):
                dve.wait_ge(var_done, n)
                dve.wait_ge(rstd_ready, n - 1)
                dve.tensor_scalar(ve[:, :], va, LN_EPS, None, ALU.add).then_inc(var_ready, 1)

            def scale(rb, n, cols):
                dve.wait_ge(spread, n)
                dve.wait_ge(squared, n)
                dve.tensor_tensor(xc[:, cols], xc[:, cols], rb, ALU.mult).then_inc(scaled, 1)

            def affine(l, n, cols):
                dve.wait_ge(loaded_mlp, l * 48 + 48)
                dve.wait_ge(scaled, n)
                dve.tensor_scalar(xc[:, cols], xc[:, cols], par[:, 0:1], par[:, 1:2], ALU.mult, ALU.add)\
                   .then_inc(xn_ready, 1)

            def slot(l, b, k, on_):
                sc = SO[:, :, SC:SC + P].rearrange("p h (r e) -> p h r e", r=2)
                o = SO[:, :, OC:OC + 2 * OE].rearrange("p h (r e) -> p h r e", e=OE)
                if on_(3):
                    j = k - 3
                    dve.wait_ge(S["s_done"], n_unit(l, b, j))
                    dve.tensor_reduce(mx[j % 2][:, :, :], sc, AX.X, ALU.max).then_inc(S["mx_ready"], 1)
                if on_(4):
                    j = k - 4
                    dve.wait_ge(S["pv_done"], n_unit(l, b, j))
                    dve.reciprocal(ri[j % 2][:, :, :], o[:, :, :, DH]).then_inc(S["ri_ready"], 1)
                if on_(3):
                    j = k - 3
                    dve.wait_ge(S["mx_ready"], n_unit(l, b, j))
                    dve.wait_ge(S["p_ready"], n_unit(l, b, j) - 2)
                    dve.tensor_tensor(sm[j % 2][:, :, :, :].rearrange("p r h e -> p h r e"), sc,
                                      mx[j % 2][:, :, :].unsqueeze(3).to_broadcast([P, 2, 2, DH]), ALU.subtract)\
                       .then_inc(S["sm_ready"], 1)
                if k % UT == 2 and on_(7):
                    centre(MU, n_ln(l, b, k), b * (2 * P) + (k // UT - 2) * P)
                if k % UT == 3 and on_(8):
                    variance(VA, n_ln(l, b, k))
                if k % UT == 0 and on_(9):
                    scale(RB, n_ln(l, b, k) - 1, bass.ds(b * (2 * P) + (k // UT - 3) * P, P))
                if on_(4):
                    j = k - 4
                    dve.wait_ge(S["ri_ready"], n_unit(l, b, j))
                    dve.wait_ge(S["po_done"], n_po(l, b, k) - 2)
                    dve.tensor_tensor(on[j % 2][:, :, :, :].rearrange("p r h e -> p h r e"), o[:, :, :, 0:DH],
                                      ri[j % 2][:, :, :].unsqueeze(3).to_broadcast([P, 2, 2, DH]), ALU.mult)\
                       .then_inc(S["on_ready"], 1)
                if on_(2):
                    j = k - 2
                    n = n_unit(l, b, j)
                    dve.wait_ge(S["rs_ready"], n)
                    dve.wait_ge(S["cm_ready"], n)
                    dve.wait_ge(S["tr_done"], n - 2)
                    dve.tensor_tensor(qr[j % 2][:, :], cm[j % 2][:, :], rs[j % 2][:, :], ALU.add)\
                       .then_inc(S["qr_ready"], 1)
                if on_(1):
                    j = k - 1
                    n = n_unit(l, b, j)
                    i = j % 2
                    dve.wait_ge(S["rn_ready"], n)
                    dve.wait_ge(S["rs_ready"], n - 2)
                    dve.tensor_tensor(heads(qn[i][:, :]), heads(QK[i]),
                                      rn[i][:, :].unsqueeze(2).to_broadcast([P, 8, DH]), ALU.mult)\
                       .then_inc(S["qn_ready"], 1)
                    dve.wait_ge(S["qn_ready"], n)
                    if j % UT == 0:
                        dve.wait_ge(tab_ready, n_tile(l, b, j // UT))
                    for s in range(2):
                        last = dve.tensor_tensor(
                            heads(cm[i][:, 256 * s:256 * s + 256]), heads(qn[i][:, 256 * s:256 * s + 256]),
                            tab[(j // UT) % 2][:, 2 * s, :].unsqueeze(1).to_broadcast([P, 4, DH]), ALU.mult)
                    last.then_inc(S["cm_ready"], 1)
                if on_(0):
                    n = n_unit(l, b, k)
                    dve.wait_ge(S["sq_ready"], n)
                    dve.tensor_reduce(ss[k % 2][:, :], heads(sq[k % 2][:, :]), AX.X, ALU.add)\
                       .then_inc(S["ss_ready"], 1)
                    dve.wait_ge(S["ss_ready"], n)
                    dve.wait_ge(S["rn_ready"], n - 2)
                    dve.tensor_scalar(sg[k % 2][:, :], ss[k % 2][:, :], 1e-24, None, ALU.max)\
                       .then_inc(S["sg_ready"], 1)
                if k % UT == 0 and on_(9):
                    affine(l, n_ln(l, b, k) - 1, bass.ds(b * (2 * P) + (k // UT - 3) * P, P))
                if on_(5) and k % UT == 0:
                    j = k - 5
                    dve.wait_ge(S["wo_done"], n_unit(l, b, j))
                    t0 = b * (2 * P) + (j // UT) * P + PAD
                    for h in range(2):
                        r = slice(64 * h, 64 * h + 64)
                        dve.tensor_tensor(X1[r, bass.ds(t0 + h, P)], AC[r, :], X0[r, bass.ds(t0 + h, P)], ALU.add)\
                           .then_inc(x1_ready, 1)

            def mlp(l):
                last_tile = l * NT + (NT + CREDIT)
                centre(MU_E, last_tile, (NT - 1) * P)
                for g in range(NG):
                    for c, (o, n) in enumerate(FCH):
                        i = 3 * g + c
                        dve.wait_ge(ha_done, l * (NG * 3) + (i + 1))
                        dve.wait_ge(gl_ready, l * (NG * 3) + (i + 1))
                        if g >= 2:
                            dve.wait_ge(mo_done, l * NG + (g - 1))
                        dve.scalar_tensor_tensor(out=hb[g % 2][c][0:n, :], in0=PS[0:n, 2 * c, :],
                                                 scalar=par[0:n, 3 + c:3 + c + 1], in1=gl[i % 2][0:n, :],
                                                 op0=ALU.add, op1=ALU.mult).then_inc(h_ready, 1)
                        if i == 0:
                            variance(VA_E, last_tile)
                        if i == 2:
                            cols = slice((NT - 1) * P, NT * P)
                            scale(RB_E, last_tile, cols)
                            affine(l, last_tile, cols)
                        if c == 0 and g > 0:
                            residual(l, g - 1)
                residual(l, NG - 1)

            def residual(l, g):
                dve.wait_ge(mo_done, l * NG + (g + 1))
                for h in range(2):
                    r = slice(64 * h, 64 * h + 64)
                    c0 = PAD + h + g * GT
                    dve.scalar_tensor_tensor(out=X0[r, c0:c0 + GT], in0=PS[r, 6 + g % 2, :], scalar=par[r, 2:3],
                                             in1=X1[r, c0:c0 + GT], op0=ALU.add, op1=ALU.add)\
                       .then_inc(x0_ready, 1)

            with dve.Fori(0, DEPTH) as l:
                layer_slots(dve, slot, l)
                dve.wait_ge(loaded_mlp, l * 48 + 48)
                mlp(l)

        @block.gpsimd
        def _(pool):
            for s in (S["kp_ready"], S["rn_ready"], S["rs_ready"], rstd_ready):
                pool.sem_inc(s, CREDIT)
            for v in vs:
                pool.memset(v[:, :, :, DH:DH + 1], 1.0)
            for q in qkt:
                last = pool.memset(q[:, 2:4, P:P + WIN], 0.0)
            last.then_inc(lay_ready, 1)
            pool.wait_ge(lay_ready, 1)
            pool.wait_ge(ready, 3)

            def stage(l, b, t):
                if not (isinstance(b, int) and b == 0 and t < 2):
                    pool.wait_ge(S["v_done"], n_unit(l, b, (t - 1) * UT - 1))
                pool.tensor_tensor(xs[t % 2][:, :], X0[:, bass.ds(b * (2 * P) + t * P, WIN + P)],
                                   ones[:, 0:1].to_broadcast([P, WIN + P]), ALU.mult).then_inc(x_staged, 1)

            def table(l, b, t):
                if not (isinstance(b, int) and b == 0 and t < 2):
                    pool.wait_ge(S["cm_ready"], n_unit(l, b, (t - 1) * UT - 1))
                pool.tensor_tensor(
                    tab[t % 2][:, :, :].rearrange("p (s c) e -> p s (c e)", s=2),
                    lay4[:, :].rearrange("p (s n) -> p s n", s=2),
                    rot[:, bass.ds(b * 2 + t, 1), :].to_broadcast([P, 2, 2 * DH]), ALU.mult).then_inc(tab_ready, 1)

            def deviation(n):
                pool.wait_ge(var_ready, n)
                pool.wait_ge(spread, n - 1)
                pool.tensor_tensor(rl[:, :], ve[:, :], half_c[:, 0:1], ALU.pow).then_inc(rstd_ready, 1)

            def slot(l, b, k, on_):
                if k % UT == 3 and on_(8):
                    deviation(n_ln(l, b, k))
                if on_(1):
                    j = k - 1
                    n = n_unit(l, b, j)
                    i = j % 2
                    pool.wait_ge(S["qn_ready"], n)
                    pool.wait_ge(S["qr_ready"], n - 2)
                    pool.wait_ge(tab_ready, n_tile(l, b, j // UT))
                    for s in range(2):
                        for h in range(2):
                            def part(x, hh):
                                return x[:, 256 * s:256 * s + 256].rearrange(
                                    "p (n h e) -> p n h e", n=4, h=2)[:, :, hh, :]
                            last = pool.tensor_tensor(
                                part(rs[i], h), part(qn[i], 1 - h),
                                tab[(j // UT) % 2][:, 2 * s + 1, 32 * h:32 * h + 32].unsqueeze(1)
                                .to_broadcast([P, 4, 32]), ALU.mult)
                    last.then_inc(S["rs_ready"], 1)
                if on_(0):
                    n = n_unit(l, b, k)
                    i = k % 2
                    g = k % UT
                    pool.wait_ge(S["s_done"], n - 4)
                    pool.wait_ge(S["qkt_ready"], n - 4)
                    pool.tensor_tensor(qkt[g][:, 2:4, 0:WIN], qkt[g][:, 2:4, P:P + WIN],
                                       kshift[:, 0:1].unsqueeze(2).to_broadcast([P, 2, WIN]), ALU.mult)\
                        .then_inc(S["kp_ready"], 1)
                    if k % UT == 1:
                        stage(l, b, k // UT + 1)
                    if k % UT == 2:
                        table(l, b, k // UT + 1)
                    pool.wait_ge(S["sg_ready"], n)
                    pool.wait_ge(S["qn_ready"], n - 2)
                    pool.tensor_tensor(rn[i][:, :], sg[i][:, :], half_c[:, :], ALU.pow).then_inc(S["rn_ready"], 1)

            with pool.Fori(0, DEPTH) as l:
                pool.wait_ge(x0_ready, l * (2 * NG) + CREDIT)
                pool.tensor_tensor(lay4[:, :], xpos[:, :], qks[:, bass.ds(l, 1), :].rearrange("p o n -> p (o n)"),
                                   ALU.mult).then_inc(lay_ready, 1)
                stage(l, 0, 0)
                pool.wait_ge(lay_ready, l + 2)
                table(l, 0, 0)
                layer_slots(pool, slot, l)
                deviation(l * NT + (NT + CREDIT))


def stage_last_layer(nc, a, m, out):
    PS, XT, XN, X0 = m["PS"], m["XT"], m["XN"], m["X0"]
    HID = 64
    FH = 512
    FC = FH // P
    STEPS = T.bit_length() - 1
    TWO_PI = 2.0 * np.pi
    TP_HI = float(np.float32(6.28125))
    TP_LO = float(np.float32(TWO_PI - 6.28125))
    ROUND = 12582912.0
    PI_F = float(np.nextafter(np.float32(np.pi), np.float32(0)))

    with ExitStack() as ctx:
        def sb(name, shape, dt=F32):
            return ctx.enter_context(nc.sbuf_tensor(name, shape, dt))

        def sem(name):
            return ctx.enter_context(nc.semaphore(name))

        sqr = sb("l_sqr", [P, T])
        hs = sb("l_hs", [P, T])
        rr = sb("l_rr", [P, FC, T])
        lw = m["l_w"]
        wabs = sb("l_wabs", [P, 2 * FC, P])
        wt = sb("l_wt", [P, 2 * FC, P])
        wsum = sb("l_wsum", [P, 2 * FC])
        wsc = sb("l_wsc", [P, 2 * FC])
        wsr = sb("l_wsr", [P, 2 * FC])
        ptot = sb("l_ptot", [P, 1])
        wfin = sb("l_wfin", [P, 2 * FC, P])
        wtt = sb("l_wtt", [P, 2 * FC, P])
        t1 = sb("l_t1", [16, FH])
        ex = sb("l_ex", [P, 4])
        ang = sb("l_ang", [P, 2])
        rev = sb("l_rev", [P, 2])
        sc2 = sb("l_sc2", [P, 2])
        ab = sb("l_ab", [P, 2])
        bs = sb("l_bs", [P, D])
        bt = sb("l_bt", [P, D])
        cs = sb("l_cs", [P, D])
        sj = sb("l_sj", [P, P])
        la = sb("l_la", [P, STEPS, 2 * P])
        tmp = [sb(f"l_tmp{i}", [P, GT]) for i in range(2)]
        yt = sb("l_yt", [P, T])
        yo = sb("l_yo", [P, NT, D])

        x1_set, v_step, a_step, p_step = sem("l_x1_set"), sem("l_v_step"), sem("l_a_step"), sem("l_p_step")
        mean_done, centred, squared, var_done, logged, rstd_ready, xn_ready = (
            sem("l_" + n) for n in ("mean_done", "centred", "squared", "var_done", "logged", "rstd_ready", "xn_ready"))
        lam_exp, lam_sin, lam_set, pow_done, pow_ready = (
            sem("l_" + n) for n in ("lam_exp", "lam_sin", "lam_set", "pow_done", "pow_ready"))
        babs, wfin_ready, wt_done, wt_ready, bt_done, bt_ready, t1_done, t1_ready, lr_done, wlr_ready = (
            sem("l_" + n) for n in ("babs", "wfin_ready", "wt_done", "wt_ready", "bt_done", "bt_ready",
                                    "t1_done", "t1_ready", "lr_done", "wlr_ready"))
        c_ready, bu_done, bu_ready, sh_done, hs_ready = (
            sem("l_" + n) for n in ("c_ready", "bu_done", "bu_ready", "sh_done", "hs_ready"))
        h_done, relu_ready, rr_ready, y_done, yd_ready, yt_ready, back_done, yo_ready, stored = (
            sem("l_" + n) for n in ("h_done", "relu_ready", "rr_ready", "y_done", "yd_ready", "yt_ready",
                                    "back_done", "yo_ready", "stored"))
        block = ctx.enter_context(nc.Block())

        scan = [(s, g) for s in range(STEPS) for g in range(NG - 1, -1, -1) if (g + 1) * GT > (1 << s)]

        def scan_count(s, g):
            while (s, g) not in scan:
                s -= 1
            return scan.index((s, g)) + 1

        def hidden_after(n):
            return range(n, n + 1) if n < NG * FC else range(0)

        @block.sync
        def _(sp):
            for g in range(NG):
                sp.wait_ge(yo_ready, g + 1)
                sp.dma_start(out[0, g * GT:(g + 1) * GT, :].rearrange("(n p) d -> p n d", p=P),
                             yo[:, 4 * g:4 * g + 4, :]).then_inc(stored, 16)
            sp.wait_ge(stored, 16 * NG)

        @block.tensor
        def _(pe):
            pe.wait_ge(x1_set, 2 * NG)
            for g in range(NG):
                pe.matmul(PS[:, g, :], m["mean_w"][:, :], XT[:, g * GT:(g + 1) * GT], start=True, stop=True)\
                  .then_inc(mean_done, 1)
            for g in range(NG):
                pe.wait_ge(squared, g + 1)
                pe.matmul(PS[:, 4 + g, :], m["mean_w"][:, :], sqr[:, g * GT:(g + 1) * GT], start=True, stop=True)\
                  .then_inc(var_done, 1)
            pe.wait_ge(centred, NG)
            pe.wait_ge(bt_ready, 1)
            pe.transpose(PS[:, 0, 0:P], bs[:, :], m["ident"][:, :]).then_inc(bt_done, 1)
            for s in range(STEPS - 1):
                pe.wait_ge(lam_set if s == 0 else pow_ready, 2 if s == 0 else s)
                pe.matmul(PS[:, 1, 0:P], la[:, s, P:2 * P], la[:, s, 0:P], start=True, stop=True)
                pe.matmul(PS[:, 1, P:2 * P], la[:, s, 0:P], la[:, s, P:2 * P], start=True, stop=True)\
                  .then_inc(pow_done, 1)
            pe.wait_ge(wfin_ready, 1)
            for c in range(2 * FC):
                last = pe.transpose(PS[:, 2 + c // 4, (c % 4) * P:(c % 4 + 1) * P], wfin[:, c, :], m["ident"][:, :])
            last.then_inc(wt_done, 1)
            pe.wait_ge(bt_ready, 2)
            pe.matmul(PS[0:16, 0, :], m["l_fb"][:, :], m["l_ut"][:, :], start=True, stop=True).then_inc(t1_done, 1)
            pe.wait_ge(t1_ready, 1)
            pe.wait_ge(pow_ready, STEPS - 1)
            pe.matmul(PS[:, 1, :], m["l_v"][:, :], t1[:, :], start=True, stop=True).then_inc(lr_done, 1)
            for g in range(NG):
                pe.wait_ge(xn_ready, g + 1)
                pe.matmul(PS[:, 4 + g, :], bt[:, :], XN[:, g * GT:(g + 1) * GT], start=True, stop=True)\
                  .then_inc(bu_done, 1)
            pe.wait_ge(wlr_ready, 1)

            def hidden(i):
                g, c = i // FC, i % FC
                if i >= 2:
                    pe.wait_ge(relu_ready, i - 1)
                pe.matmul(PS[:, 6 + i % 2, :], wtt[:, c, :], XN[:, g * GT:(g + 1) * GT], start=True, stop=True)\
                  .then_inc(h_done, 1)

            for n, (s, g) in enumerate(scan):
                lo = max(g * GT, 1 << s)
                if s == 0:
                    pe.wait_ge(bu_ready, NG)
                else:
                    need = max(scan_count(s - 1, gg) for gg in
                               range((lo - (1 << s)) // GT, ((g + 1) * GT - (1 << s) - 1) // GT + 1))
                    pe.wait_ge(hs_ready, need)
                if n >= 4:
                    pe.wait_ge(hs_ready, n - 3)
                pe.matmul(PS[:, n % 4, 0:(g + 1) * GT - lo], la[:, s, 0:P],
                          hs[:, lo - (1 << s):(g + 1) * GT - (1 << s)], start=True, stop=True).then_inc(sh_done, 1)
                for i in hidden_after(n):
                    hidden(i)
            pe.wait_ge(hs_ready, len(scan))
            pe.wait_ge(c_ready, 1)
            for g in range(NG):
                cols = slice(g * GT, (g + 1) * GT)
                pe.matmul(PS[:, g, :], cs[:, :], hs[:, cols], start=True, stop=False)
                pe.wait_ge(rr_ready, FC * (g + 1))
                for c in range(FC):
                    last = pe.matmul(PS[:, g, :], wtt[:, FC + c, :], rr[:, c, cols], start=False, stop=(c == FC - 1))
                last.then_inc(y_done, 1)
            for g in range(NG):
                pe.wait_ge(yt_ready, g + 1)
                for n in range(4 * g, 4 * g + 4):
                    last = pe.transpose(PS[:, 4 + g, (n % 4) * P:(n % 4 + 1) * P], yt[:, n * P:(n + 1) * P],
                                        m["ident"][:, :])
                last.then_inc(back_done, 1)

        @block.scalar
        def _(act):
            act.wait_ge(m["loaded_l"], 16 * 8)
            act.activation(ex[:, 0:3], m["l_vec"][:, 0:3], ACT.Exp).then_inc(lam_exp, 1)
            act.wait_ge(lam_exp, 1)
            act.activation(ex[:, 3:4], ex[:, 0:1], ACT.Exp, scale=-1.0).then_inc(lam_exp, 1)
            act.activation(wabs[:, :, :], lw[:, :, :], ACT.Abs).then_inc(babs, 1)
            act.wait_ge(lam_sin, 1)
            act.activation(sc2[:, :], rev[:, :], ACT.Sin).then_inc(lam_exp, 1)
            for g in range(NG):
                act.wait_ge(centred, g + 1)
                act.activation(sqr[:, g * GT:(g + 1) * GT], XN[:, g * GT:(g + 1) * GT], ACT.Square)\
                   .then_inc(squared, 1)
            act.wait_ge(bt_done, 1)
            act.activation(bt[:, :], PS[:, 0, 0:P], ACT.Copy).then_inc(a_step, 1)
            for s in range(STEPS - 1):
                act.wait_ge(pow_done, s + 1)
                act.activation(la[:, s + 1, :], PS[:, 1, 0:2 * P], ACT.Copy).then_inc(pow_ready, 1)
                if s == 2:
                    act.wait_ge(var_done, NG)
                    act.activation(sqr[:, :], flat(PS[:, 4:8, :]), ACT.Ln, bias=m["eps_c"][:, 0:1])\
                       .then_inc(logged, 1)
                    act.wait_ge(logged, 1)
                    act.activation(sqr[:, :], sqr[:, :], ACT.Exp, scale=-0.5).then_inc(rstd_ready, 1)
            act.wait_ge(wt_done, 1)
            act.activation(wtt[:, :, :].rearrange("p c n -> p (c n)"), flat(PS[:, 2:4, :]), ACT.Copy)\
               .then_inc(wt_ready, 1)
            act.wait_ge(t1_done, 1)
            act.activation(t1[:, :], PS[0:16, 0, :], ACT.Copy, scale=m["l_gate"][0:16, 0:1]).then_inc(t1_ready, 1)
            for g in range(NG):
                act.wait_ge(bu_done, g + 1)
                act.activation(hs[:, g * GT:(g + 1) * GT], PS[:, 4 + g, :], ACT.Copy).then_inc(bu_ready, 1)
            for i in range(NG * FC):
                g, c = i // FC, i % FC
                act.wait_ge(h_done, i + 1)
                act.activation(rr[:, c, g * GT:(g + 1) * GT], PS[:, 6 + i % 2, :], ACT.Relu).then_inc(relu_ready, 1)
            for g in range(NG):
                act.wait_ge(back_done, g + 1)
                act.activation(yo[:, 4 * g:4 * g + 4, :].rearrange("p n d -> p (n d)"), PS[:, 4 + g, :], ACT.Copy)\
                   .then_inc(yo_ready, 1)

        @block.gpsimd
        def _(pool):
            for i in range(NG * FC):
                g, c = i // FC, i % FC
                r = rr[:, c, g * GT:(g + 1) * GT]
                pool.wait_ge(relu_ready, i + 1)
                pool.tensor_tensor(r, r, r, ALU.mult).then_inc(rr_ready, 1)

        @block.vector
        def _(dve):
            for g in range(NG):
                for h in range(2):
                    r = slice(64 * h, 64 * h + 64)
                    c0 = g * GT
                    dve.tensor_tensor(XT[r, c0:c0 + GT], XT[r, c0:c0 + GT],
                                      X0[r, PAD + h + c0:PAD + h + c0 + GT], ALU.add).then_inc(x1_set, 1)
            step = [0]

            def chain(ins):
                step[0] += 1
                ins.then_inc(v_step, 1)
                dve.wait_ge(v_step, step[0])

            dve.wait_ge(lam_exp, 2)
            chain(dve.tensor_scalar(ang[:, 0:1], ex[:, 1:2], 1.0 / TWO_PI, None, ALU.mult))
            chain(dve.tensor_scalar(ang[:, 1:2], ex[:, 1:2], 1.0 / TWO_PI, 0.25, ALU.mult, ALU.add))
            chain(dve.tensor_scalar(ang[:, :], ang[:, :], ROUND, ROUND, ALU.add, ALU.subtract))
            for i in range(2):
                chain(dve.scalar_tensor_tensor(out=rev[:, i:i + 1], in0=ang[:, i:i + 1], scalar=-TP_HI,
                                               in1=ex[:, 1:2], op0=ALU.mult, op1=ALU.add))
            chain(dve.scalar_tensor_tensor(out=rev[:, :], in0=ang[:, :], scalar=-TP_LO, in1=rev[:, :],
                                           op0=ALU.mult, op1=ALU.add))
            chain(dve.tensor_scalar(rev[:, 1:2], rev[:, 1:2], float(np.pi / 2), None, ALU.add))
            dve.tensor_scalar(rev[:, :], rev[:, :], PI_F, -PI_F, ALU.min, ALU.max).then_inc(lam_sin, 1)
            for g in range(NG):
                cols = slice(g * GT, (g + 1) * GT)
                dve.wait_ge(mean_done, g + 1)
                dve.tensor_tensor(XN[:, cols], XT[:, cols], PS[:, g, :], ALU.subtract).then_inc(centred, 1)
            dve.tensor_scalar(bs[:, :], m["l_b"][:, :], ex[:, 2:3], None, ALU.mult).then_inc(bt_ready, 1)
            dve.wait_ge(lam_exp, 3)
            chain(dve.tensor_scalar(ab[:, 0:1], sc2[:, 1:2], ex[:, 3:4], None, ALU.mult))
            chain(dve.tensor_scalar(ab[:, 1:2], sc2[:, 0:1], ex[:, 3:4], m["l_vec"][:, 3:4], ALU.mult, ALU.mult))
            for h in range(2):
                chain(dve.tensor_scalar(sj[:, 64 * h:64 * h + 64], m["ident"][:, 64 - 64 * h:128 - 64 * h], ab[:, 1:2],
                                        None, ALU.mult))
            dve.scalar_tensor_tensor(out=la[:, 0, 0:P], in0=m["ident"][:, :], scalar=ab[:, 0:1], in1=sj[:, :],
                                     op0=ALU.mult, op1=ALU.add).then_inc(lam_set, 1)
            dve.scalar_tensor_tensor(out=la[:, 0, P:2 * P], in0=m["ident"][:, :], scalar=ab[:, 0:1], in1=sj[:, :],
                                     op0=ALU.mult, op1=ALU.subtract).then_inc(lam_set, 1)
            dve.tensor_scalar(cs[:, :], m["l_ct"][:, :], m["l_vec"][:, 3:4], None, ALU.mult).then_inc(c_ready, 1)
            dve.wait_ge(babs, 1)
            chain(dve.tensor_reduce(wsum[:, :], wabs[:, :, :], AX.X, ALU.add))
            chain(dve.tensor_reduce(ptot[:, :], wsum[:, FC:2 * FC], AX.X, ALU.add))
            chain(dve.tensor_scalar(wsc[:, 0:FC], wsum[:, 0:FC], 1.0 / D, 1e-5, ALU.mult, ALU.max))
            chain(dve.tensor_scalar(wsc[:, FC:2 * FC], ptot[:, 0:1].to_broadcast([P, FC]), 1.0 / FH, 1e-5,
                                    ALU.mult, ALU.max))
            chain(dve.reciprocal(wsr[:, :], wsc[:, :]))
            wide = [P, 2 * FC, P]
            chain(dve.tensor_tensor(wt[:, :, :], lw[:, :, :], wsr[:, :].unsqueeze(2).to_broadcast(wide), ALU.mult))
            chain(dve.tensor_scalar(wt[:, :, :], wt[:, :, :], ROUND, ROUND, ALU.add, ALU.subtract))
            chain(dve.tensor_scalar(wt[:, :, :], wt[:, :, :], -1.0, 1.0, ALU.max, ALU.min))
            chain(dve.tensor_tensor(wt[:, :, :], wt[:, :, :], lw[:, :, :], ALU.subtract))
            chain(dve.tensor_tensor(wt[:, :, :], wt[:, :, :], lw[:, :, :], ALU.add))
            dve.tensor_tensor(wfin[:, :, :], wt[:, :, :], wsc[:, :].unsqueeze(2).to_broadcast(wide), ALU.mult)\
               .then_inc(wfin_ready, 1)
            dve.wait_ge(a_step, 1)
            dve.sem_inc(bt_ready, 1)
            dve.wait_ge(rstd_ready, 1)
            for g in range(NG):
                cols = slice(g * GT, (g + 1) * GT)
                dve.tensor_tensor(XN[:, cols], XN[:, cols], sqr[:, cols], ALU.mult).then_inc(xn_ready, 1)
            dve.wait_ge(lr_done, 1)
            dve.wait_ge(wt_ready, 1)
            w = wtt[:, 0:FC, :].rearrange("p c n -> p (c n)")
            dve.tensor_tensor(w, w, PS[:, 1, :], ALU.add).then_inc(wlr_ready, 1)
            for n, (s, g) in enumerate(scan):
                lo = max(g * GT, 1 << s)
                cols = slice(lo, (g + 1) * GT)
                if s == 0:
                    dve.wait_ge(bu_ready, NG)
                dve.wait_ge(sh_done, n + 1)
                dve.tensor_tensor(hs[:, cols], PS[:, n % 4, 0:(g + 1) * GT - lo], hs[:, cols], ALU.add)\
                   .then_inc(hs_ready, 1)
            for g in range(NG):
                cols = slice(g * GT, (g + 1) * GT)
                dve.wait_ge(y_done, g + 1)
                dve.scalar_tensor_tensor(out=tmp[g % 2][:, :], in0=XN[:, cols], scalar=m["l_vec"][:, 4:5],
                                         in1=PS[:, g, :], op0=ALU.mult, op1=ALU.add).then_inc(yd_ready, 1)
                dve.wait_ge(yd_ready, g + 1)
                dve.tensor_tensor(yt[:, cols], XT[:, cols], tmp[g % 2][:, :], ALU.add).then_inc(yt_ready, 1)


def constants():
    half = np.arange(0, DH, 2, dtype=np.float32)
    inv_freq = (1.0 / np.power(np.float32(10000.0), half / np.float32(DH))).astype(np.float32)
    freqs = (np.arange(T, dtype=np.float32)[:, None] * inv_freq[None, :]).astype(np.float32).astype(np.float64)
    cos = np.concatenate([np.cos(freqs)] * 2, -1)
    sin = np.concatenate([np.sin(freqs)] * 2, -1)
    rot = np.zeros((P, NT + 1, 2, DH), np.float32)
    rot[:, :NT, 0] = cos.reshape(NT, P, DH).transpose(1, 0, 2)
    rot[:, :NT, 1] = sin.reshape(NT, P, DH).transpose(1, 0, 2)
    base = ((half.astype(np.float64) + 0.4 * DH) / (1.4 * DH))
    base = np.concatenate([base, base])
    power = (np.arange(P) - P // 2)[:, None] / (WIN // 2)
    sc = base[None, :] ** power
    sign = np.concatenate([-np.ones(DH // 2), np.ones(DH // 2)])
    xpos = np.stack([8.0 * sc, 8.0 * sc * sign, 1.0 / sc, sign / sc], 1).astype(np.float32)
    kshift = np.concatenate([base, base])[:, None] ** (P / (WIN // 2))
    i, c = np.arange(P)[:, None] % WIN, np.arange(2 * WIN)[None, :]
    ok = (c >= i) & (c <= i + WIN)
    first = ok & ~((np.arange(P)[:, None] < WIN) & (c < WIN))
    mask = np.stack([np.where(v, 0.0, MASKED) for v in (np.tile(first, 2), np.tile(ok, 2))], 1)
    q, c = np.arange(P)[:, None], np.arange(2 * P)[None, :]
    own = c - P <= q
    a_mask = np.stack([np.where(v, 0.0, MASKED) for v in (own & (c >= P), own)], 1)
    g = np.arange(96) // 8
    return {
        "a_mask": a_mask.astype(np.float32),
        "a_bmask": (g[:, None] == g[None, :]).astype(np.float32),
        "c_ident": np.eye(P, dtype=np.float32),
        "c_rot": rot.reshape(P, NT + 1, 2 * DH),
        "c_xpos": xpos.reshape(P, 4 * DH),
        "c_kshift": kshift.astype(np.float32),
        "c_mask": mask.astype(np.float32),
    }


def lay_out(x):
    def chunks(v):
        z = np.zeros((DEPTH, len(FCH) * P), np.float32)
        z[:, :FF] = v
        return z.reshape(DEPTH, len(FCH), P).transpose(0, 2, 1)

    b1 = np.asarray(x["L0_ffn_b1"])
    par = np.concatenate([np.asarray(x["L0_ffn_ln_g"])[:, :, None], np.asarray(x["L0_ffn_ln_b"])[:, :, None],
                          np.asarray(x["L0_ffn_b2"])[:, :, None], chunks(b1[:, :FF]), chunks(b1[:, FF:])], 2)
    w2 = np.zeros((DEPTH, len(FCH) * P, D), np.float32)
    w2[:, :FF] = np.asarray(x["L0_ffn_W2"])
    qs, ks = np.asarray(x["L0_ffn_q_scale"]), np.asarray(x["L0_ffn_k_scale"])
    h = DH // 2
    def f(n):
        return np.asarray(x[n])

    def twice(n):
        return np.concatenate([f(n), f(n)])

    sign = np.concatenate([np.ones(64), -np.ones(64)]).astype(np.float32)
    vec = np.stack([twice("L1_attn_nu_log"), twice("L1_attn_theta_log"), twice("L1_attn_gamma_log"), sign,
                    f("L1_attn_D")], 1)
    four = np.concatenate([qs, qs[:, h:], qs[:, :h], ks, ks[:, h:], ks[:, :h]], 1)
    return {
        "a_w": np.concatenate([f("L0_attn_W" + c) for c in "qkvo"], 1),
        "a_bo": f("L0_attn_bo")[:, None],
        "l_vec": vec,
        "l_gate": np.broadcast_to(f("L1_ffn_gate").reshape(1, 1), (P, 1)),
        "l_b": np.concatenate([f("L1_attn_B_re"), f("L1_attn_B_im")], 0),
        "l_ct": np.concatenate([f("L1_attn_C_re").T, f("L1_attn_C_im").T], 0),
        "l_ut": f("L1_ffn_u").T,
        "l_w": np.concatenate([f("L1_ffn_w_fc").reshape(4, P, D).transpose(1, 0, 2),
                               f("L1_ffn_w_proj").reshape(P, 4, P)], 1),
        "l_par": par,
        "l_w2": w2.reshape(DEPTH, len(FCH), P, D).transpose(0, 2, 1, 3).reshape(DEPTH, P, len(FCH) * D),
        "l_wo": np.asarray(x["L0_ffn_Wo"]).reshape(DEPTH, HEADS // 2, P, D).transpose(0, 2, 1, 3)
        .reshape(DEPTH, P, HEADS // 2 * D),
        "c_qk_scales": np.broadcast_to(four[None], (P, DEPTH, 4 * DH)),
    }


_INS = ["L0_attn_x", "L0_ffn_Wqkv", "L0_ffn_W1", "L1_ffn_fast_b", "L1_ffn_v"]
_OUTS = [((1, T, D), "float32")]


def kernel(**inputs):
    import concourse.bacc as _bacc
    from concourse.bass_utils import run_bass_kernel_spmd as _run

    nc = _bacc.Bacc("TRN2", target_bir_lowering=False, num_devices=1)
    given = {n: np.asarray(inputs[n]) for n in _INS}
    given.update(lay_out(inputs))
    given.update(constants())
    arrays, args = {}, {}
    for name, v in given.items():
        v = np.ascontiguousarray(v)
        arrays[f"in_{name}_dram"] = v
        args[name] = nc.dram_tensor(f"in_{name}_dram", v.shape, mybir.dt.from_np(v.dtype), kind="ExternalInput").ap()
    shape, dtype = _OUTS[0]
    out = nc.dram_tensor("out_0_dram", shape, mybir.dt.from_np(np.dtype(dtype)), kind="ExternalOutput").ap()
    program(nc, args, out)
    r = _run(nc, [arrays], core_ids=[0])
    return r.results[0]["out_0_dram"]
```

```python
from contextlib import ExitStack

import concourse.bass as bass
import numpy as np
from concourse import mybir

F32 = mybir.dt.float32
BF16 = mybir.dt.bfloat16
F32R = mybir.dt.float32r
I32 = mybir.dt.int32
HI_BITS = -4096
ALU = mybir.AluOpType
ACT = mybir.ActivationFunctionType
AX = mybir.AxisListType

P = 128
T = 2048
D = 128
NT = T // P
NG = 4
GT = T // NG
BANK = 512

DEPTH = 6
HEADS = 16
DH = 64
WIN = 32
INNER = HEADS * DH
FF = int(D * 4 * 2 / 3)
FCH = [(c * P, min(P, FF - c * P)) for c in range(-(-FF // P))]
PAD = WIN
XW = PAD + T + P + 1
UT = 4
UNITS = NT * UT
BODY = 8
WCH = 2 * INNER // BANK
LAG = 5
CREDIT = 8
MASKED = -1.0e30
LN_EPS = 1e-5
ROUND = 12582912.0

FH = 512
FC = FH // P
NPAR = 3 + 2 * len(FCH)


def flat(ap):
    return ap.rearrange("p a b -> p (a b)")


def program(nc, a, out):
    ctx = ExitStack()
    with ctx:
        def sb(name, shape, dt=F32):
            return ctx.enter_context(nc.sbuf_tensor(name, shape, dt))

        def sem(name):
            return ctx.enter_context(nc.semaphore(name))

        PS = ctx.enter_context(nc.psum_tensor("PS", [P, 8, BANK], F32))

        XT = sb("XT", [P, T])
        XN = sb("XN", [P, T])
        X0 = sb("X0", [P, XW])
        X1 = sb("X1", [P, XW])
        ident = sb("ident", [P, P])
        ident_bf = sb("ident_bf", [P, P], BF16)
        mean_w = sb("mean_w", [P, P])
        eps_c = sb("eps_c", [P, 1])

        loaded_x = sem("loaded_x")
        loaded_const = sem("loaded_const")
        const_ready = sem("const_ready")
        ident_ready = sem("ident_ready")

        a_w = sb("a_w", [P, 4 * D])
        a_bo = sb("a_bo", [P, 1])
        a_maskf = sb("a_maskf", [P, 2, 2 * P])
        a_bmask = sb("a_bmask", [96, 96])
        l_w = sb("l_w", [P, 8, P])
        l_vec = sb("l_vec", [P, 5])
        l_wfin = sb("l_wfin", [P, 8, P])
        l_wfin_ready = sem("l_wfin_ready")
        l_gate = sb("l_gate", [P, 1])
        l_b = sb("l_b", [P, D])
        l_ct = sb("l_ct", [P, D])
        l_fb = sb("l_fb", [16, 16])
        l_ut = sb("l_ut", [16, 512])
        l_v = sb("l_v", [16, D])
        loaded_a = sem("loaded_a")
        loaded_l = sem("loaded_l")

        wqkv = sb("wqkv", [P, 3 * INNER])
        wo = sb("wo", [P, HEADS // 2, D])
        w1 = sb("w1", [P, 2 * FF])
        w2 = sb("w2", [P, len(FCH), D])
        par = sb("par", [P, NPAR])
        qks = sb("qks", [P, DEPTH, 4 * DH])
        xpos = sb("xpos", [P, 4 * DH])
        rot = sb("rot", [P, NT + 1, 2 * DH])
        kshift = sb("kshift", [P, 1])
        maskf = sb("maskf", [P, 2, P])
        loaded_tab, loaded_qkv, loaded_wo, loaded_mlp = (sem(n) for n in
                                                        ("loaded_tab", "loaded_qkv", "loaded_wo", "loaded_mlp"))
        w_hi = sb("w_hi", [P, 2 * INNER], F32R)
        w_lo = sb("w_lo", [P, 2 * INNER], F32R)
        w_cut = [sb(f"w_cut{i}", [P, BANK], I32) for i in range(2)]
        w_cut_ready, w_hi_ready, w_lo_ready = (sem(n) for n in ("w_cut_ready", "w_hi_ready", "w_lo_ready"))
        w = dict(PS=PS, XT=XT, XN=XN, X0=X0, X1=X1, ident=ident, ident_bf=ident_bf, mean_w=mean_w, eps_c=eps_c,
                      loaded_x=loaded_x, loaded_const=loaded_const, const_ready=const_ready,
                      ident_ready=ident_ready, a_w=a_w, a_bo=a_bo,
                      a_maskf=a_maskf, a_bmask=a_bmask, w_hi=w_hi, w_lo=w_lo, w_cut=w_cut,
                      w_cut_ready=w_cut_ready, w_hi_ready=w_hi_ready, w_lo_ready=w_lo_ready,
                      l_w=l_w, l_wfin=l_wfin, l_wfin_ready=l_wfin_ready, l_vec=l_vec, l_gate=l_gate, l_b=l_b,
                      l_ct=l_ct, l_fb=l_fb, l_ut=l_ut, l_v=l_v, loaded_a=loaded_a, loaded_l=loaded_l, wqkv=wqkv, wo=wo, w1=w1,
                      w2=w2, par=par, qks=qks, xpos=xpos, rot=rot, kshift=kshift, maskf=maskf,
                      loaded_tab=loaded_tab, loaded_qkv=loaded_qkv, loaded_wo=loaded_wo, loaded_mlp=loaded_mlp)
        stage_norm_input(nc, a, w)
        stage_mixed_attention(nc, a, w)
        stage_layers(nc, a, w)
        stage_last_layer(nc, a, w, out)


def stage_norm_input(nc, a, m):
    PS, XT, XN, X0, X1 = m["PS"], m["XT"], m["XN"], m["X0"], m["X1"]
    with ExitStack() as ctx:
        def sb(name, shape, dt=F32):
            return ctx.enter_context(nc.sbuf_tensor(name, shape, dt))

        def sem(name):
            return ctx.enter_context(nc.semaphore(name))

        xin = sb("xin", [P, NT, D])
        sqr = sb("sqr", [P, T])
        turned = sem("turned")
        xt_ready = sem("xt_ready")
        mean_done = sem("mean_done")
        centred = sem("centred")
        squared = sem("squared")
        var_done = sem("var_done")
        logged = sem("logged")
        rstd_ready = sem("rstd_ready")
        xn_ready = sem("xn_ready")
        x0_set = sem("x0_set")
        x0_shifted = sem("x0_shifted")
        block = ctx.enter_context(nc.Block())

        @block.sync
        def _(sp):
            sp.dma_start(m["ident"][:, :], a["c_ident"]).then_inc(m["loaded_const"], 16)
            for q in range(NG):
                sp.dma_start(xin[:, 4 * q:4 * q + 4, :],
                             a["L0_attn_x"][0, q * GT:(q + 1) * GT, :].rearrange("(n p) d -> p n d", p=P))\
                  .then_inc(m["loaded_x"], 16)
            sp.dma_start(m["a_w"][:, :], a["a_w"]).then_inc(m["loaded_a"], 16)
            sp.dma_start(m["a_bo"][:, :], a["a_bo"]).then_inc(m["loaded_a"], 16)
            sp.dma_start(m["a_maskf"][:, :, :], a["a_mask"]).then_inc(m["loaded_a"], 16)
            sp.dma_start(m["a_bmask"][:, :], a["a_bmask"]).then_inc(m["loaded_a"], 16)
            sp.dma_start(m["wqkv"][:, :], a["L0_ffn_Wqkv"][0, :, :]).then_inc(m["loaded_qkv"], 16)
            for t, n in ((m["qks"][:, :, :], "c_qk_scales"), (m["xpos"][:, :], "c_xpos"), (m["rot"][:, :, :], "c_rot"),
                         (m["kshift"][:, :], "c_kshift"), (m["maskf"][:, :, :], "c_mask")):
                sp.dma_start(t, a[n]).then_inc(m["loaded_tab"], 16)
            sp.dma_start(flat(m["wo"][:, :, :]), a["l_wo"][0, :, :]).then_inc(m["loaded_wo"], 16)
            sp.dma_start(m["w1"][:, :], a["L0_ffn_W1"][0, :, :]).then_inc(m["loaded_mlp"], 16)
            sp.dma_start(flat(m["w2"][:, :, :]), a["l_w2"][0, :, :]).then_inc(m["loaded_mlp"], 16)
            sp.dma_start(m["par"][:, :], a["l_par"][0, :, :]).then_inc(m["loaded_mlp"], 16)
            for t, n in ((m["l_vec"], "l_vec"), (m["l_gate"], "l_gate"), (m["l_b"], "l_b"), (m["l_ct"], "l_ct"),
                         (m["l_fb"], "L1_ffn_fast_b"), (m["l_ut"], "l_ut"), (m["l_v"], "L1_ffn_v")):
                sp.dma_start(t[:, :], a[n]).then_inc(m["loaded_l"], 16)
            sp.dma_start(m["l_w"][:, :, :], a["l_w"]).then_inc(m["loaded_l"], 16)

        @block.gpsimd
        def _(pool):
            pool.memset(m["mean_w"][:, :], 1.0 / D).then_inc(m["const_ready"], 1)
            pool.memset(m["eps_c"][:, :], LN_EPS).then_inc(m["const_ready"], 1)
            pool.memset(X0[:, :], 0.0).then_inc(m["const_ready"], 1)
            pool.memset(X1[:, :], 0.0).then_inc(m["const_ready"], 1)

        @block.tensor
        def _(pe):
            pe.wait_ge(m["loaded_const"], 16)
            pe.wait_ge(m["loaded_x"], 16 * NG)
            for n in range(NT):
                pe.transpose(PS[:, n // 4, (n % 4) * P:(n % 4 + 1) * P], xin[:, n, :], m["ident"][:, :])\
                  .then_inc(turned, 1)
            pe.wait_ge(m["const_ready"], 4)
            for g in range(NG):
                pe.wait_ge(xt_ready, g + 1)
                pe.matmul(PS[:, 4 + g, :], m["mean_w"][:, :], XT[:, g * GT:(g + 1) * GT], start=True, stop=True)\
                  .then_inc(mean_done, 1)
            for g in range(NG):
                pe.wait_ge(squared, g + 1)
                pe.matmul(PS[:, g, :], m["mean_w"][:, :], sqr[:, g * GT:(g + 1) * GT], start=True, stop=True)\
                  .then_inc(var_done, 1)

        @block.scalar
        def _(act):
            for g in range(NG):
                act.wait_ge(turned, 4 * g + 4)
                act.activation(XT[:, g * GT:(g + 1) * GT], PS[:, g, :], ACT.Copy).then_inc(xt_ready, 1)
            for g in range(NG):
                act.wait_ge(centred, g + 1)
                act.activation(sqr[:, g * GT:(g + 1) * GT], XN[:, g * GT:(g + 1) * GT], ACT.Square)\
                   .then_inc(squared, 1)

            def upper_w(c):
                act.wait_ge(m["w_cut_ready"], c + 1)
                act.activation(m["w_hi"][:, c * BANK:(c + 1) * BANK], m["w_cut"][c % 2][:, :].bitcast(F32), ACT.Copy)\
                   .then_inc(m["w_hi_ready"], 1)

            upper_w(0)
            upper_w(1)
            act.wait_ge(var_done, NG)
            act.wait_ge(m["const_ready"], 4)
            act.activation(sqr[:, :], flat(PS[:, 0:4, :]), ACT.Ln, bias=m["eps_c"][:, 0:1]).then_inc(logged, 1)
            act.wait_ge(logged, 1)
            for h in range(2):
                half = sqr[:, h * T // 2:(h + 1) * T // 2]
                act.activation(half, half, ACT.Exp, scale=-0.5).then_inc(rstd_ready, 1)
            upper_w(2)
            upper_w(3)
            for g in range(NG):
                act.wait_ge(xn_ready, g + 1)
                act.activation(X0[64:128, PAD + 1 + g * GT:PAD + 1 + (g + 1) * GT],
                               XN[64:128, g * GT:(g + 1) * GT], ACT.Copy).then_inc(x0_shifted, 1)

        @block.vector
        def _(dve):
            dve.wait_ge(m["loaded_const"], 16)
            dve.tensor_copy(m["ident_bf"][:, :], m["ident"][:, :]).then_inc(m["ident_ready"], 1)
            for g in range(NG):
                dve.wait_ge(mean_done, g + 1)
                dve.tensor_tensor(XN[:, g * GT:(g + 1) * GT], XT[:, g * GT:(g + 1) * GT], PS[:, 4 + g, :],
                                  ALU.subtract).then_inc(centred, 1)
            def layernorm():
                dve.wait_ge(m["const_ready"], 4)
                for g in range(NG):
                    cols = slice(g * GT, (g + 1) * GT)
                    dve.wait_ge(rstd_ready, 1 + g // 2)
                    dve.tensor_tensor(XN[:, cols], XN[:, cols], sqr[:, cols], ALU.mult).then_inc(xn_ready, 1)
                for g in range(NG):
                    cols = slice(g * GT, (g + 1) * GT)
                    dve.wait_ge(xn_ready, g + 1)
                    dve.tensor_copy(X0[0:64, PAD + g * GT:PAD + (g + 1) * GT], XN[0:64, cols]).then_inc(x0_set, 1)

            dve.wait_ge(m["loaded_qkv"], 16)
            for c in range(WCH):
                w = m["wqkv"][:, c * BANK:(c + 1) * BANK]
                cut = m["w_cut"][c % 2]
                if c >= 2:
                    dve.wait_ge(m["w_hi_ready"], c - 1)
                dve.tensor_scalar(cut[:, :], w.bitcast(I32), HI_BITS, None, ALU.bitwise_and)\
                   .then_inc(m["w_cut_ready"], 1)
                dve.wait_ge(m["w_cut_ready"], c + 1)
                dve.tensor_tensor(m["w_lo"][:, c * BANK:(c + 1) * BANK], w, cut[:, :].bitcast(F32), ALU.subtract)\
                   .then_inc(m["w_lo_ready"], 1)
            layernorm()


def stage_mixed_attention(nc, a, m):
    PS, XT, XN, maskf, bmask = m["PS"], m["XT"], m["XN"], m["a_maskf"], m["a_bmask"]
    LH, E = 4, 8
    LW = LH * E
    GW = D - LW
    GH = GW // E
    BLK = 64
    PA = PS[:, 0, :]
    PB = PS[0:LW, 1, :]
    SCO = PS[:, 2:4, :].rearrange("p b n -> p (b n)").rearrange("p (h n) -> p h n", h=LH)
    PTB = PS[:, 4:6, :].rearrange("p b n -> p (b n)")
    QF = PS[0:GW, 6, 0:P]
    CT = PS[:, 6, P:2 * P]
    OG = PS[:, 6, 2 * P:2 * P + GW]
    OL = PS[:, 6, 2 * P + GW:2 * P + GW + LH * (E + 1)].rearrange("p (h e) -> p h e", h=LH)
    CX = PS[0:GW, 7, 0:GW + 1]

    with ExitStack() as ctx:
        def sb(name, shape, dt=F32):
            return ctx.enter_context(nc.sbuf_tensor(name, shape, dt))

        def sem(name):
            return ctx.enter_context(nc.semaphore(name))

        wq_z = sb("wq_z", [P, LH, LW])
        mask = sb("a_mask", [P, 2, 2 * P], BF16)
        ones = sb("a_ones", [P, 1])
        xs = [sb(f"a_xs{i}", [P, P]) for i in range(2)]
        qk = [sb(f"a_qk{i}", [P, 2 * D]) for i in range(2)]
        kt = [sb(f"a_kt{i}", [LW, P]) for i in range(4)]
        qz = [sb(f"a_qz{i}", [LW, LH, P]) for i in range(2)]
        vx = [sb(f"a_vx{i}", [P, GW + 1]) for i in range(2)]
        vl = [sb(f"a_vl{i}", [P, LH, E + 1]) for i in range(4)]
        qm = [sb(f"a_qm{i}", [P, GH]) for i in range(2)]
        qd = [sb(f"a_qd{i}", [P, GW]) for i in range(2)]
        qe = [sb(f"a_qe{i}", [P, GW]) for i in range(2)]
        qs = [sb(f"a_qs{i}", [P, GH]) for i in range(2)]
        qi = [sb(f"a_qi{i}", [P, GH]) for i in range(2)]
        qf = [sb(f"a_qf{i}", [P, GW]) for i in range(2)]
        ke = [sb(f"a_ke{i}", [P, GW]) for i in range(2)]
        kp = [sb(f"a_kp{i}", [P, GW]) for i in range(2)]
        kf = [sb(f"a_kf{i}", [P, GW]) for i in range(2)]
        qft = [sb(f"a_qft{i}", [GW, P]) for i in range(2)]
        cx = sb("a_cx", [GW, GW + 1])
        cd = sb("a_cd", [GW, 1])
        cr = sb("a_cr", [GW, 1])
        cn = [sb(f"a_cn{i}", [GW, GW]) for i in range(2)]
        mx = sb("a_mx", [P, LH])
        sm = sb("a_sm", [P, LH, 2 * P])
        pr = [sb(f"a_pr{i}", [P, LH, 2 * P]) for i in range(2)]
        pt = sb("a_pt", [P, LH * 2 * P])
        oi = sb("a_oi", [P, LH])
        oc = [sb(f"a_oc{i}", [P, D]) for i in range(4)]
        oct_ = sb("a_oct", [P, P])

        prepared = sem("a_prepared")
        zeroed = sem("a_zeroed")
        pe_sems = ("proj", "qft", "cx", "sc", "pt", "pv", "ct", "out")
        act_sems = ("qk", "kt", "qz", "vx", "vl", "ke", "qe", "qfe", "ex", "pte", "cte")
        dve_sems = ("qm", "qs", "qi", "kf", "cxa", "cda", "cra", "cn", "mx", "sm", "og", "oi", "ol", "xt")
        pool_sems = ("xs", "qd", "qf", "kp")
        sems = {f"{e}_{n}": sem(f"a_{e}_{n}") for e, ns in (
            ("pe", pe_sems), ("act", act_sems), ("dve", dve_sems), ("pool", pool_sems)) for n in ns}
        S = sems
        block = ctx.enter_context(nc.Block())
        TB = 4

        def n_(b, j):
            return b * TB + (CREDIT + j + 1)

        def n2(b, j, i):
            return b * (2 * TB) + (CREDIT + 2 * j + i + 1)

        def credit(eng, names):
            for n in names:
                eng.sem_inc(sems[n], CREDIT)

        def tiles(eng, slot):
            for k in range(TB):
                slot(0, k, lambda lag, k=k: k >= lag)
            with eng.Fori(1, NT // TB) as b:
                for k in range(TB):
                    slot(b, k, lambda lag: True)
            for k in range(3):
                slot(NT // TB, k, lambda lag, k=k: k < lag)

        @block.tensor
        def _(pe):
            def slot(b, k, on_):
                if on_(0):
                    pe.wait_ge(S["pool_xs"], n_(b, k))
                    pe.wait_ge(S["act_vl"], n_(b, k) - 1)
                    x = xs[k % 2][:, :]
                    pe.matmul(PA[:, 0:3 * D], x, m["a_w"][:, 0:3 * D], start=True, stop=True)
                    pe.matmul(PA[0:LW, 3 * D:4 * D], m["a_w"][:, D:D + LW], x, start=True, stop=True)
                    for h in range(LH):
                        last = pe.matmul(PB[:, h * P:(h + 1) * P], wq_z[:, h, :], x, start=True, stop=True)
                    last.then_inc(S["pe_proj"], 1)
                if on_(2):
                    j = k - 2
                    pe.wait_ge(S["act_ex"], n_(b, j))
                    pe.wait_ge(S["act_pte"], n_(b, j) - 1)
                    for h in range(LH):
                        for c in range(2):
                            last = pe.transpose(PTB[:, (2 * h + c) * P:(2 * h + c + 1) * P],
                                                pr[j % 2][:, h, c * P:(c + 1) * P], m["ident"][:, :])
                    last.then_inc(S["pe_pt"], 1)
                if on_(1) or on_(3):
                    if on_(2):
                        pe.wait_ge(S["dve_og"], n_(b, k - 2))
                    pe.wait_ge(S["dve_ol"], n_(b, k - 3))
                    pe.wait_ge(S["dve_xt"], n_(b, k - 4))
                if on_(1):
                    j = k - 1
                    pe.wait_ge(S["pool_qf"], n_(b, j))
                    pe.transpose(QF, qf[j % 2][:, :], m["ident"][:, :]).then_inc(S["pe_qft"], 1)
                if on_(3):
                    pe.transpose(CT, oc[(k - 3) % 4][:, :], m["ident"][:, :]).then_inc(S["pe_ct"], 1)

                def scores(hs):
                    j = k - 1
                    first = isinstance(b, int) and b == 0 and j == 0
                    for h in hs:
                        pe.matmul(SCO[:, h, :], m["ident_bf"][:, :], mask[:, 0 if first else 1, :],
                                  start=(h % 2 == 0), stop=False, skip_group_check=True)
                    for h in hs:
                        for c in range(2):
                            last = pe.matmul(SCO[:, h, c * P:(c + 1) * P], qz[j % 2][:, h, :],
                                             kt[(j - 1 + c) % 4][:, :], start=False, stop=True,
                                             skip_group_check=True)
                    return last

                def linear(i):
                    j = k - 1
                    rows = slice(BLK * i, BLK * i + BLK)
                    pe.wait_ge(S["dve_cn"], n2(b, j, i) - 1)
                    pe.matmul(OG[rows, :], qft[j % 2][:, rows], cn[i][:, :], start=True, stop=True)
                    pe.wait_ge(S["dve_kf"], n_(b, j))
                    pe.wait_ge(S["act_vx"], n_(b, j))
                    pe.matmul(CX, kf[j % 2][rows, :], vx[j % 2][rows, :], start=True, stop=True)\
                      .then_inc(S["pe_cx"], 1)

                if on_(1):
                    pe.wait_ge(S["act_kt"], n_(b, k - 1))
                    pe.wait_ge(S["act_qz"], n_(b, k - 1))
                    pe.wait_ge(S["dve_sm"], n_(b, k - 1) - 1)
                    scores((0, 1))
                    pe.wait_ge(S["act_qfe"], n_(b, k - 1))
                if on_(3):
                    pe.wait_ge(S["act_cte"], n_(b, k - 3))
                if on_(1):
                    linear(0)
                if on_(3):
                    pe.matmul(CT, m["a_w"][:, 3 * D:4 * D], oct_[:, :], start=True, stop=True).then_inc(S["pe_out"], 1)
                if on_(1):
                    scores((2, 3)).then_inc(S["pe_sc"], 1)
                if on_(2):
                    j = k - 2
                    pe.wait_ge(S["act_pte"], n_(b, j))
                    pe.wait_ge(S["act_vl"], n_(b, j))
                    for h in range(LH):
                        for c in range(2):
                            last = pe.matmul(OL[:, h, :], pt[:, (2 * h + c) * P:(2 * h + c + 1) * P],
                                             vl[(j - 1 + c) % 4][:, h, :], start=(c == 0), stop=(c == 1))
                    last.then_inc(S["pe_pv"], 1)
                if on_(1):
                    linear(1)

            credit(pe, ["pe_" + n for n in pe_sems])
            pe.wait_ge(prepared, 3)
            pe.wait_ge(zeroed, 2)
            pe.wait_ge(m["loaded_a"], 64)
            tiles(pe, slot)

        @block.scalar
        def _(act):
            def slot(b, k, on_):
                n = n_(b, k)
                i = k % 2
                if on_(0):
                    act.wait_ge(S["pe_proj"], n)
                    act.wait_ge(S["pool_qd"], n - 2)
                    act.wait_ge(S["pool_kp"], n - 2)
                    act.wait_ge(S["act_ke"], n - 2)
                    act.activation(qk[i][:, :], PA[:, 0:2 * D], ACT.Copy).then_inc(S["act_qk"], 1)
                    act.wait_ge(S["pe_sc"], n - 2)
                    act.activation(kt[k % 4][:, :], PA[0:LW, 3 * D:4 * D], ACT.Copy).then_inc(S["act_kt"], 1)
                    act.activation(qz[i][:, :, :].rearrange("p h n -> p (h n)"), PB, ACT.Copy)\
                       .then_inc(S["act_qz"], 1)
                    act.wait_ge(S["pe_cx"], n2(b, k - 2, 1))
                    act.activation(vx[i][:, 0:GW], PA[:, 2 * D + LW:3 * D], ACT.Copy).then_inc(S["act_vx"], 1)
                    act.wait_ge(S["pe_pv"], n - 3)
                    act.activation(vl[k % 4][:, :, 0:E],
                                   PA[:, 2 * D:2 * D + LW].rearrange("p (h e) -> p h e", h=LH), ACT.Copy)\
                       .then_inc(S["act_vl"], 1)
                if on_(3):
                    act.wait_ge(S["pe_ct"], n_(b, k - 3))
                if on_(1):
                    j = k - 1
                    act.wait_ge(S["pe_qft"], n_(b, j))
                    act.wait_ge(S["pe_cx"], n2(b, j - 2, 1))
                    act.activation(qft[j % 2][:, :], QF, ACT.Copy).then_inc(S["act_qfe"], 1)
                if on_(3):
                    act.wait_ge(S["pe_out"], n_(b, k - 3) - 1)
                    act.activation(oct_[:, :], CT, ACT.Copy).then_inc(S["act_cte"], 1)
                if on_(2):
                    j = k - 2
                    act.wait_ge(S["pe_pt"], n_(b, j))
                    act.wait_ge(S["pe_pv"], n_(b, j) - 1)
                    act.activation(pt[:, :], PTB, ACT.Copy).then_inc(S["act_pte"], 1)
                if on_(0):
                    act.wait_ge(S["act_qk"], n)
                    act.wait_ge(S["dve_kf"], n - 2)
                    act.activation(ke[i][:, :], qk[i][:, D + LW:2 * D], ACT.Exp).then_inc(S["act_ke"], 1)
                    act.wait_ge(S["pool_qd"], n)
                    act.wait_ge(S["pool_qf"], n - 2)
                    act.activation(qe[i][:, :], qd[i][:, :], ACT.Exp).then_inc(S["act_qe"], 1)
                if on_(1):
                    j = k - 1
                    act.wait_ge(S["dve_sm"], n_(b, j))
                    act.wait_ge(S["pe_pt"], n_(b, j) - 2)
                    act.activation(pr[j % 2][:, :, :], sm[:, :, :], ACT.Exp, scale=float(E) ** -0.5)\
                       .then_inc(S["act_ex"], 1)

            credit(act, ["act_" + n for n in act_sems])
            act.wait_ge(zeroed, 2)
            tiles(act, slot)

        @block.vector
        def _(dve):
            def heads(x, n=GH):
                return x.rearrange("p (h e) -> p h e", h=n)

            def slot(b, k, on_):
                if on_(0):
                    n = n_(b, k)
                    i = k % 2
                    dve.wait_ge(S["act_qk"], n)
                    dve.wait_ge(S["pool_qd"], n - 2)
                    dve.tensor_reduce(qm[i][:, :], heads(qk[i][:, LW:D]), AX.X, ALU.max).then_inc(S["dve_qm"], 1)
                def context(j, i):
                    nb = n2(b, j, i)
                    dve.wait_ge(S["pe_cx"], nb)
                    dve.wait_ge(S["dve_cn"], nb - 1)
                    dve.tensor_tensor(cx[:, :], CX, cx[:, :], ALU.add).then_inc(S["dve_cxa"], 1)
                    dve.wait_ge(S["dve_cxa"], nb)
                    dve.tensor_scalar(cd[:, :], cx[:, GW:GW + 1], 1e-6, None, ALU.add).then_inc(S["dve_cda"], 1)
                    dve.wait_ge(S["dve_cda"], nb)
                    dve.reciprocal(cr[:, :], cd[:, :]).then_inc(S["dve_cra"], 1)
                    dve.wait_ge(S["dve_cra"], nb)
                    dve.scalar_tensor_tensor(out=cn[(i + 1) % 2][:, :], in0=cx[:, 0:GW], scalar=cr[:, 0:1],
                                             in1=bmask[:, :], op0=ALU.mult, op1=ALU.mult).then_inc(S["dve_cn"], 1)

                if on_(1):
                    j = k - 1
                    context(j, 0)
                    n = n_(b, j)
                    dve.wait_ge(S["pe_sc"], n)
                    dve.tensor_reduce(mx[:, :], SCO, AX.X, ALU.max).then_inc(S["dve_mx"], 1)
                    dve.wait_ge(S["dve_mx"], n)
                    dve.wait_ge(S["act_ex"], n - 1)
                    dve.tensor_tensor(sm[:, :, :], SCO, mx[:, :].unsqueeze(2).to_broadcast([P, LH, 2 * P]),
                                      ALU.subtract).then_inc(S["dve_sm"], 1)
                if on_(0):
                    n = n_(b, k)
                    i = k % 2
                    dve.wait_ge(S["act_qe"], n)
                    dve.tensor_reduce(qs[i][:, :], heads(qe[i][:, :]), AX.X, ALU.add).then_inc(S["dve_qs"], 1)
                    dve.wait_ge(S["dve_qs"], n)
                    dve.wait_ge(S["pool_qf"], n - 2)
                    dve.reciprocal(qi[i][:, :], qs[i][:, :]).then_inc(S["dve_qi"], 1)
                    dve.wait_ge(S["act_ke"], n)
                    dve.wait_ge(S["pool_kp"], n)
                    dve.wait_ge(S["pe_cx"], n2(b, k - 2, 1))
                    dve.scalar_tensor_tensor(out=kf[i][:, :], in0=ke[i][:, :], scalar=1.0, in1=kp[i][:, :],
                                             op0=ALU.min, op1=ALU.add).then_inc(S["dve_kf"], 1)
                if on_(3):
                    dve.wait_ge(S["pe_out"], n_(b, k - 3))
                if on_(2):
                    dve.wait_ge(S["pe_pv"], n_(b, k - 2))
                if on_(1):
                    j = k - 1
                    dve.wait_ge(S["pe_cx"], n2(b, j, 1))
                    dve.wait_ge(S["pe_ct"], n_(b, j) - 4)
                    dve.tensor_copy(oc[j % 4][:, LW:D], OG).then_inc(S["dve_og"], 1)
                if on_(2):
                    j = k - 2
                    n = n_(b, j)
                    dve.reciprocal(oi[:, :], OL[:, :, E]).then_inc(S["dve_oi"], 1)
                    dve.wait_ge(S["dve_oi"], n)
                    dve.tensor_tensor(heads(oc[j % 4][:, 0:LW], LH), OL[:, :, 0:E],
                                      oi[:, :].unsqueeze(2).to_broadcast([P, LH, E]), ALU.mult)\
                       .then_inc(S["dve_ol"], 1)
                if on_(3):
                    j = k - 3
                    cols = bass.ds(b * (TB * P) + j * P, P)
                    dve.scalar_tensor_tensor(out=XT[:, cols], in0=CT, scalar=m["a_bo"][:, 0:1], in1=XT[:, cols],
                                             op0=ALU.add, op1=ALU.add).then_inc(S["dve_xt"], 1)
                if on_(1):
                    context(k - 1, 1)

            credit(dve, ["dve_" + n for n in dve_sems])
            dve.wait_ge(m["loaded_a"], 64)
            dve.tensor_copy(mask[:, :, :], maskf[:, :, :]).then_inc(prepared, 1)
            dve.memset(cx[:, :], 0.0).then_inc(prepared, 1)
            dve.memset(cn[0][:, :], 0.0).then_inc(prepared, 1)
            dve.wait_ge(prepared, 3)
            dve.wait_ge(zeroed, 2)
            tiles(dve, slot)

        @block.gpsimd
        def _(pool):
            def heads(x):
                return x.rearrange("p (h e) -> p h e", h=GH)

            def slot(b, k, on_):
                n = n_(b, k)
                i = k % 2
                if on_(0):
                    pool.wait_ge(S["pe_proj"], n - 2)
                    pool.tensor_tensor(xs[i][:, :], XN[:, bass.ds(b * (TB * P) + k * P, P)],
                                       ones[:, 0:1].to_broadcast([P, P]), ALU.mult).then_inc(S["pool_xs"], 1)
                if on_(1):
                    j = k - 1
                    pool.wait_ge(S["dve_qi"], n - 1)
                    pool.wait_ge(S["act_qe"], n - 1)
                    pool.wait_ge(S["pe_qft"], n - 3)
                    pool.tensor_tensor(heads(qf[j % 2][:, :]), heads(qe[j % 2][:, :]),
                                       qi[j % 2][:, :].unsqueeze(2).to_broadcast([P, GH, E]), ALU.mult)\
                        .then_inc(S["pool_qf"], 1)
                if on_(0):
                    pool.wait_ge(S["act_qk"], n)
                    pool.wait_ge(S["dve_qm"], n)
                    pool.wait_ge(S["act_qe"], n - 2)
                    pool.wait_ge(S["dve_kf"], n - 2)
                    pool.tensor_tensor(heads(qd[i][:, :]), heads(qk[i][:, LW:D]),
                                       qm[i][:, :].unsqueeze(2).to_broadcast([P, GH, E]), ALU.subtract)\
                        .then_inc(S["pool_qd"], 1)
                    pool.tensor_scalar(kp[i][:, :], qk[i][:, D + LW:2 * D], 0.0, None, ALU.max)\
                        .then_inc(S["pool_kp"], 1)

            credit(pool, ["pool_" + n for n in pool_sems])
            pool.memset(ones[:, :], 1.0)
            pool.memset(wq_z[:, :, :], 0.0)
            pool.memset(kt[3][:, :], 0.0)
            for v in vx:
                pool.memset(v[:, :], 1.0)
            for v in vl:
                last = pool.memset(v[:, :, :], 1.0)
            last.then_inc(zeroed, 1)
            pool.wait_ge(zeroed, 1)
            pool.wait_ge(m["loaded_a"], 64)
            for h in range(LH):
                last = pool.tensor_copy(wq_z[:, h, h * E:(h + 1) * E], m["a_w"][:, h * E:(h + 1) * E])
            last.then_inc(zeroed, 1)
            pool.wait_ge(zeroed, 2)
            tiles(pool, slot)


def stage_layers(nc, a, m):
    PS, X0, X1 = m["PS"], m["X0"], m["X1"]
    wqkv, wo, w1, w2, par, qks, xpos, rot, kshift, maskf = (
        m[n] for n in ("wqkv", "wo", "w1", "w2", "par", "qks", "xpos", "rot", "kshift", "maskf"))
    loaded_tab, loaded_qkv, loaded_wo, loaded_mlp = (
        m[n] for n in ("loaded_tab", "loaded_qkv", "loaded_wo", "loaded_mlp"))
    w_hi, w_lo, w_cut = m["w_hi"], m["w_lo"], m["w_cut"]
    w_cut_ready, w_hi_ready, w_lo_ready = m["w_cut_ready"], m["w_hi_ready"], m["w_lo_ready"]
    QK = [PS[:, 0, :], PS[:, 1, :]]
    VB = PS[:, 2, :]
    TR = PS[:, 3, :]
    PO = PS[:, 4, :]
    SO = PS[:, 5:7, :]
    SC, OC, OE = 0, 2 * 2 * WIN, DH + 1
    AC = PS[:, 7, 0:P]
    LN = BANK - P
    MU, VA, RB = PS[:, 5, LN:BANK], PS[:, 6, LN:LN + 1], PS[:, 5, LN:BANK]
    MU_E, VA_E, RB_E = PS[:, 7, LN:BANK], PS[:, 7, LN:LN + 1], PS[:, 7, LN:BANK]

    with ExitStack() as ctx:
        def sb(name, shape, dt=F32):
            return ctx.enter_context(nc.sbuf_tensor(name, shape, dt))

        def sem(name):
            return ctx.enter_context(nc.semaphore(name))

        mask = sb("mask", [P, 2, P], BF16)
        half_c = sb("half_c", [P, 8])
        ones = sb("ones", [P, 1])
        x_hi = [sb(f"x_hi{i}", [P, P], F32R) for i in range(2)]
        x_lo = [sb(f"x_lo{i}", [P, P], F32R) for i in range(2)]
        x_cut = sb("x_cut", [P, P], I32)
        xs = [sb(f"xs{i}", [P, WIN + P]) for i in range(2)]
        lay4 = sb("lay4", [P, 4 * DH])
        tab = [sb(f"tab{i}", [P, 4, DH]) for i in range(2)]
        sq = [sb(f"sq{i}", [P, BANK]) for i in range(2)]
        ss = [sb(f"ss{i}", [P, 8]) for i in range(2)]
        sg = [sb(f"sg{i}", [P, 8]) for i in range(2)]
        rn = [sb(f"rn{i}", [P, 8]) for i in range(2)]
        qn = [sb(f"qn{i}", [P, BANK]) for i in range(2)]
        cm = [sb(f"cm{i}", [P, BANK]) for i in range(2)]
        rs = [sb(f"rs{i}", [P, BANK]) for i in range(2)]
        qr = [sb(f"qr{i}", [P, BANK]) for i in range(2)]
        qkt = [sb(f"qkt{i}", [P, 4, WIN + P]) for i in range(UT)]
        vs = [sb(f"vs{i}", [P, 4, 2, DH + 1]) for i in range(4)]
        mx = [sb(f"mx{i}", [P, 2, 2]) for i in range(2)]
        sm = [sb(f"sm{i}", [P, 2, 2, DH]) for i in range(2)]
        pr = [sb(f"pr{i}", [P, 2, P]) for i in range(2)]
        po = [sb(f"po{i}", [P, BANK]) for i in range(2)]
        ri = [sb(f"ri{i}", [P, 2, 2]) for i in range(2)]
        on = [sb(f"on{i}", [P, 2, 2, DH]) for i in range(2)]
        xc = sb("xc", [P, T])
        sqt = sb("sqt", [P, P])
        ve = sb("ve", [P, 1])
        rl = sb("rl", [P, 1])
        gl = [sb(f"gl{i}", [P, GT]) for i in range(2)]
        hb = [[sb(f"hb{i}_{c}", [P, GT]) for c in range(len(FCH))] for i in range(2)]

        wsum = sb("wsum", [P, 2 * FC])
        wsc = sb("wsc", [P, 2 * FC])
        wsr = sb("wsr", [P, 2 * FC])
        ptot = sb("ptot", [P, 1])
        wfin = m["l_wfin"]
        scale_step, scale_ready, tern_step = sem("scale_step"), sem("scale_ready"), sem("tern_step")
        ready = sem("ready")
        unit_sems = {n: sem("u_" + n) for n in (
            "qk_done", "v_done", "tr_done", "pv_done", "s_done", "wo_done", "po_done",
            "sq_ready", "v_ready", "qkt_ready", "po_ready", "p_ready",
            "ss_ready", "qn_ready", "cm_ready", "qr_ready", "ri_ready", "on_ready", "mx_ready", "sm_ready",
            "kp_ready", "sg_ready", "rn_ready", "rs_ready")}
        S = unit_sems
        x_cut_ready, x_hi_ready, x_lo_ready = (sem(n) for n in ("x_cut_ready", "x_hi_ready", "x_lo_ready"))
        x_staged, tab_ready, lay_ready, x1_ready = (sem(n) for n in ("x_staged", "tab_ready", "lay_ready", "x1_ready"))
        mean_done, centred, squared, var_done, var_ready, rstd_ready, spread, scaled, xn_ready = (
            sem(n) for n in ("f_mean_done", "f_centred", "f_squared", "f_var_done", "f_var_ready", "f_rstd_ready",
                             "f_spread", "f_scaled", "f_xn_ready"))
        ha_done, hg_done, gl_ready, h_ready, mo_done, x0_ready = (
            sem(n) for n in ("ha_done", "hg_done", "gl_ready", "h_ready", "mo_done", "x0_ready"))
        block = ctx.enter_context(nc.Block())

        def n_unit(l, b, j):
            return l * UNITS + b * BODY + (CREDIT + j + 1)

        def n_po(l, b, k):
            return l * (UNITS + 1) + b * BODY + (CREDIT + k - 3 + 1)

        def n_tile(l, b, t):
            return l * (NT + 1) + b * 2 + (t + 1)

        def n_x1(l, b, t):
            return l * (2 * NT) + b * 4 + 2 * (t + 1)

        def n_ln(l, b, k):
            return l * NT + b * 2 + (CREDIT + k // UT - 1)

        def layer_slots(eng, slot, l, after=None):
            for b in range(2):
                for k in range(BODY):
                    if (b, k) != (0, 0):
                        slot(l, b, k, lambda lag, s=b * BODY + k: s >= lag)
            with eng.Fori(2, UNITS // BODY) as b:
                for k in range(BODY):
                    slot(l, b, k, lambda lag: True)
            for k in range(LAG):
                slot(l, UNITS // BODY, k, lambda lag, k=k: k < lag)
                if after is not None:
                    after(k)

        def first_slot(slot, l):
            slot(l, 0, 0, lambda lag: lag == 0)

        @block.sync
        def _(sp):
            def load_qkv(l):
                sp.dma_start(wqkv[:, :], a["L0_ffn_Wqkv"][bass.ds(l, 1), :, :].rearrange("o p n -> p (o n)"))\
                  .then_inc(loaded_qkv, 16)

            def load_wo(l):
                sp.dma_start(flat(wo[:, :, :]), a["l_wo"][bass.ds(l, 1), :, :].rearrange("o p n -> p (o n)"))\
                  .then_inc(loaded_wo, 16)

            def load_mlp(l):
                sp.dma_start(w1[:, :], a["L0_ffn_W1"][bass.ds(l, 1), :, :].rearrange("o p n -> p (o n)"))\
                  .then_inc(loaded_mlp, 16)
                sp.dma_start(flat(w2[:, :, :]), a["l_w2"][bass.ds(l, 1), :, :].rearrange("o p n -> p (o n)"))\
                  .then_inc(loaded_mlp, 16)
                sp.dma_start(par[:, :], a["l_par"][bass.ds(l, 1), :, :].rearrange("o p n -> p (o n)"))\
                  .then_inc(loaded_mlp, 16)

            with sp.Fori(0, DEPTH - 1) as l:
                sp.wait_ge(S["v_done"], n_unit(l, 0, UNITS - 1))
                load_qkv(l + 1)
                sp.wait_ge(S["wo_done"], n_unit(l, 0, UNITS - 1))
                load_wo(l + 1)
                sp.wait_ge(x0_ready, l * (2 * NG) + 2 * NG + CREDIT)
                load_mlp(l + 1)

        @block.tensor
        def _(pe):
            def mean(out_, cols):
                pe.matmul(out_, m["mean_w"][:, :], X1[:, cols], start=True, stop=True).then_inc(mean_done, 1)

            def variance(out_):
                pe.matmul(out_, sqt[:, :], m["mean_w"][:, 0:1], start=True, stop=True).then_inc(var_done, 1)

            def spread_out(out_):
                pe.matmul(out_, rl[:, 0:1].to_broadcast([P, P]), m["ident"][:, :], start=True, stop=True)\
                  .then_inc(spread, 1)

            def slot(l, b, k, on_):
                if on_(0):
                    g, par_ = k % UT, (k // UT) % 2
                    if g == 0:
                        pe.wait_ge(x_staged, n_tile(l, b, k // UT))
                        pe.wait_ge(x_hi_ready, n_tile(l, b, k // UT) + CREDIT)
                        pe.wait_ge(x_lo_ready, n_tile(l, b, k // UT) + CREDIT)
                    pe.wait_ge(S["qn_ready"], n_unit(l, b, k) - 2)

                    def heads_of(w):
                        return w[:, :].rearrange("p (s n) -> p s n", s=2)[:, :, g * 256:(g + 1) * 256]

                    pe.matmul(QK[k % 2], x_hi[par_][:, :], heads_of(w_hi), start=True, stop=False)
                    pe.matmul(QK[k % 2], x_hi[par_][:, :], heads_of(w_lo), start=False, stop=False)
                    pe.matmul(QK[k % 2], x_lo[par_][:, :], heads_of(w_hi), start=False, stop=True)\
                      .then_inc(S["qk_done"], 1)
                def values(windows):
                    g, par_ = k % UT, (k // UT) % 2
                    wv = wqkv[:, 2 * INNER + g * 256:2 * INNER + (g + 1) * 256].rearrange(
                        "p (r h e) -> p h r e", r=2, h=2)
                    for w in windows:
                        for h in range(2):
                            last = pe.matmul(VB[64 * h:64 * h + 64, w * P:(w + 1) * P],
                                             xs[par_][:, WIN * w:WIN * w + 2 * WIN], wv[:, h, :, :],
                                             start=True, stop=True)
                    return last

                if on_(0):
                    pe.wait_ge(S["v_ready"], n_unit(l, b, k) - 1)
                    values((0, 1, 2))
                if on_(3) or on_(4):
                    pe.wait_ge(S["po_ready"], n_po(l, b, k) - 1)
                    last = None
                    if on_(3):
                        j = k - 3
                        pe.wait_ge(S["p_ready"], n_unit(l, b, j))
                        for p in range(2):
                            last = pe.transpose(PO[:, p * P:(p + 1) * P], pr[j % 2][:, p, :], m["ident"][:, :])
                    if on_(4):
                        j = k - 4
                        pe.wait_ge(S["on_ready"], n_unit(l, b, j))
                        for p in range(2):
                            last = pe.transpose(PO[:, (2 + p) * P:(3 + p) * P],
                                                on[j % 2][:, p, :, :].rearrange("p a b -> p (a b)"), m["ident"][:, :])
                    last.then_inc(S["po_done"], 1)
                if on_(5):
                    j = k - 5
                    g = j % UT
                    if g == 0:
                        pe.wait_ge(x1_ready, n_x1(l, b, j // UT) - 2 + CREDIT)
                    pe.wait_ge(S["po_ready"], n_po(l, b, k) - 1)
                    for p in range(2):
                        last = pe.matmul(AC, wo[:, 2 * g + p, :], po[(k - 1) % 2][:, (2 + p) * P:(3 + p) * P],
                                         start=(g == 0 and p == 0), stop=(g == UT - 1 and p == 1))
                    last.then_inc(S["wo_done"], 1)
                if on_(2):
                    j = k - 2
                    pe.wait_ge(S["qr_ready"], n_unit(l, b, j))
                    pe.wait_ge(S["qkt_ready"], n_unit(l, b, j) - 1)
                    for p in range(4):
                        last = pe.transpose(TR[:, p * P:(p + 1) * P], qr[j % 2][:, p * P:(p + 1) * P], m["ident"][:, :])
                    last.then_inc(S["tr_done"], 1)
                if on_(4):
                    pe.wait_ge(S["on_ready"], n_unit(l, b, k - 4))
                if on_(3):
                    pe.wait_ge(S["sm_ready"], n_unit(l, b, k - 3))
                    pe.wait_ge(S["v_ready"], n_unit(l, b, k - 3))
                    pe.wait_ge(S["po_ready"], n_po(l, b, k))
                first_tile = isinstance(b, int) and b == 0 and k - 2 < UT

                def open_with_mask():
                    for h in range(2):
                        pe.matmul(SO[:, h, SC:SC + P], m["ident_bf"][:, :], mask[:, 0 if first_tile else 1, :],
                                  start=True, stop=False, skip_group_check=True)

                if on_(0):
                    values((3,)).then_inc(S["v_done"], 1)
                elif on_(3):
                    open_with_mask()
                if k % UT == 1 and on_(6):
                    pe.wait_ge(x1_ready, n_x1(l, b, k // UT - 2) + CREDIT)
                    mean(MU, bass.ds(b * (2 * P) + (k // UT - 2) * P + PAD, P))
                if k % UT == 2 and on_(7):
                    pe.wait_ge(squared, n_ln(l, b, k))
                    variance(VA)
                if k % UT == 3 and on_(8):
                    pe.wait_ge(rstd_ready, n_ln(l, b, k))
                    spread_out(RB)
                if on_(3):
                    j = k - 3
                    for p in range(2):
                        for w in range(4):
                            for h in range(2):
                                rows = slice(64 * h, 64 * h + 64)
                                last = pe.matmul(SO[WIN * w:WIN * w + WIN, h, OC + p * OE:OC + (p + 1) * OE],
                                                 po[k % 2][rows, p * P + WIN * w:p * P + WIN * w + WIN],
                                                 vs[j % 4][rows, w, p, :], start=True, stop=True,
                                                 skip_group_check=True)
                    last.then_inc(S["pv_done"], 1)
                if on_(2):
                    pe.wait_ge(S["qkt_ready"], n_unit(l, b, k - 2))
                    pe.wait_ge(S["kp_ready"], n_unit(l, b, k - 2))
                    open_with_mask()
                if on_(2):
                    j = k - 2
                    g = j % UT
                    for p in range(2):
                        for w in range(4):
                            for h in range(2):
                                rows = slice(64 * h, 64 * h + 64)
                                last = pe.matmul(SO[WIN * w:WIN * w + WIN, h, SC + p * 64:SC + (p + 1) * 64],
                                                 qkt[g][rows, p, WIN + WIN * w:2 * WIN + WIN * w],
                                                 qkt[g][rows, 2 + p, WIN * w:WIN * w + 2 * WIN],
                                                 start=False, stop=True, skip_group_check=True)
                    last.then_inc(S["s_done"], 1)

            def hidden(l, g, c):
                o, n = FCH[c]
                if c == 0:
                    pe.wait_ge(xn_ready, l * NT + (4 * g + 4 + CREDIT))
                if g > 0:
                    pe.wait_ge(h_ready, l * (NG * 3) + (g - 1) * 3 + c + 1)
                x = xc[:, g * GT:(g + 1) * GT]
                pe.matmul(PS[0:n, 2 * c + 1, :], w1[:, FF + o:FF + o + n], x, start=True, stop=True)\
                  .then_inc(hg_done, 1)
                pe.matmul(PS[0:n, 2 * c, :], w1[:, o:o + n], x, start=True, stop=True).then_inc(ha_done, 1)

            def outp(l, g):
                pe.wait_ge(h_ready, l * (NG * 3) + g * 3 + 3)
                if g == 1:
                    pe.wait_ge(scaled, l * NT + (NT + CREDIT))
                if g >= 2:
                    pe.wait_ge(x0_ready, l * (2 * NG) + 2 * (g - 1) + CREDIT)
                for c, (o, n) in enumerate(FCH):
                    last = pe.matmul(PS[:, 6 + g % 2, :], w2[0:n, c, :], hb[g % 2][c][0:n, :],
                                     start=(c == 0), stop=(c == len(FCH) - 1))
                last.then_inc(mo_done, 1)

            def early(l, k):
                if k == 2:
                    pe.wait_ge(loaded_mlp, l * 48 + 48)
                    pe.wait_ge(S["sq_ready"], n_unit(l, 0, UNITS - 1))
                    pe.wait_ge(S["qn_ready"], n_unit(l, 0, UNITS - 1))
                    hidden(l, 0, 0)
                if k == 3:
                    pe.wait_ge(S["v_ready"], n_unit(l, 0, UNITS - 1))
                    pe.wait_ge(S["qkt_ready"], n_unit(l, 0, UNITS - 1))
                    hidden(l, 0, 1)

            def start(l):
                pe.wait_ge(loaded_qkv, l * 16 + 16)
                pe.wait_ge(w_hi_ready, l * WCH + WCH)
                pe.wait_ge(w_lo_ready, l * WCH + WCH)
                first_slot(slot, l)

            def mlp(l, more):
                pe.wait_ge(x1_ready, n_x1(l, 0, NT - 1) + CREDIT)
                mean(MU_E, slice(PAD + (NT - 1) * P, PAD + NT * P))
                pe.wait_ge(S["po_ready"], n_po(l, 0, UNITS + 3))
                pe.wait_ge(scaled, l * NT + (NT - 1 + CREDIT))
                hidden(l, 0, 2)
                pe.wait_ge(squared, l * NT + (NT + CREDIT))
                variance(VA_E)
                hidden(l, 1, 0)
                pe.wait_ge(rstd_ready, l * NT + (NT + CREDIT))
                spread_out(RB_E)
                outp(l, 0)
                for g in range(1, NG):
                    for c in range(len(FCH)):
                        if (g, c) != (1, 0):
                            hidden(l, g, c)
                        if c == 0 and g > 1:
                            outp(l, g - 1)
                if more:
                    pe.wait_ge(h_ready, l * (NG * 3) + (NG * 3 - 1))
                    start(l + 1)
                outp(l, NG - 1)

            for s in (S["qk_done"], S["v_done"], S["tr_done"], S["pv_done"], S["s_done"], S["wo_done"], S["po_done"],
                      mean_done, var_done, spread):
                pe.sem_inc(s, CREDIT)
            pe.wait_ge(ready, 3)

            def layer(l, more):
                pe.wait_ge(loaded_wo, l * 16 + 16)
                layer_slots(pe, slot, l, lambda k: early(l, k))
                mlp(l, more)

            start(0)
            with pe.Fori(0, DEPTH - 1) as l:
                layer(l, True)
            layer(DEPTH - 1, False)

        @block.scalar
        def _(act):
            def squares(n, cols):
                act.wait_ge(centred, n)
                act.wait_ge(var_done, n - 1)
                act.activation(sqt[:, :], xc[:, cols], ACT.Square).then_inc(squared, 1)

            def slot(l, b, k, on_):
                if on_(3):
                    j = k - 3
                    act.wait_ge(S["sm_ready"], n_unit(l, b, j))
                    act.wait_ge(S["po_done"], n_po(l, b, k) - 2)
                    act.activation(pr[j % 2][:, :, :].rearrange("p a b -> p (a b)"),
                                   sm[j % 2][:, :, :, :].rearrange("p a b c -> p (a b c)"), ACT.Exp)\
                       .then_inc(S["p_ready"], 1)
                if k % UT == 2 and on_(7):
                    squares(n_ln(l, b, k), bass.ds(b * (2 * P) + (k // UT - 2) * P, P))
                if on_(0):
                    act.wait_ge(S["qk_done"], n_unit(l, b, k))
                    act.wait_ge(S["ss_ready"], n_unit(l, b, k) - 2)
                    act.activation(sq[k % 2][:, :], QK[k % 2], ACT.Square).then_inc(S["sq_ready"], 1)
                if on_(3) or on_(4):
                    act.wait_ge(S["po_done"], n_po(l, b, k))
                    lo, hi = (0 if on_(3) else 2 * P), (4 * P if on_(4) else 2 * P)
                    if on_(3):
                        act.wait_ge(S["pv_done"], n_unit(l, b, k - 3) - 2)
                    if on_(4):
                        act.wait_ge(S["wo_done"], n_unit(l, b, k - 4) - 2)
                    act.activation(po[k % 2][:, lo:hi], PO[:, lo:hi], ACT.Copy).then_inc(S["po_ready"], 1)
                if on_(2):
                    j = k - 2
                    act.wait_ge(S["tr_done"], n_unit(l, b, j))
                    act.wait_ge(S["kp_ready"], n_unit(l, b, j))
                    act.activation(qkt[j % UT][:, :, WIN:WIN + P], TR.rearrange("p (a b) -> p a b", a=4), ACT.Copy)\
                       .then_inc(S["qkt_ready"], 1)
                if on_(0):
                    act.wait_ge(S["v_done"], n_unit(l, b, k))
                    act.wait_ge(S["pv_done"], n_unit(l, b, k) - 4)
                    act.activation(vs[k % 4][:, :, :, 0:DH], VB.rearrange("p (w r e) -> p w r e", w=4, r=2),
                                   ACT.Copy).then_inc(S["v_ready"], 1)
                    if k % UT == 3:
                        upper_x(l, b, k // UT + 1)

            def upper_x(l, b, t):
                act.wait_ge(x_cut_ready, n_tile(l, b, t) + CREDIT)
                act.wait_ge(S["qk_done"], n_unit(l, b, (t - 1) * UT - 1))
                act.activation(x_hi[t % 2][:, :], x_cut[:, :].bitcast(F32), ACT.Copy).then_inc(x_hi_ready, 1)

            def upper_w(l, c):
                act.wait_ge(w_cut_ready, l * WCH + (c + 1))
                act.wait_ge(S["qk_done"], n_unit(l, 0, -1))
                act.activation(w_hi[:, c * BANK:(c + 1) * BANK], w_cut[c % 2][:, :].bitcast(F32), ACT.Copy)\
                   .then_inc(w_hi_ready, 1)

            def mlp(l, more):
                for g in range(NG):
                    for c, (o, n) in enumerate(FCH):
                        i = 3 * g + c
                        act.wait_ge(hg_done, l * (NG * 3) + (i + 1))
                        act.wait_ge(h_ready, l * (NG * 3) + (i + 1 - 2)) if i >= 2 else None
                        act.activation(gl[i % 2][0:n, :], PS[0:n, 2 * c + 1, :], ACT.Gelu,
                                       bias=par[0:n, 3 + 3 + c:3 + 3 + c + 1]).then_inc(gl_ready, 1)
                        if i == 0:
                            squares(l * NT + (NT + CREDIT), slice((NT - 1) * P, NT * P))
                        if more and i in (4, 6, 8, 10):
                            upper_w(l + 1, i // 2 - 2)
                        if more and i == 9:
                            upper_x(l + 1, 0, 0)
                if more:
                    first_slot(slot, l + 1)

            for s in (S["sq_ready"], S["v_ready"], S["qkt_ready"], S["po_ready"], S["p_ready"], squared,
                      x_hi_ready):
                act.sem_inc(s, CREDIT)
            act.wait_ge(ready, 3)

            def layer(l, more):
                layer_slots(act, slot, l)
                act.wait_ge(loaded_mlp, l * 48 + 48)
                mlp(l, more)

            upper_x(0, 0, 0)
            first_slot(slot, 0)
            with act.Fori(0, DEPTH - 1) as l:
                layer(l, True)
            layer(DEPTH - 1, False)

        @block.vector
        def _(dve):
            for s in (S["ss_ready"], S["sg_ready"], S["qn_ready"], S["cm_ready"], S["qr_ready"], S["ri_ready"], S["on_ready"],
                      S["mx_ready"], S["sm_ready"], x1_ready, x0_ready, centred, var_ready, scaled, xn_ready,
                      x_cut_ready, x_lo_ready):
                dve.sem_inc(s, CREDIT)
            dve.wait_ge(loaded_tab, 80)
            dve.memset(half_c[:, :], -0.5).then_inc(ready, 1)
            dve.memset(ones[:, :], 1.0).then_inc(ready, 1)
            dve.tensor_copy(mask[:, :, :], maskf[:, :, :]).then_inc(ready, 1)

            def heads(x):
                return x.rearrange("p (h e) -> p h e", e=DH)

            def halve_x(l, b, t):
                n = n_tile(l, b, t)
                x = xs[t % 2][:, WIN:WIN + P]
                dve.wait_ge(x_staged, n)
                dve.wait_ge(x_hi_ready, n - 1 + CREDIT)
                dve.tensor_scalar(x_cut[:, :], x.bitcast(I32), HI_BITS, None, ALU.bitwise_and).then_inc(x_cut_ready, 1)
                dve.wait_ge(x_cut_ready, n + CREDIT)
                dve.wait_ge(S["qk_done"], n_unit(l, b, (t - 1) * UT - 1))
                dve.tensor_tensor(x_lo[t % 2][:, :], x, x_cut[:, :].bitcast(F32), ALU.subtract).then_inc(x_lo_ready, 1)

            def halve_w(l, c):
                n = l * WCH + (c + 1)
                w = wqkv[:, c * BANK:(c + 1) * BANK]
                dve.wait_ge(loaded_qkv, l * 16 + 16)
                dve.wait_ge(w_hi_ready, n - 2)
                dve.tensor_scalar(w_cut[c % 2][:, :], w.bitcast(I32), HI_BITS, None, ALU.bitwise_and)\
                   .then_inc(w_cut_ready, 1)
                dve.wait_ge(w_cut_ready, n)
                dve.wait_ge(S["qk_done"], n_unit(l, 0, -1))
                dve.tensor_tensor(w_lo[:, c * BANK:(c + 1) * BANK], w, w_cut[c % 2][:, :].bitcast(F32), ALU.subtract)\
                   .then_inc(w_lo_ready, 1)

            def centre(mu, n, c0):
                dve.wait_ge(mean_done, n)
                static = isinstance(c0, int)
                dve.tensor_tensor(xc[:, slice(c0, c0 + P) if static else bass.ds(c0, P)],
                                  X1[:, slice(PAD + c0, PAD + c0 + P) if static else bass.ds(c0 + PAD, P)],
                                  mu, ALU.subtract).then_inc(centred, 1)

            def variance(va, n):
                dve.wait_ge(var_done, n)
                dve.wait_ge(rstd_ready, n - 1)
                dve.tensor_scalar(ve[:, :], va, LN_EPS, None, ALU.add).then_inc(var_ready, 1)

            def scale(rb, n, cols):
                dve.wait_ge(spread, n)
                dve.wait_ge(squared, n)
                dve.tensor_tensor(xc[:, cols], xc[:, cols], rb, ALU.mult).then_inc(scaled, 1)

            def affine(l, n, cols):
                dve.wait_ge(loaded_mlp, l * 48 + 48)
                dve.wait_ge(scaled, n)
                dve.tensor_scalar(xc[:, cols], xc[:, cols], par[:, 0:1], par[:, 1:2], ALU.mult, ALU.add)\
                   .then_inc(xn_ready, 1)

            def slot(l, b, k, on_):
                sc = SO[:, :, SC:SC + P].rearrange("p h (r e) -> p h r e", r=2)
                o = SO[:, :, OC:OC + 2 * OE].rearrange("p h (r e) -> p h r e", e=OE)
                if on_(3):
                    j = k - 3
                    dve.wait_ge(S["s_done"], n_unit(l, b, j))
                    dve.tensor_reduce(mx[j % 2][:, :, :], sc, AX.X, ALU.max).then_inc(S["mx_ready"], 1)
                if on_(4):
                    j = k - 4
                    dve.wait_ge(S["pv_done"], n_unit(l, b, j))
                    dve.reciprocal(ri[j % 2][:, :, :], o[:, :, :, DH]).then_inc(S["ri_ready"], 1)
                if on_(3):
                    j = k - 3
                    dve.wait_ge(S["mx_ready"], n_unit(l, b, j))
                    dve.wait_ge(S["p_ready"], n_unit(l, b, j) - 2)
                    dve.tensor_tensor(sm[j % 2][:, :, :, :].rearrange("p r h e -> p h r e"), sc,
                                      mx[j % 2][:, :, :].unsqueeze(3).to_broadcast([P, 2, 2, DH]), ALU.subtract)\
                       .then_inc(S["sm_ready"], 1)
                if k % UT == 2 and on_(7):
                    centre(MU, n_ln(l, b, k), b * (2 * P) + (k // UT - 2) * P)
                if k % UT == 3 and on_(8):
                    variance(VA, n_ln(l, b, k))
                if k % UT == 0 and on_(9):
                    scale(RB, n_ln(l, b, k) - 1, bass.ds(b * (2 * P) + (k // UT - 3) * P, P))
                if on_(4):
                    j = k - 4
                    dve.wait_ge(S["ri_ready"], n_unit(l, b, j))
                    dve.wait_ge(S["po_done"], n_po(l, b, k) - 2)
                    dve.tensor_tensor(on[j % 2][:, :, :, :].rearrange("p r h e -> p h r e"), o[:, :, :, 0:DH],
                                      ri[j % 2][:, :, :].unsqueeze(3).to_broadcast([P, 2, 2, DH]), ALU.mult)\
                       .then_inc(S["on_ready"], 1)
                if on_(2):
                    j = k - 2
                    n = n_unit(l, b, j)
                    dve.wait_ge(S["rs_ready"], n)
                    dve.wait_ge(S["cm_ready"], n)
                    dve.wait_ge(S["tr_done"], n - 2)
                    dve.tensor_tensor(qr[j % 2][:, :], cm[j % 2][:, :], rs[j % 2][:, :], ALU.add)\
                       .then_inc(S["qr_ready"], 1)
                if on_(1):
                    j = k - 1
                    n = n_unit(l, b, j)
                    i = j % 2
                    dve.wait_ge(S["rn_ready"], n)
                    dve.wait_ge(S["rs_ready"], n - 2)
                    dve.tensor_tensor(heads(qn[i][:, :]), heads(QK[i]),
                                      rn[i][:, :].unsqueeze(2).to_broadcast([P, 8, DH]), ALU.mult)\
                       .then_inc(S["qn_ready"], 1)
                    dve.wait_ge(S["qn_ready"], n)
                    if j % UT == 0:
                        dve.wait_ge(tab_ready, n_tile(l, b, j // UT))
                    for s in range(2):
                        last = dve.tensor_tensor(
                            heads(cm[i][:, 256 * s:256 * s + 256]), heads(qn[i][:, 256 * s:256 * s + 256]),
                            tab[(j // UT) % 2][:, 2 * s, :].unsqueeze(1).to_broadcast([P, 4, DH]), ALU.mult)
                    last.then_inc(S["cm_ready"], 1)
                if on_(0):
                    n = n_unit(l, b, k)
                    dve.wait_ge(S["sq_ready"], n)
                    dve.tensor_reduce(ss[k % 2][:, :], heads(sq[k % 2][:, :]), AX.X, ALU.add)\
                       .then_inc(S["ss_ready"], 1)
                    dve.wait_ge(S["ss_ready"], n)
                    dve.wait_ge(S["rn_ready"], n - 2)
                    dve.tensor_scalar(sg[k % 2][:, :], ss[k % 2][:, :], 1e-24, None, ALU.max)\
                       .then_inc(S["sg_ready"], 1)
                if k % UT == 2 and on_(0):
                    halve_x(l, b, k // UT + 1)
                if k % UT == 0 and on_(9):
                    affine(l, n_ln(l, b, k) - 1, bass.ds(b * (2 * P) + (k // UT - 3) * P, P))
                if on_(5) and k % UT == 0:
                    j = k - 5
                    dve.wait_ge(S["wo_done"], n_unit(l, b, j))
                    t0 = b * (2 * P) + (j // UT) * P + PAD
                    for h in range(2):
                        r = slice(64 * h, 64 * h + 64)
                        dve.tensor_tensor(X1[r, bass.ds(t0 + h, P)], AC[r, :], X0[r, bass.ds(t0 + h, P)], ALU.add)\
                           .then_inc(x1_ready, 1)

            def ternary_scales():
                step = [0]

                def chain(ins):
                    step[0] += 1
                    ins.then_inc(scale_step, 1)
                    dve.wait_ge(scale_step, step[0])

                dve.wait_ge(m["loaded_l"], 16 * 8)
                lw = m["l_w"]
                chain(dve.scalar_tensor_tensor(out=wfin[:, :, :], in0=lw[:, :, :], scalar=-1.0, in1=lw[:, :, :],
                                               op0=ALU.mult, op1=ALU.max))
                chain(dve.tensor_reduce(wsum[:, :], wfin[:, :, :], AX.X, ALU.add))
                chain(dve.tensor_reduce(ptot[:, :], wsum[:, FC:2 * FC], AX.X, ALU.add))
                chain(dve.tensor_scalar(wsc[:, 0:FC], wsum[:, 0:FC], 1.0 / D, 1e-5, ALU.mult, ALU.max))
                chain(dve.tensor_scalar(wsc[:, FC:2 * FC], ptot[:, 0:1].to_broadcast([P, FC]), 1.0 / FH, 1e-5,
                                        ALU.mult, ALU.max))
                dve.reciprocal(wsr[:, :], wsc[:, :]).then_inc(scale_ready, 1)

            def mlp(l, more):
                last_tile = l * NT + (NT + CREDIT)
                centre(MU_E, last_tile, (NT - 1) * P)
                for g in range(NG):
                    for c, (o, n) in enumerate(FCH):
                        i = 3 * g + c
                        dve.wait_ge(ha_done, l * (NG * 3) + (i + 1))
                        dve.wait_ge(gl_ready, l * (NG * 3) + (i + 1))
                        if g >= 2:
                            dve.wait_ge(mo_done, l * NG + (g - 1))
                        dve.scalar_tensor_tensor(out=hb[g % 2][c][0:n, :], in0=PS[0:n, 2 * c, :],
                                                 scalar=par[0:n, 3 + c:3 + c + 1], in1=gl[i % 2][0:n, :],
                                                 op0=ALU.add, op1=ALU.mult).then_inc(h_ready, 1)
                        if i == 0:
                            variance(VA_E, last_tile)
                        if i == 2:
                            cols = slice((NT - 1) * P, NT * P)
                            scale(RB_E, last_tile, cols)
                            affine(l, last_tile, cols)
                        if c == 0 and g > 0:
                            residual(l, g - 1)
                        if not more and i == 3:
                            ternary_scales()
                        if more and i in (3, 5, 7, 9):
                            halve_w(l + 1, i // 2 - 1)
                        if more and i == 8:
                            halve_x(l + 1, 0, 0)
                if more:
                    first_slot(slot, l + 1)
                residual(l, NG - 1)

            def residual(l, g):
                dve.wait_ge(mo_done, l * NG + (g + 1))
                for h in range(2):
                    r = slice(64 * h, 64 * h + 64)
                    c0 = PAD + h + g * GT
                    dve.scalar_tensor_tensor(out=X0[r, c0:c0 + GT], in0=PS[r, 6 + g % 2, :], scalar=par[r, 2:3],
                                             in1=X1[r, c0:c0 + GT], op0=ALU.add, op1=ALU.add)\
                       .then_inc(x0_ready, 1)

            def layer(l, more):
                layer_slots(dve, slot, l)
                dve.wait_ge(loaded_mlp, l * 48 + 48)
                mlp(l, more)

            halve_x(0, 0, 0)
            first_slot(slot, 0)
            with dve.Fori(0, DEPTH - 1) as l:
                layer(l, True)
            layer(DEPTH - 1, False)

        @block.gpsimd
        def _(pool):
            for s in (S["kp_ready"], S["rn_ready"], S["rs_ready"], rstd_ready):
                pool.sem_inc(s, CREDIT)
            for v in vs:
                pool.memset(v[:, :, :, DH:DH + 1], 1.0)
            for q in qkt:
                last = pool.memset(q[:, 2:4, P:P + WIN], 0.0)
            last.then_inc(lay_ready, 1)
            pool.wait_ge(lay_ready, 1)
            pool.wait_ge(ready, 3)

            def stage(l, b, t):
                if not (isinstance(b, int) and b == 0 and t < 2):
                    pool.wait_ge(S["v_done"], n_unit(l, b, (t - 1) * UT - 1))
                pool.tensor_tensor(xs[t % 2][:, :], X0[:, bass.ds(b * (2 * P) + t * P, WIN + P)],
                                   ones[:, 0:1].to_broadcast([P, WIN + P]), ALU.mult).then_inc(x_staged, 1)

            def table(l, b, t):
                if not (isinstance(b, int) and b == 0 and t < 2):
                    pool.wait_ge(S["cm_ready"], n_unit(l, b, (t - 1) * UT - 1))
                pool.tensor_tensor(
                    tab[t % 2][:, :, :].rearrange("p (s c) e -> p s (c e)", s=2),
                    lay4[:, :].rearrange("p (s n) -> p s n", s=2),
                    rot[:, bass.ds(b * 2 + t, 1), :].to_broadcast([P, 2, 2 * DH]), ALU.mult).then_inc(tab_ready, 1)

            def deviation(n):
                pool.wait_ge(var_ready, n)
                pool.wait_ge(spread, n - 1)
                pool.tensor_tensor(rl[:, :], ve[:, :], half_c[:, 0:1], ALU.pow).then_inc(rstd_ready, 1)

            def slot(l, b, k, on_):
                if k % UT == 3 and on_(8):
                    deviation(n_ln(l, b, k))
                if on_(1):
                    j = k - 1
                    n = n_unit(l, b, j)
                    i = j % 2
                    pool.wait_ge(S["qn_ready"], n)
                    pool.wait_ge(S["qr_ready"], n - 2)
                    pool.wait_ge(tab_ready, n_tile(l, b, j // UT))
                    for s in range(2):
                        for h in range(2):
                            def part(x, hh):
                                return x[:, 256 * s:256 * s + 256].rearrange(
                                    "p (n h e) -> p n h e", n=4, h=2)[:, :, hh, :]
                            last = pool.tensor_tensor(
                                part(rs[i], h), part(qn[i], 1 - h),
                                tab[(j // UT) % 2][:, 2 * s + 1, 32 * h:32 * h + 32].unsqueeze(1)
                                .to_broadcast([P, 4, 32]), ALU.mult)
                    last.then_inc(S["rs_ready"], 1)
                if on_(0):
                    n = n_unit(l, b, k)
                    i = k % 2
                    g = k % UT
                    pool.wait_ge(S["s_done"], n - 4)
                    pool.wait_ge(S["qkt_ready"], n - 4)
                    pool.tensor_tensor(qkt[g][:, 2:4, 0:WIN], qkt[g][:, 2:4, P:P + WIN],
                                       kshift[:, 0:1].unsqueeze(2).to_broadcast([P, 2, WIN]), ALU.mult)\
                        .then_inc(S["kp_ready"], 1)
                    if k % UT == 1:
                        stage(l, b, k // UT + 1)
                    if k % UT == 2:
                        table(l, b, k // UT + 1)
                    pool.wait_ge(S["sg_ready"], n)
                    pool.wait_ge(S["qn_ready"], n - 2)
                    pool.tensor_tensor(rn[i][:, :], sg[i][:, :], half_c[:, :], ALU.pow).then_inc(S["rn_ready"], 1)

            def start(l, first):
                if not first:
                    pool.wait_ge(x0_ready, l * (2 * NG) + (2 - 2 * NG + CREDIT))
                    pool.wait_ge(x_lo_ready, l * (NT + 1) + CREDIT)
                pool.tensor_tensor(lay4[:, :], xpos[:, :], qks[:, bass.ds(l, 1), :].rearrange("p o n -> p (o n)"),
                                   ALU.mult).then_inc(lay_ready, 1)
                stage(l, 0, 0)
                pool.wait_ge(lay_ready, l + 2)
                table(l, 0, 0)
                first_slot(slot, l)

            def layer(l, more):
                pool.wait_ge(x0_ready, l * (2 * NG) + CREDIT)
                layer_slots(pool, slot, l)
                deviation(l * NT + (NT + CREDIT))
                if more:
                    start(l + 1, False)

            start(0, True)
            with pool.Fori(0, DEPTH - 1) as l:
                layer(l, True)
            layer(DEPTH - 1, False)

            pool.wait_ge(scale_ready, 1)
            lw, wide = m["l_w"], [P, 2 * FC, P]
            steps = (
                lambda: pool.tensor_tensor(wfin[:, :, :], lw[:, :, :], wsr[:, :].unsqueeze(2).to_broadcast(wide),
                                           ALU.mult),
                lambda: pool.tensor_scalar(wfin[:, :, :], wfin[:, :, :], ROUND, None, ALU.add),
                lambda: pool.tensor_scalar(wfin[:, :, :], wfin[:, :, :], ROUND, None, ALU.subtract),
                lambda: pool.tensor_scalar(wfin[:, :, :], wfin[:, :, :], -1.0, 1.0, ALU.max, ALU.min),
                lambda: pool.tensor_tensor(wfin[:, :, :], wfin[:, :, :], lw[:, :, :], ALU.subtract),
                lambda: pool.tensor_tensor(wfin[:, :, :], wfin[:, :, :], lw[:, :, :], ALU.add))
            for n, op in enumerate(steps):
                op().then_inc(tern_step, 1)
                pool.wait_ge(tern_step, n + 1)
            pool.tensor_tensor(wfin[:, :, :], wfin[:, :, :], wsc[:, :].unsqueeze(2).to_broadcast(wide), ALU.mult)\
                .then_inc(m["l_wfin_ready"], 1)


def stage_last_layer(nc, a, m, out):
    PS, XT, XN, X0 = m["PS"], m["XT"], m["XN"], m["X0"]
    HID = 64
    STEPS = T.bit_length() - 1
    TWO_PI = 2.0 * np.pi
    TP_HI = float(np.float32(6.28125))
    TP_LO = float(np.float32(TWO_PI - 6.28125))
    PI_F = float(np.nextafter(np.float32(np.pi), np.float32(0)))

    with ExitStack() as ctx:
        def sb(name, shape, dt=F32):
            return ctx.enter_context(nc.sbuf_tensor(name, shape, dt))

        def sem(name):
            return ctx.enter_context(nc.semaphore(name))

        sqr = sb("l_sqr", [P, T])
        hs = sb("l_hs", [P, T])
        rr = sb("l_rr", [P, FC, T])
        lw = m["l_w"]
        wtt = sb("l_wtt", [P, 2 * FC, P])
        t1 = sb("l_t1", [16, FH])
        ex = sb("l_ex", [P, 4])
        ang = sb("l_ang", [P, 2])
        rev = sb("l_rev", [P, 2])
        sc2 = sb("l_sc2", [P, 2])
        ab = sb("l_ab", [P, 2])
        bs = sb("l_bs", [P, D])
        bt = sb("l_bt", [P, D])
        cs = sb("l_cs", [P, D])
        sj = sb("l_sj", [P, P])
        la = sb("l_la", [P, STEPS, 2 * P])
        tmp = [sb(f"l_tmp{i}", [P, GT]) for i in range(2)]
        yt = sb("l_yt", [P, T])
        yo = sb("l_yo", [P, NT, D])

        x1_set, v_step, a_step, p_step = sem("l_x1_set"), sem("l_v_step"), sem("l_a_step"), sem("l_p_step")
        mean_done, centred, squared, var_done, logged, rstd_ready, xn_ready = (
            sem("l_" + n) for n in ("mean_done", "centred", "squared", "var_done", "logged", "rstd_ready", "xn_ready"))
        lam_exp, lam_sin, lam_set, pow_done, pow_ready = (
            sem("l_" + n) for n in ("lam_exp", "lam_sin", "lam_set", "pow_done", "pow_ready"))
        wt_done, wt_ready, bt_done, bt_ready, t1_done, t1_ready, lr_done, wlr_ready = (
            sem("l_" + n) for n in ("wt_done", "wt_ready", "bt_done", "bt_ready",
                                    "t1_done", "t1_ready", "lr_done", "wlr_ready"))
        c_ready, bu_done, bu_ready, sh_done, hs_ready = (
            sem("l_" + n) for n in ("c_ready", "bu_done", "bu_ready", "sh_done", "hs_ready"))
        h_done, relu_ready, rr_ready, y_done, yd_ready, yt_ready, back_done, yo_ready, stored = (
            sem("l_" + n) for n in ("h_done", "relu_ready", "rr_ready", "y_done", "yd_ready", "yt_ready",
                                    "back_done", "yo_ready", "stored"))
        block = ctx.enter_context(nc.Block())

        scan = [(s, g) for s in range(STEPS) for g in range(NG - 1, -1, -1) if (g + 1) * GT > (1 << s)]

        def scan_count(s, g):
            while (s, g) not in scan:
                s -= 1
            return scan.index((s, g)) + 1

        def hidden_after(n):
            return range(n, n + 1) if n < NG * FC else range(0)

        @block.sync
        def _(sp):
            for g in range(NG):
                sp.wait_ge(yo_ready, g + 1)
                sp.dma_start(out[0, g * GT:(g + 1) * GT, :].rearrange("(n p) d -> p n d", p=P),
                             yo[:, 4 * g:4 * g + 4, :]).then_inc(stored, 16)
            sp.wait_ge(stored, 16 * NG)

        @block.tensor
        def _(pe):
            pe.wait_ge(m["loaded_l"], 16 * 8)
            pe.matmul(PS[0:16, 4, :], m["l_fb"][:, :], m["l_ut"][:, :], start=True, stop=True).then_inc(t1_done, 1)
            pe.wait_ge(m["l_wfin_ready"], 1)
            for c in range(2 * FC):
                last = pe.transpose(PS[:, 6 + c // 4, (c % 4) * P:(c % 4 + 1) * P], m["l_wfin"][:, c, :],
                                    m["ident"][:, :])
            last.then_inc(wt_done, 1)
            pe.wait_ge(t1_ready, 1)
            pe.matmul(PS[:, 5, :], m["l_v"][:, :], t1[:, :], start=True, stop=True).then_inc(lr_done, 1)
            for g in range(NG):
                pe.wait_ge(x1_set, 2 * g + 2)
                pe.matmul(PS[:, g, :], m["mean_w"][:, :], XT[:, g * GT:(g + 1) * GT], start=True, stop=True)\
                  .then_inc(mean_done, 1)
            pe.wait_ge(wt_ready, 1)
            pe.wait_ge(wlr_ready, 1)
            for g in range(NG):
                pe.wait_ge(squared, g + 1)
                pe.matmul(PS[:, 4 + g, :], m["mean_w"][:, :], sqr[:, g * GT:(g + 1) * GT], start=True, stop=True)\
                  .then_inc(var_done, 1)
                if g == 1:
                    pe.wait_ge(centred, NG)
                    pe.wait_ge(bt_ready, 1)
                    pe.transpose(PS[:, 0, 0:P], bs[:, :], m["ident"][:, :]).then_inc(bt_done, 1)
            pe.wait_ge(a_step, 1)
            for g in range(NG):
                pe.wait_ge(xn_ready, g + 1)
                pe.matmul(PS[:, 4 + g, :], bt[:, :], XN[:, g * GT:(g + 1) * GT], start=True, stop=True)\
                  .then_inc(bu_done, 1)
            pe.wait_ge(wlr_ready, 1)

            def hidden(i):
                g, c = i // FC, i % FC
                if i >= 2:
                    pe.wait_ge(relu_ready, i - 1)
                pe.matmul(PS[:, 6 + i % 2, :], wtt[:, c, :], XN[:, g * GT:(g + 1) * GT], start=True, stop=True)\
                  .then_inc(h_done, 1)

            def power(s):
                pe.matmul(PS[:, 5, 0:P], la[:, s, P:2 * P], la[:, s, 0:P], start=True, stop=True)
                pe.matmul(PS[:, 5, P:2 * P], la[:, s, 0:P], la[:, s, P:2 * P], start=True, stop=True)\
                  .then_inc(pow_done, 1)

            for n, (s, g) in enumerate(scan):
                lo = max(g * GT, 1 << s)
                if s == 0:
                    pe.wait_ge(bu_ready, NG)
                    pe.wait_ge(lam_set, 2)
                else:
                    if g == NG - 1:
                        pe.wait_ge(pow_ready, s)
                    need = max(scan_count(s - 1, gg) for gg in
                               range((lo - (1 << s)) // GT, ((g + 1) * GT - (1 << s) - 1) // GT + 1))
                    pe.wait_ge(hs_ready, need)
                if n >= 4:
                    pe.wait_ge(hs_ready, n - 3)
                pe.matmul(PS[:, n % 4, 0:(g + 1) * GT - lo], la[:, s, 0:P],
                          hs[:, lo - (1 << s):(g + 1) * GT - (1 << s)], start=True, stop=True).then_inc(sh_done, 1)
                if g == NG - 1 and s < STEPS - 1:
                    power(s)
                for i in hidden_after(n):
                    hidden(i)
            pe.wait_ge(hs_ready, len(scan))
            pe.wait_ge(c_ready, 1)
            for g in range(NG):
                cols = slice(g * GT, (g + 1) * GT)
                pe.matmul(PS[:, g, :], cs[:, :], hs[:, cols], start=True, stop=False)
                pe.wait_ge(rr_ready, FC * (g + 1))
                for c in range(FC):
                    last = pe.matmul(PS[:, g, :], wtt[:, FC + c, :], rr[:, c, cols], start=False, stop=(c == FC - 1))
                last.then_inc(y_done, 1)
            for g in range(NG):
                pe.wait_ge(yt_ready, g + 1)
                for n in range(4 * g, 4 * g + 4):
                    last = pe.transpose(PS[:, 4 + g, (n % 4) * P:(n % 4 + 1) * P], yt[:, n * P:(n + 1) * P],
                                        m["ident"][:, :])
                last.then_inc(back_done, 1)

        @block.scalar
        def _(act):
            act.wait_ge(m["loaded_l"], 16 * 8)
            act.wait_ge(t1_done, 1)
            act.activation(t1[:, :], PS[0:16, 4, :], ACT.Copy, scale=m["l_gate"][0:16, 0:1]).then_inc(t1_ready, 1)
            act.activation(ex[:, 0:3], m["l_vec"][:, 0:3], ACT.Exp).then_inc(lam_exp, 1)
            act.wait_ge(lam_exp, 1)
            act.activation(ex[:, 3:4], ex[:, 0:1], ACT.Exp, scale=-1.0).then_inc(lam_exp, 1)
            act.wait_ge(wt_done, 1)
            act.activation(wtt[:, :, :].rearrange("p c n -> p (c n)"), flat(PS[:, 6:8, :]), ACT.Copy)\
               .then_inc(wt_ready, 1)
            act.wait_ge(lam_sin, 1)
            act.activation(sc2[:, :], rev[:, :], ACT.Sin).then_inc(lam_exp, 1)
            for g in range(NG):
                act.wait_ge(centred, g + 1)
                act.activation(sqr[:, g * GT:(g + 1) * GT], XN[:, g * GT:(g + 1) * GT], ACT.Square)\
                   .then_inc(squared, 1)
            act.wait_ge(bt_done, 1)
            act.activation(bt[:, :], PS[:, 0, 0:P], ACT.Copy).then_inc(a_step, 1)
            act.wait_ge(var_done, NG)
            act.activation(sqr[:, :], flat(PS[:, 4:8, :]), ACT.Ln, bias=m["eps_c"][:, 0:1]).then_inc(logged, 1)
            act.wait_ge(logged, 1)
            for h in range(2):
                half = sqr[:, h * T // 2:(h + 1) * T // 2]
                act.activation(half, half, ACT.Exp, scale=-0.5).then_inc(rstd_ready, 1)
            for g in range(NG):
                act.wait_ge(bu_done, g + 1)
                act.activation(hs[:, g * GT:(g + 1) * GT], PS[:, 4 + g, :], ACT.Copy).then_inc(bu_ready, 1)
            for n, (s, g) in enumerate(scan):
                if g == NG - 1 and s < STEPS - 1:
                    act.wait_ge(pow_done, s + 1)
                    act.activation(la[:, s + 1, :], PS[:, 5, 0:2 * P], ACT.Copy).then_inc(pow_ready, 1)
                for i in hidden_after(n):
                    act.wait_ge(h_done, i + 1)
                    act.activation(rr[:, i % FC, i // FC * GT:(i // FC + 1) * GT], PS[:, 6 + i % 2, :], ACT.Relu)\
                       .then_inc(relu_ready, 1)
            for g in range(NG):
                act.wait_ge(back_done, g + 1)
                act.activation(yo[:, 4 * g:4 * g + 4, :].rearrange("p n d -> p (n d)"), PS[:, 4 + g, :], ACT.Copy)\
                   .then_inc(yo_ready, 1)

        @block.gpsimd
        def _(pool):
            for i in range(NG * FC):
                g, c = i // FC, i % FC
                r = rr[:, c, g * GT:(g + 1) * GT]
                pool.wait_ge(relu_ready, i + 1)
                pool.tensor_tensor(r, r, r, ALU.mult).then_inc(rr_ready, 1)

        @block.vector
        def _(dve):
            for g in range(NG):
                for h in range(2):
                    r = slice(64 * h, 64 * h + 64)
                    c0 = g * GT
                    dve.tensor_tensor(XT[r, c0:c0 + GT], XT[r, c0:c0 + GT],
                                      X0[r, PAD + h + c0:PAD + h + c0 + GT], ALU.add).then_inc(x1_set, 1)
            dve.wait_ge(lr_done, 1)
            dve.wait_ge(wt_ready, 1)
            w = wtt[:, 0:FC, :].rearrange("p c n -> p (c n)")
            dve.tensor_tensor(w, w, PS[:, 5, :], ALU.add).then_inc(wlr_ready, 1)
            step = [0]

            def chain(ins):
                step[0] += 1
                ins.then_inc(v_step, 1)
                dve.wait_ge(v_step, step[0])

            dve.wait_ge(lam_exp, 2)
            chain(dve.tensor_scalar(ang[:, 0:1], ex[:, 1:2], 1.0 / TWO_PI, None, ALU.mult))
            chain(dve.tensor_scalar(ang[:, 1:2], ex[:, 1:2], 1.0 / TWO_PI, 0.25, ALU.mult, ALU.add))
            chain(dve.tensor_scalar(ang[:, :], ang[:, :], ROUND, ROUND, ALU.add, ALU.subtract))
            for i in range(2):
                chain(dve.scalar_tensor_tensor(out=rev[:, i:i + 1], in0=ang[:, i:i + 1], scalar=-TP_HI,
                                               in1=ex[:, 1:2], op0=ALU.mult, op1=ALU.add))
            chain(dve.scalar_tensor_tensor(out=rev[:, :], in0=ang[:, :], scalar=-TP_LO, in1=rev[:, :],
                                           op0=ALU.mult, op1=ALU.add))
            chain(dve.tensor_scalar(rev[:, 1:2], rev[:, 1:2], float(np.pi / 2), None, ALU.add))
            dve.tensor_scalar(rev[:, :], rev[:, :], PI_F, -PI_F, ALU.min, ALU.max).then_inc(lam_sin, 1)
            for g in range(NG):
                cols = slice(g * GT, (g + 1) * GT)
                dve.wait_ge(mean_done, g + 1)
                dve.tensor_tensor(XN[:, cols], XT[:, cols], PS[:, g, :], ALU.subtract).then_inc(centred, 1)
            dve.tensor_scalar(bs[:, :], m["l_b"][:, :], ex[:, 2:3], None, ALU.mult).then_inc(bt_ready, 1)
            dve.wait_ge(lam_exp, 3)
            chain(dve.tensor_scalar(ab[:, 0:1], sc2[:, 1:2], ex[:, 3:4], None, ALU.mult))
            chain(dve.tensor_scalar(ab[:, 1:2], sc2[:, 0:1], ex[:, 3:4], m["l_vec"][:, 3:4], ALU.mult, ALU.mult))
            for h in range(2):
                chain(dve.tensor_scalar(sj[:, 64 * h:64 * h + 64], m["ident"][:, 64 - 64 * h:128 - 64 * h], ab[:, 1:2],
                                        None, ALU.mult))
            dve.scalar_tensor_tensor(out=la[:, 0, 0:P], in0=m["ident"][:, :], scalar=ab[:, 0:1], in1=sj[:, :],
                                     op0=ALU.mult, op1=ALU.add).then_inc(lam_set, 1)
            dve.scalar_tensor_tensor(out=la[:, 0, P:2 * P], in0=m["ident"][:, :], scalar=ab[:, 0:1], in1=sj[:, :],
                                     op0=ALU.mult, op1=ALU.subtract).then_inc(lam_set, 1)
            dve.tensor_scalar(cs[:, :], m["l_ct"][:, :], m["l_vec"][:, 3:4], None, ALU.mult).then_inc(c_ready, 1)
            for g in range(NG):
                cols = slice(g * GT, (g + 1) * GT)
                dve.wait_ge(rstd_ready, 1 + g // 2)
                dve.tensor_tensor(XN[:, cols], XN[:, cols], sqr[:, cols], ALU.mult).then_inc(xn_ready, 1)
            for n, (s, g) in enumerate(scan):
                lo = max(g * GT, 1 << s)
                cols = slice(lo, (g + 1) * GT)
                if s == 0:
                    dve.wait_ge(bu_ready, NG)
                dve.wait_ge(sh_done, n + 1)
                dve.tensor_tensor(hs[:, cols], PS[:, n % 4, 0:(g + 1) * GT - lo], hs[:, cols], ALU.add)\
                   .then_inc(hs_ready, 1)
            for g in range(NG):
                cols = slice(g * GT, (g + 1) * GT)
                dve.wait_ge(y_done, g + 1)
                dve.scalar_tensor_tensor(out=tmp[g % 2][:, :], in0=XN[:, cols], scalar=m["l_vec"][:, 4:5],
                                         in1=PS[:, g, :], op0=ALU.mult, op1=ALU.add).then_inc(yd_ready, 1)
                dve.wait_ge(yd_ready, g + 1)
                dve.tensor_tensor(yt[:, cols], XT[:, cols], tmp[g % 2][:, :], ALU.add).then_inc(yt_ready, 1)


def constants():
    half = np.arange(0, DH, 2, dtype=np.float32)
    inv_freq = (1.0 / np.power(np.float32(10000.0), half / np.float32(DH))).astype(np.float32)
    freqs = (np.arange(T, dtype=np.float32)[:, None] * inv_freq[None, :]).astype(np.float32).astype(np.float64)
    cos = np.concatenate([np.cos(freqs)] * 2, -1)
    sin = np.concatenate([np.sin(freqs)] * 2, -1)
    rot = np.zeros((P, NT + 1, 2, DH), np.float32)
    rot[:, :NT, 0] = cos.reshape(NT, P, DH).transpose(1, 0, 2)
    rot[:, :NT, 1] = sin.reshape(NT, P, DH).transpose(1, 0, 2)
    base = ((half.astype(np.float64) + 0.4 * DH) / (1.4 * DH))
    base = np.concatenate([base, base])
    power = (np.arange(P) - P // 2)[:, None] / (WIN // 2)
    sc = base[None, :] ** power
    sign = np.concatenate([-np.ones(DH // 2), np.ones(DH // 2)])
    xpos = np.stack([8.0 * sc, 8.0 * sc * sign, 1.0 / sc, sign / sc], 1).astype(np.float32)
    kshift = np.concatenate([base, base])[:, None] ** (P / (WIN // 2))
    i, c = np.arange(P)[:, None] % WIN, np.arange(2 * WIN)[None, :]
    ok = (c >= i) & (c <= i + WIN)
    first = ok & ~((np.arange(P)[:, None] < WIN) & (c < WIN))
    mask = np.stack([np.where(v, 0.0, MASKED) for v in (np.tile(first, 2), np.tile(ok, 2))], 1)
    q, c = np.arange(P)[:, None], np.arange(2 * P)[None, :]
    own = c - P <= q
    a_mask = np.stack([np.where(v, 0.0, MASKED) for v in (own & (c >= P), own)], 1)
    g = np.arange(96) // 8
    return {
        "a_mask": a_mask.astype(np.float32),
        "a_bmask": (g[:, None] == g[None, :]).astype(np.float32),
        "c_ident": np.eye(P, dtype=np.float32),
        "c_rot": rot.reshape(P, NT + 1, 2 * DH),
        "c_xpos": xpos.reshape(P, 4 * DH),
        "c_kshift": kshift.astype(np.float32),
        "c_mask": mask.astype(np.float32),
    }


def lay_out(x):
    def chunks(v):
        z = np.zeros((DEPTH, len(FCH) * P), np.float32)
        z[:, :FF] = v
        return z.reshape(DEPTH, len(FCH), P).transpose(0, 2, 1)

    b1 = np.asarray(x["L0_ffn_b1"])
    par = np.concatenate([np.asarray(x["L0_ffn_ln_g"])[:, :, None], np.asarray(x["L0_ffn_ln_b"])[:, :, None],
                          np.asarray(x["L0_ffn_b2"])[:, :, None], chunks(b1[:, :FF]), chunks(b1[:, FF:])], 2)
    w2 = np.zeros((DEPTH, len(FCH) * P, D), np.float32)
    w2[:, :FF] = np.asarray(x["L0_ffn_W2"])
    qs, ks = np.asarray(x["L0_ffn_q_scale"]), np.asarray(x["L0_ffn_k_scale"])
    h = DH // 2
    def f(n):
        return np.asarray(x[n])

    def twice(n):
        return np.concatenate([f(n), f(n)])

    sign = np.concatenate([np.ones(64), -np.ones(64)]).astype(np.float32)
    vec = np.stack([twice("L1_attn_nu_log"), twice("L1_attn_theta_log"), twice("L1_attn_gamma_log"), sign,
                    f("L1_attn_D")], 1)
    four = np.concatenate([qs, qs[:, h:], qs[:, :h], ks, ks[:, h:], ks[:, :h]], 1)
    return {
        "a_w": np.concatenate([f("L0_attn_W" + c) for c in "qkvo"], 1),
        "a_bo": f("L0_attn_bo")[:, None],
        "l_vec": vec,
        "l_gate": np.broadcast_to(f("L1_ffn_gate").reshape(1, 1), (P, 1)),
        "l_b": np.concatenate([f("L1_attn_B_re"), f("L1_attn_B_im")], 0),
        "l_ct": np.concatenate([f("L1_attn_C_re").T, f("L1_attn_C_im").T], 0),
        "l_ut": f("L1_ffn_u").T,
        "l_w": np.concatenate([f("L1_ffn_w_fc").reshape(4, P, D).transpose(1, 0, 2),
                               f("L1_ffn_w_proj").reshape(P, 4, P)], 1),
        "l_par": par,
        "l_w2": w2.reshape(DEPTH, len(FCH), P, D).transpose(0, 2, 1, 3).reshape(DEPTH, P, len(FCH) * D),
        "l_wo": np.asarray(x["L0_ffn_Wo"]).reshape(DEPTH, HEADS // 2, P, D).transpose(0, 2, 1, 3)
        .reshape(DEPTH, P, HEADS // 2 * D),
        "c_qk_scales": np.broadcast_to(four[None], (P, DEPTH, 4 * DH)),
    }


_INS = ["L0_attn_x", "L0_ffn_Wqkv", "L0_ffn_W1", "L1_ffn_fast_b", "L1_ffn_v"]
_OUTS = [((1, T, D), "float32")]


def kernel(**inputs):
    import concourse.bacc as _bacc
    from concourse.bass_utils import run_bass_kernel_spmd as _run

    nc = _bacc.Bacc("TRN2", target_bir_lowering=False, num_devices=1)
    given = {n: np.asarray(inputs[n]) for n in _INS}
    given.update(lay_out(inputs))
    given.update(constants())
    arrays, args = {}, {}
    for name, v in given.items():
        v = np.ascontiguousarray(v)
        arrays[f"in_{name}_dram"] = v
        args[name] = nc.dram_tensor(f"in_{name}_dram", v.shape, mybir.dt.from_np(v.dtype), kind="ExternalInput").ap()
    shape, dtype = _OUTS[0]
    out = nc.dram_tensor("out_0_dram", shape, mybir.dt.from_np(np.dtype(dtype)), kind="ExternalOutput").ap()
    program(nc, args, out)
    r = _run(nc, [arrays], core_ids=[0])
    return r.results[0]["out_0_dram"]
```
